# Optimizing a Trainium2 kernel written in Bass

```python
import numpy as np
import jax
import jax.numpy as jnp

def _softmax(x, axis=-1):
    return jax.nn.softmax(x, axis=axis)

def _gelu(x):
    return jax.nn.gelu(x, approximate=True)

def _silu(x):
    return jax.nn.silu(x)

def _sigmoid(x):
    return jax.nn.sigmoid(x)

def _layernorm(x, axis=-1, eps=1e-05):
    m = jnp.mean(x, axis=axis, keepdims=True)
    v = jnp.var(x, axis=axis, keepdims=True)
    return (x - m) / jnp.sqrt(v + eps)

def _scatter_add(tgt, idx, src, axis=0):
    return tgt.at[idx].add(src)

def _segment_sum(src, seg, n):
    return jax.ops.segment_sum(src, seg, n)
kernel_name = 'mk_xattn_ffn_d2_seqx_r8_277810'

def setup_inputs(seed: int=0):
    np.random.seed(seed)
    _w = jnp.asarray

    def _rec_inputs():
        import jax
        import jax.numpy as jnp
        _rk = jax.random.key(seed)
        x = 7.22e-05 + 1 * jax.random.normal(jax.random.fold_in(_rk, 1), (8, 128, 128), jnp.float32)
        _lenS = 128 - jax.random.randint(jax.random.fold_in(_rk, 7), (8,), 0, max(1, 128 // 4) + 1, jnp.int32)
        _lenS2 = 77 - jax.random.randint(jax.random.fold_in(_rk, 8), (8,), 0, max(1, 77 // 4) + 1, jnp.int32)
        _ctx_768P = jax.random.normal(jax.random.fold_in(_rk, 11), (8, 16, 96), jnp.float32)
        _ctx_768c = jax.random.dirichlet(jax.random.fold_in(_rk, 511), 0.3 * jnp.ones((16,), jnp.float32), (8, 77))
        _ctx_768t = jnp.einsum('bsk,bkd->bsd', _ctx_768c, _ctx_768P)
        _ctx_768t = _ctx_768t * jax.lax.rsqrt(jnp.mean(jnp.square(_ctx_768t)) + 1e-12) * 0.953939
        ctx_768 = 2.09791e-05 + 1.00001 * (_ctx_768t + 0.3 * jax.random.normal(jax.random.fold_in(_rk, 611), (8, 77, 96), jnp.float32))
        return (x, ctx_768)
    x, ctx_768 = _rec_inputs()

    def _L0_xattn_setup():
        import jax, jax.numpy as jnp
        import numpy as np
        NUM_HEADS = 16
        key = jax.random.key(seed)
        ks = jax.random.split(key, 8)
        dim, cond_dim = (128, 96)
        B, N, condN = (4, 256, 128)
        s = lambda k, shp, fan: jax.random.normal(k, shp, dtype=jnp.float32) * fan ** (-0.5)
        return {'x': jax.random.normal(ks[0], (B, N, dim), dtype=jnp.float32), 'cond': jax.random.normal(ks[1], (B, condN, cond_dim), dtype=jnp.float32), 'q_w': s(ks[2], (dim, dim), dim), 'q_b': jnp.zeros((dim,), jnp.float32), 'kv_w': s(ks[3], (cond_dim, 2 * dim), cond_dim), 'kv_b': jnp.zeros((2 * dim,), jnp.float32), 'proj_w': s(ks[4], (dim, dim), dim), 'proj_b': jnp.zeros((dim,), jnp.float32)}
    _L0_xattn_all = _L0_xattn_setup()
    _L0_xattn_in = {k: v for k, v in _L0_xattn_all.items() if k in ('q_w', 'q_b', 'kv_w', 'kv_b', 'proj_w', 'proj_b')}
    del _L0_xattn_all

    def _L0_ffn_setup():
        import jax, jax.numpy as jnp
        import numpy as np
        H = 128
        I = 128
        E = 16
        K = 4
        LIMIT = 7.0
        ALPHA = 1.702
        EPS = 1e-05
        key = jax.random.key(seed)
        ks = jax.random.split(key, 8)
        x = jax.random.normal(ks[0], (2, 64, H), dtype=jnp.float32)
        norm_scale = jnp.ones((H,), dtype=jnp.float32)
        wg = jax.random.normal(ks[1], (H, E), dtype=jnp.float32) * 0.02
        bg = jax.random.normal(ks[2], (E,), dtype=jnp.float32) * 0.02
        w1 = jax.random.normal(ks[3], (E, H, 2 * I), dtype=jnp.float32) * 0.02
        b1 = jax.random.normal(ks[4], (E, 2 * I), dtype=jnp.float32) * 0.02
        w2 = jax.random.normal(ks[5], (E, I, H), dtype=jnp.float32) * 0.02
        b2 = jax.random.normal(ks[6], (E, H), dtype=jnp.float32) * 0.02
        return {'x': x, 'norm_scale': norm_scale, 'wg': wg, 'bg': bg, 'w1': w1, 'b1': b1, 'w2': w2, 'b2': b2}
    _L0_ffn_all = _L0_ffn_setup()
    _L0_ffn_in = {k: v for k, v in _L0_ffn_all.items() if k in ('norm_scale', 'wg', 'bg', 'w1', 'b1', 'w2', 'b2')}
    del _L0_ffn_all

    def _L1_xattn_setup():
        import jax, jax.numpy as jnp
        import numpy as np
        HEADS = 16
        DIM_HEAD = 64
        key = jax.random.key(seed)
        ks = jax.random.split(key, 7)
        B, Nq, Dq = (4, 256, 128)
        Nk, Dc = (128, 96)
        inner = HEADS * DIM_HEAD
        sq = 1.0 / np.sqrt(Dq)
        sc = 1.0 / np.sqrt(Dc)
        si = 1.0 / np.sqrt(inner)
        return {'x': jax.random.normal(ks[0], (B, Nq, Dq), dtype=jnp.float32), 'context': jax.random.normal(ks[1], (B, Nk, Dc), dtype=jnp.float32), 'Wq': jax.random.normal(ks[2], (Dq, inner), dtype=jnp.float32) * sq, 'Wk': jax.random.normal(ks[3], (Dc, inner), dtype=jnp.float32) * sc, 'Wv': jax.random.normal(ks[4], (Dc, inner), dtype=jnp.float32) * sc, 'Wo': jax.random.normal(ks[5], (inner, Dq), dtype=jnp.float32) * si, 'bo': jax.random.normal(ks[6], (Dq,), dtype=jnp.float32) * 0.01}
    _L1_xattn_all = _L1_xattn_setup()
    _L1_xattn_in = {k: v for k, v in _L1_xattn_all.items() if k in ('Wq', 'Wk', 'Wv', 'Wo', 'bo')}
    del _L1_xattn_all

    def _L1_ffn_setup():
        import jax, jax.numpy as jnp
        import numpy as np
        H, E, DFF = (128, 8, 512)
        key = jax.random.key(seed)
        ks = jax.random.split(key, 7)
        s = lambda *shape: 1.0 / np.sqrt(shape[-2] if len(shape) > 1 else shape[-1])
        x = jax.random.normal(ks[0], (2, 256, H), dtype=jnp.float32)
        Wr = jax.random.normal(ks[1], (H, E), dtype=jnp.float32) * (1.0 / np.sqrt(H))
        br = jnp.zeros((E,), dtype=jnp.float32)
        W1 = jax.random.normal(ks[2], (E, H, DFF), dtype=jnp.float32) * (1.0 / np.sqrt(H))
        b1 = jnp.zeros((E, DFF), dtype=jnp.float32)
        W2 = jax.random.normal(ks[3], (E, DFF, H), dtype=jnp.float32) * (1.0 / np.sqrt(DFF))
        b2 = jnp.zeros((E, H), dtype=jnp.float32)
        return {'x': x, 'Wr': Wr, 'br': br, 'W1': W1, 'b1': b1, 'W2': W2, 'b2': b2}
    _L1_ffn_all = _L1_ffn_setup()
    _L1_ffn_in = {k: v for k, v in _L1_ffn_all.items() if k in ('Wr', 'br', 'W1', 'b1', 'W2', 'b2')}
    del _L1_ffn_all
    return {'x': x, 'ctx_768': ctx_768, 'L0_xattn_q_w': _L0_xattn_in['q_w'], 'L0_xattn_q_b': _L0_xattn_in['q_b'], 'L0_xattn_kv_w': _L0_xattn_in['kv_w'], 'L0_xattn_kv_b': _L0_xattn_in['kv_b'], 'L0_xattn_proj_w': _L0_xattn_in['proj_w'], 'L0_xattn_proj_b': _L0_xattn_in['proj_b'], 'L0_ffn_norm_scale': _L0_ffn_in['norm_scale'], 'L0_ffn_wg': _L0_ffn_in['wg'], 'L0_ffn_bg': _L0_ffn_in['bg'], 'L0_ffn_w1': _L0_ffn_in['w1'], 'L0_ffn_b1': _L0_ffn_in['b1'], 'L0_ffn_w2': _L0_ffn_in['w2'], 'L0_ffn_b2': _L0_ffn_in['b2'], 'L1_xattn_Wq': _L1_xattn_in['Wq'], 'L1_xattn_Wk': _L1_xattn_in['Wk'], 'L1_xattn_Wv': _L1_xattn_in['Wv'], 'L1_xattn_Wo': _L1_xattn_in['Wo'], 'L1_xattn_bo': _L1_xattn_in['bo'], 'L1_ffn_Wr': _L1_ffn_in['Wr'], 'L1_ffn_br': _L1_ffn_in['br'], 'L1_ffn_W1': _L1_ffn_in['W1'], 'L1_ffn_b1': _L1_ffn_in['b1'], 'L1_ffn_W2': _L1_ffn_in['W2'], 'L1_ffn_b2': _L1_ffn_in['b2']}

def reference(x, ctx_768, L0_xattn_q_w, L0_xattn_q_b, L0_xattn_kv_w, L0_xattn_kv_b, L0_xattn_proj_w, L0_xattn_proj_b, L0_ffn_norm_scale, L0_ffn_wg, L0_ffn_bg, L0_ffn_w1, L0_ffn_b1, L0_ffn_w2, L0_ffn_b2, L1_xattn_Wq, L1_xattn_Wk, L1_xattn_Wv, L1_xattn_Wo, L1_xattn_bo, L1_ffn_Wr, L1_ffn_br, L1_ffn_W1, L1_ffn_b1, L1_ffn_W2, L1_ffn_b2):
    import jax
    import jax.numpy as jnp

    def _L0_xattn_ref(x, cond, q_w, q_b, kv_w, kv_b, proj_w, proj_b):
        import jax, jax.numpy as jnp
        import numpy as np
        NUM_HEADS = 16
        B, N, C = x.shape
        condN = cond.shape[1]
        H = NUM_HEADS
        hd = C // H
        scale = hd ** (-0.5)
        q = (x @ q_w + q_b).reshape(B, N, H, hd).transpose(0, 2, 1, 3)
        kv = (cond @ kv_w + kv_b).reshape(B, condN, 2, H, hd)
        k = kv[:, :, 0].transpose(0, 2, 1, 3)
        v = kv[:, :, 1].transpose(0, 2, 1, 3)
        attn = jnp.einsum('bhnd,bhmd->bhnm', q * scale, k)
        attn = jax.nn.softmax(attn, axis=-1)
        out = jnp.einsum('bhnm,bhmd->bhnd', attn, v)
        out = out.transpose(0, 2, 1, 3).reshape(B, N, C)
        return out @ proj_w + proj_b

    def _L0_ffn_ref(x, norm_scale, wg, bg, w1, b1, w2, b2):
        import jax, jax.numpy as jnp
        import numpy as np
        H = 128
        I = 128
        E = 16
        K = 4
        LIMIT = 7.0
        ALPHA = 1.702
        EPS = 1e-05
        shape = x.shape
        xf = x.reshape(-1, shape[-1])
        xn = xf * jax.lax.rsqrt(jnp.mean(xf * xf, axis=-1, keepdims=True) + EPS) * norm_scale
        logits = xn @ wg + bg
        vals, idx = jax.lax.top_k(logits, K)
        gates = jax.nn.softmax(vals, axis=-1)
        gate_full = jnp.einsum('tke,tk->te', jax.nn.one_hot(idx, E, dtype=gates.dtype), gates)
        h = jnp.einsum('th,ehd->etd', xn, w1) + b1[:, None, :]
        a = jnp.minimum(h[..., ::2], LIMIT)
        b = jnp.clip(h[..., 1::2], -LIMIT, LIMIT)
        s = a * jax.nn.sigmoid(ALPHA * a) * (b + 1.0)
        y = jnp.einsum('eti,eih->eth', s, w2) + b2[:, None, :]
        t = jnp.einsum('eth,te->th', y, gate_full)
        return x + t.reshape(shape)

    def _L1_xattn_ref(x, context, Wq, Wk, Wv, Wo, bo):
        import jax, jax.numpy as jnp
        import numpy as np
        HEADS = 16
        DIM_HEAD = 64
        B, Nq, _ = x.shape
        Nk = context.shape[1]
        h, dh = (HEADS, DIM_HEAD)
        q = (x @ Wq).reshape(B, Nq, h, dh)
        k = (context @ Wk).reshape(B, Nk, h, dh)
        v = (context @ Wv).reshape(B, Nk, h, dh)
        scale = 1.0 / jnp.sqrt(jnp.asarray(dh, dtype=x.dtype))
        scores = jnp.einsum('bqhd,bkhd->bhqk', q, k) * scale
        attn = jax.nn.softmax(scores, axis=-1)
        out = jnp.einsum('bhqk,bkhd->bqhd', attn, v).reshape(B, Nq, h * dh)
        return out @ Wo + bo

    def _L1_ffn_ref(x, Wr, br, W1, b1, W2, b2):
        import jax, jax.numpy as jnp
        import numpy as np
        H, E, DFF = (128, 8, 512)
        B, S, Hd = x.shape
        n_exp = W1.shape[0]
        xt = x.reshape(-1, Hd)
        logits = xt @ Wr + br
        probs = jax.nn.softmax(logits, axis=-1)
        gate = jnp.max(probs, axis=-1)
        idx = jnp.argmax(probs, axis=-1)
        h1 = jnp.maximum(jnp.einsum('th,ehf->etf', xt, W1) + b1[:, None, :], 0.0)
        ye = jnp.einsum('etf,efh->eth', h1, W2) + b2[:, None, :]
        onehot = jax.nn.one_hot(idx, n_exp, dtype=xt.dtype)
        y = jnp.einsum('te,eth->th', onehot, ye) * gate[:, None]
        return y.reshape(B, S, Hd)
    x = x + _L0_xattn_ref(_layernorm(x, axis=-1), ctx_768, L0_xattn_q_w, L0_xattn_q_b, L0_xattn_kv_w, L0_xattn_kv_b, L0_xattn_proj_w, L0_xattn_proj_b)
    x = x + _L0_ffn_ref(_layernorm(x, axis=-1), L0_ffn_norm_scale, L0_ffn_wg, L0_ffn_bg, L0_ffn_w1, L0_ffn_b1, L0_ffn_w2, L0_ffn_b2)
    x = x + _L1_xattn_ref(_layernorm(x, axis=-1), ctx_768, L1_xattn_Wq, L1_xattn_Wk, L1_xattn_Wv, L1_xattn_Wo, L1_xattn_bo)
    x = x + _L1_ffn_ref(_layernorm(x, axis=-1), L1_ffn_Wr, L1_ffn_br, L1_ffn_W1, L1_ffn_b1, L1_ffn_W2, L1_ffn_b2)
    return x

_drawn_inputs = setup_inputs


def setup_inputs(seed=0):
    import zlib

    import numpy as np

    out = dict(_drawn_inputs(seed))
    spreads = {'L0_xattn_q_b': (0.0, 0.283),
     'L0_xattn_kv_b': (0.0, 0.1),
     'L0_xattn_proj_b': (0.0, 0.1),
     'L0_ffn_norm_scale': (1.0, 0.6),
     'L1_ffn_br': (0.0, 0.28),
     'L1_ffn_b1': (0.0, 0.65),
     'L1_ffn_b2': (0.0, 0.455)}
    factors = {'L0_ffn_wg': 4.635,
     'L0_ffn_bg': 8.0,
     'L0_ffn_w1': 4.993,
     'L0_ffn_b1': 8.0,
     'L0_ffn_w2': 4.661,
     'L0_ffn_b2': 6.169,
     'L1_xattn_bo': 6.107}
    for name, (base, spread) in spreads.items():
        noise = np.random.default_rng([zlib.crc32(name.encode()), seed]).standard_normal(out[name].shape)
        drawn = base * np.exp(spread * noise) if base else spread * noise
        out[name] = jnp.asarray(drawn.astype(out[name].dtype))
    for name, factor in factors.items():
        out[name] = (out[name] * factor).astype(out[name].dtype)
    return out
```

```python
from contextlib import ExitStack

import numpy as np

import concourse.bass as bass
from concourse import mybir

ALU = mybir.AluOpType
ACT = mybir.ActivationFunctionType
F32 = mybir.dt.float32
I32 = mybir.dt.int32
U32 = mybir.dt.uint32
AX_X = mybir.AxisListType.X

B = 8
T = 128
D = 128
M = 77
DC = 96
NH = 16
HD = (8, 64)
NG = 4
GH = NH // NG
GM = GH * M
E = (16, 8)
TOPK = (4, 1)
CAND = 8
REGION = CAND + 1
TILES = (48, 16)
FF = (128, 512)
WCOL = (2 * 128 + 128 + 2, 512 + 512 + 4)
EPS = 1e-5
LIMIT = 7.0
ALPHA = 1.702
UNROLL = (4, 2)

C_ID = 0
C_LT = C_ID + 128
C_ONE = C_LT + 128
C_IOTA = C_ONE + 128
C_HEAD = C_IOTA + 48
C_RB = C_HEAD + 4
C_PL = C_RB + 16
C_PL_W = 3 + 16
C_NH = C_PL + 2 * C_PL_W
C_ALL = C_NH + 1


def shape_constants():
    c = np.zeros((128, C_ALL), np.float32)
    p = np.arange(128)
    c[:, C_ID:C_ID + 128] = np.eye(128)
    c[:, C_LT:C_LT + 128] = p[:, None] < p[None, :]
    c[:, C_ONE:C_ONE + 128] = 1
    c[:, C_IOTA:C_IOTA + 48] = np.arange(48)
    c[:, C_HEAD:C_HEAD + 4] = (p[:, None] % 32) // 8 == np.arange(4)[None, :]
    c[:, C_RB:C_RB + 16] = np.arange(16) * REGION * 128
    for layer in range(2):
        o = C_PL + layer * C_PL_W
        e, t = p // CAND, p % CAND
        c[:, o] = 128 * t
        c[:, o + 1] = REGION * e + t - REGION * E[layer]
        c[:, o + 2] = e
        c[:, o + 3:o + 3 + E[layer]] = 128 * (e[:, None] < np.arange(E[layer])[None, :])
    c[:, C_NH] = -0.5
    return c


def plan_banks():
    job, count = {}, {}

    def use(bank, *what):
        count[bank] = count.get(bank, 0) + 1
        job[(bank, *what)] = count[bank]

    for n in range(2):
        use(f"T{n}", "k0", n)
    use("O", "v0", 0)
    use("M", "v0", 1)
    for n in range(2):
        use(f"S{n}", "xT0", n)
    for n in range(2):
        use(f"S{2 + n}", "q0", n)

    def scores(layer, b):
        for g in range(NG):
            use(f"S{g}", "scores", layer, b, g)

    def attention(layer):
        for b in range(B + 3):
            if layer and b + 1 < B:
                use("M", "xT", b + 1)
            if 0 <= b - 1 < B:
                use("O" if layer else "M", "oT", layer, b - 1, 0)
            if layer and b + 1 < B:
                use("M", "q", b + 1, 0)
            if layer and 0 <= b - 1 < B:
                use("O", "oT", layer, b - 1, 1)
            if layer and b + 1 < B:
                use("M", "q", b + 1, 1)
            if b < B:
                use("T0", "pT", layer, b, 0)
            if 0 <= b - 2 < B:
                use("M", "xnT", layer, b - 2)
            if b < B:
                use("T1", "pT", layer, b, 1)
            if 0 <= b - 1 < B:
                use("O" if layer else "M", "proj", layer, b - 1)
            if b < B:
                use("O", "pv", layer, b, 0)
                use("T0", "pT", layer, b, 2)
            if 0 <= b - 2 < B:
                use("M", "logits", layer, b - 2)
            if b < B:
                if layer:
                    use("O", "pv", layer, b, 1)
                use("T1", "pT", layer, b, 3)
            if 0 <= b - 3 < B:
                use("M", "rank", layer, b - 3)
            if b + 1 < B:
                scores(layer, b + 1)
            if layer and b < B:
                use("M", "pv", layer, b, 2)
                use("O", "pv", layer, b, 3)

    def tables(layer):
        use("O", "count", layer)
        use("O", "pos", layer)
        use("O", "table", layer)
        use("M", "start", layer)
        for n in range(2):
            use(f"T{n}", "gT", layer, n)
        for n in range(2):
            use(f"T{n}", "b2", layer, n)

    def loop(layer):
        turns = TILES[layer] // UNROLL[layer]
        for bank, per in LOOP_USES[layer].items():
            count[bank] = count.get(bank, 0)
            job[(bank, "loop", layer)] = count[bank]
            count[bank] += per * turns

    scores(0, 0)
    attention(0)
    for n in range(16):
        use(f"S{n % 4}", "k1", n)
        if n == 7:
            tables(0)
    loop(0)
    for n in range(16):
        use(f"S{n % 4}", "v1", n)
    use("M", "xT", 0)
    use("M", "q", 0, 0)
    use("M", "q", 0, 1)
    scores(1, 0)
    attention(1)
    tables(1)
    loop(1)
    return job


LOOP_USES = (
    {"T0": 1, "T1": 1, "S0": 1, "S1": 1, "S2": 1, "S3": 1, "O": 1, "M": 1},
    {"T0": 1, "T1": 1, "S0": 1, "S1": 1, "S2": 1, "S3": 1, "O": 1, "M": 1},
)


def build(nc, x, ctxT, cst, q_w, q_b, kv_w, kv_b, proj_w, proj_b, norm_s, wg, bg, wp0, b2_0,
          Wq, Wk, Wv, Wo, bo, Wr, br, wp1, b2_1, out):
    job = plan_banks()
    rows = (REGION * E[0] + 1) * 128
    xs_dram = nc.dram_tensor("dispatched", [rows, D], F32, kind="Internal").ap()
    ys_dram = [nc.dram_tensor(f"expert_out{n}", [TILES[n] * 128, D], F32, kind="Internal").ap() for n in range(2)]

    with ExitStack() as ctx:
        def sb(name, shape, dt=F32):
            return ctx.enter_context(nc.sbuf_tensor(name, shape, dt))

        def sem(name):
            return ctx.enter_context(nc.semaphore(name))

        bank = {n: ctx.enter_context(nc.psum_tensor(f"bank_{n}", [128, 512], F32))
                for n in ("S0", "S1", "S2", "S3", "T0", "T1", "O", "M")}
        filled = {n: sem(f"filled_{n}") for n in bank}
        freed = {n: sem(f"freed_{n}") for n in bank}

        C = sb("C", [128, C_ALL])
        ident = C[:, C_ID:C_ID + 128]
        before = C[:, C_LT:C_LT + 128]
        ones = C[:, C_ONE:C_ONE + 128]
        X = sb("X", [128, B, D])
        XB = sb("XB", [128, B, D])
        XR = sb("XR", [128, B, D])
        XF = sb("XF", [128, B, D])
        XN = sb("XN", [128, B, D])
        X2 = sb("X2", [128, B, D])
        XA = sb("XA", [128, B, D])
        ctx_sb = sb("ctx_sb", [DC, B * M])
        qw_sb = sb("qw_sb", [128, 128])
        qb_sb = sb("qb_sb", [128, 1])
        kvw_sb = sb("kvw_sb", [DC, 256])
        kvb_sb = sb("kvb_sb", [128, 2])
        pw_sb = sb("pw_sb", [128, 128])
        pb_sb = sb("pb_sb", [128, 128])
        ns_sb = sb("ns_sb", [128, 128])
        wg_sb = sb("wg_sb", [128, 16])
        bg_sb = sb("bg_sb", [128, 16])
        b20_sb = sb("b20_sb", [16, 128])
        Wq_sb = sb("Wq_sb", [128, 1024])
        Wk_sb = sb("Wk_sb", [DC, 1024])
        Wv_sb = sb("Wv_sb", [DC, 1024])
        Wo_sb = sb("Wo_sb", [128, 8, 128])
        bo_sb = sb("bo_sb", [128, 128])
        Wr_sb = sb("Wr_sb", [128, 8])
        br_sb = sb("br_sb", [128, 8])
        b21_sb = sb("b21_sb", [8, 128])
        wr_l, br_l, b2_l = (wg_sb, Wr_sb), (bg_sb, br_sb), (b20_sb, b21_sb)

        QT0 = sb("QT0", [128, B * T])
        KX0 = sb("KX0", [128, GH, B * M])
        V0 = sb("V0", [M, B, NH, HD[0] + 1])
        K1 = sb("K1", [128, 8, B * M])
        V1 = sb("V1", [M, B, NH, HD[1] + 1])
        XT1 = sb("XT1", [128, 128])
        QT1 = sb("QT1", [128, 2, 8, 128])
        XT0 = QT1[:, 0, :, :].rearrange("p c t -> p (c t)")
        P = sb("P", [128, 2, NG, GM])
        PT = sb("PT", [M, NG, GH * 128])
        negmax = sb("negmax", [128, NG, GH])
        recip = sb("recip", [128, NG, NH])
        OS = sb("OS", [128, NH * 64])
        OT = sb("OT", [128, 8, 128])
        XNT = sb("XNT", [128, 128])
        zeros = sb("zeros", [128, 128])

        st6 = sb("st6", [128, B, 6])
        mv = sb("mv", [128, B, 2])
        var_eps = sb("var_eps", [128, B])
        rstd = sb("rstd", [128, B])
        rms = sb("rms", [128, B])
        rrms = sb("rrms", [128, B])

        lg = sb("lg", [128, 16])
        top8 = sb("top8", [128, 8])
        idx8 = sb("idx8", [128, 8], U32)
        vdif = sb("vdif", [128, B, 8])
        vexp = sb("vexp", [128, B, 8])
        vsum = sb("vsum", [128, B])
        vrec = sb("vrec", [128, B])
        gates = sb("gates", [128, B, 4])
        hot = sb("hot", [128, B, 4, 16])
        mask = sb("mask", [128, B, 16])
        mcum = sb("mcum", [128, B, 16])
        posm = sb("posm", [128, 16])
        prod = sb("prod", [128, 4, 16])
        slot_f = sb("slot_f", [128, B, 4])
        slot_u = sb("slot_u", [128, B, 4], U32)
        gfp = sb("gfp", [128, B, 4, 16])
        gf = sb("gf", [128, B, 16])
        mexp = sb("mexp", [128, 16, CAND])
        act_c = sb("act_c", [128, 1])
        act_bc = sb("act_bc", [128, 128])
        pos_c = sb("pos_c", [128, 1])
        ohj = sb("ohj", [128, 48])
        table = sb("table", [1, 96], I32)
        region_shift = sb("region_shift", [128, 16])
        red = sb("red", [128, B, 4])
        yslot = sb("yslot", [128, B, 4], U32)
        gfT = sb("gfT", [16, B * 128])
        G = sb("G", [128, 2, 4, 128])

        w0 = sb("w0", [128, 4, WCOL[0]])
        w1 = sb("w1", [128, 2, WCOL[1]])
        xin = sb("xin", [128, 4, 128])
        xeT = sb("xeT", [128, 4, 128])
        ha = sb("ha", [128, 4, 128])
        hb = sb("hb", [128, 4, 128])
        th = sb("th", [128, 4, 128])
        hu = sb("hu", [128, 4, 128])
        hs = sb("hs", [128, 4, 128])
        h1 = (ha, hb)
        yo = sb("yo", [128, 4, 128])

        ld_x = [sem(f"ld_x{n}") for n in range(2)]
        ld_a = sem("ld_a")
        ld_b = sem("ld_b")
        ld_c = sem("ld_c")
        dve_step = sem("dve_step")
        act_step = sem("act_step")
        pool_step = sem("pool_step")
        ones_v = sem("ones_v")
        zero_set = sem("zero_set")
        zeroed = [sem(f"zeroed{n}") for n in range(REGION)]
        xb_ready = sem("xb_ready")
        ln_stats = sem("ln_stats")
        ln_rstd = sem("ln_rstd")
        xa_ready = sem("xa_ready")
        exp_done = sem("exp_done")
        rt_stats = sem("rt_stats")
        rt_rstd = sem("rt_rstd")
        xn_ready = sem("xn_ready")
        vdif_ready = sem("vdif_ready")
        vexp_ready = sem("vexp_ready")
        mask_ready = sem("mask_ready")
        slot_ready = sem("slot_ready")
        scattered = [sem(f"scattered{n}") for n in range(2)]
        gf_ready = sem("gf_ready")
        mexp_ready = sem("mexp_ready")
        act_ready = sem("act_ready")
        ohj_ready = sem("ohj_ready")
        yslot_ready = sem("yslot_ready")
        base_ready = sem("base_ready")
        gathered = [sem(f"gathered{n}") for n in range(2)]
        combined = sem("combined")
        x_in = [[sem(f"x_in{n}_{u}") for u in range(UNROLL[n])] for n in range(2)]
        w_in = [[sem(f"w_in{n}_{u}") for u in range(UNROLL[n])] for n in range(2)]
        bias_up = sem("bias_up")
        th_ready = sem("th_ready")
        hs_ready = sem("hs_ready")
        y_out = [sem(f"y_out{n}") for n in range(2)]
        y_copied = [sem(f"y_copied{n}") for n in range(2)]
        out_done = sem("out_done")

        def J(b, *what):
            return job[(b, *what)]

        def obank(layer, what):
            return "O" if layer else "M"

        def pvbank(layer, g):
            return "M" if layer and g == 2 else "O"

        def pvjob(layer, b, g):
            bk = pvbank(layer, g)
            return bk, J(bk, "pv", layer, b, g if layer else 0)

        S_OFF = (0, B * NG)

        block = ctx.enter_context(nc.Block())

        @block.sync
        def _(sp):
            xv = x.rearrange("b t d -> t b d")
            sp.dma_start(X[:, 0:4, :], xv[:, 0:4, :]).then_inc(ld_x[0], 16)
            sp.dma_start(X[:, 4:8, :], xv[:, 4:8, :]).then_inc(ld_x[1], 16)
            sp.dma_start(qw_sb[:], q_w).then_inc(ld_a, 16)
            sp.dma_start(qb_sb[:], q_b).then_inc(ld_a, 16)
            sp.dma_start(pb_sb[:], proj_b.partition_broadcast(128)).then_inc(ld_b, 16)
            sp.dma_start(pw_sb[:], proj_w).then_inc(ld_b, 16)
            sp.dma_start(ns_sb[:], norm_s.partition_broadcast(128)).then_inc(ld_b, 16)
            sp.dma_start(wg_sb[:], wg).then_inc(ld_b, 16)
            sp.dma_start(bg_sb[:], bg.partition_broadcast(128)).then_inc(ld_b, 16)
            sp.dma_start(b20_sb[:], b2_0).then_inc(ld_b, 16)
            sp.wait_ge(zero_set, 1)
            xz = xs_dram[0:REGION * E[0] * 128, :].rearrange("(e r p) d -> r p e d", r=REGION, p=128)
            for r in range(REGION):
                sp.dma_start(xz[r], zeros[:, None, :].to_broadcast([128, E[0], D])).then_inc(zeroed[r], 16)
            sp.dma_start(xs_dram[REGION * E[0] * 128:rows, :], zeros[:, :]).then_inc(zeroed[REGION - 1], 16)
            sp.dma_start(Wk_sb[:], Wk).then_inc(ld_c, 16)
            sp.dma_start(Wv_sb[:], Wv).then_inc(ld_c, 16)
            sp.dma_start(Wq_sb[:], Wq).then_inc(ld_c, 16)
            sp.dma_start(Wo_sb[:], Wo).then_inc(ld_c, 16)
            sp.dma_start(bo_sb[:], bo.partition_broadcast(128)).then_inc(ld_c, 16)
            sp.dma_start(Wr_sb[:], Wr).then_inc(ld_c, 16)
            sp.dma_start(br_sb[:], br.partition_broadcast(128)).then_inc(ld_c, 16)
            sp.dma_start(b21_sb[:], b2_1).then_inc(ld_c, 16)

            for layer in range(2):
                U = UNROLL[layer]
                turns = TILES[layer] // U
                wp, wbuf = ((wp0, w0), (wp1, w1))[layer]
                sp.wait_ge(freed["O"], J("O", "table", layer))
                sp.wait_ge(scattered[layer], 16 * B * TOPK[layer])
                sp.wait_ge(zeroed[REGION - 1], 32)
                lb = [J(f"T{u // 2}", "loop", layer) for u in range(U)] if layer == 0 else [J(f"T{u}", "loop", 1) for u in range(U)]

                def turn(i, first):
                    for u in range(U):
                        j = i * U + u
                        tb = f"T{u // 2}" if layer == 0 else f"T{u}"
                        row = sp.value_load(table[0:1, bass.ds(j, 1)], min_val=0, max_val=REGION * E[layer])
                        row = sp.snap(row * 128)
                        own_weights = layer == 1 or u % 2 == 1
                        if own_weights:
                            ex = sp.value_load(table[0:1, bass.ds(j + TILES[layer], 1)], min_val=0, max_val=E[layer] - 1)
                        if not first:
                            sp.wait_ge(filled[tb], i + J(tb, "loop", layer))
                        sp.dma_start(xin[:, u, :], xs_dram[bass.ds(row, 128), :]).then_inc(x_in[layer][u], 16)
                        if own_weights:
                            if not first:
                                yb = ("O", "M")[u // 2] if layer == 0 else ("O", "M")[u]
                                sp.wait_ge(filled[yb], i + J(yb, "loop", layer))
                            sp.dma_start(wbuf[:, u, :], wp[bass.ds(ex, 1), :, :].rearrange("e p n -> p (e n)"))\
                                .then_inc(w_in[layer][u], 16)

                turn(0, True)
                with sp.Fori(1, turns) as i:
                    turn(i, False)
            for n in range(2):
                sp.wait_ge(y_out[n], 16 * (TILES[n] // UNROLL[n]))
            sp.wait_ge(out_done, 16 * B)

        @block.gpsimd
        def _(pool):
            steps = [0]

            def link(ins):
                steps[0] += 1
                ins.then_inc(pool_step, 1)
                pool.wait_ge(pool_step, steps[0])

            nc.gpsimd.memset(zeros[:], 0.0).then_inc(zero_set, 1)
            nc.gpsimd.memset(V0[:], 1.0).then_inc(ones_v, 1)
            nc.gpsimd.memset(V1[:], 1.0).then_inc(ones_v, 1)

            def rsqrt_eps(dst, tmp, src, n):
                link(nc.gpsimd.tensor_scalar(tmp, src, EPS, None, ALU.add))
                return nc.gpsimd.tensor_tensor(dst, tmp, C[:, C_NH:C_NH + 1].to_broadcast([128, n]) if n > 1 else C[:, C_NH:C_NH + 1], ALU.pow)

            pool.wait_ge(ld_a, LD_A)
            pool.wait_ge(ln_stats, 1)
            for b in range(B):
                ins = rsqrt_eps(rstd[:, b:b + 1], var_eps[:, b:b + 1], mv[:, b, 1:2], 1)
                ins.then_inc(ln_rstd, 1)
            pool.wait_ge(ld_b, LD_B)
            for b in range(B):
                nc.gpsimd.tensor_tensor(XB[:, b, :], X[:, b, :], pb_sb[:], ALU.add).then_inc(xb_ready, 1)

            def route_rstd(layer, b):
                pool.wait_ge(rt_stats, layer * B + b + 1)
                if layer == 0:
                    link(rsqrt_eps(rstd[:, b:b + 1], var_eps[:, b:b + 1], mv[:, b, 1:2], 1))
                    link(nc.gpsimd.tensor_scalar(rms[:, b:b + 1], mv[:, b, 1:2], rstd[:, b:b + 1], rstd[:, b:b + 1],
                                                 ALU.mult, ALU.mult))
                    rsqrt_eps(rrms[:, b:b + 1], var_eps[:, b:b + 1], rms[:, b:b + 1], 1).then_inc(rt_rstd, 1)
                else:
                    rsqrt_eps(rstd[:, b:b + 1], var_eps[:, b:b + 1], mv[:, b, 1:2], 1).then_inc(rt_rstd, 1)

            def scatter(layer, b):
                pool.wait_ge(slot_ready, layer * B + b + 1)
                if layer == 0:
                    pool.wait_ge(zeroed[b], 16)
                for k in range(TOPK[layer]):
                    nc.gpsimd.indirect_dma_start(
                        out=xs_dram, out_offset=bass.IndirectOffsetOnAxis(ap=slot_u[:, b, k:k + 1], axis=0),
                        in_=XN[:, b, :], in_offset=None).then_inc(scattered[layer], 16)

            def gather(layer, b):
                if b >= 2:
                    pool.wait_ge(combined, layer * B + b - 1)
                for k in range(TOPK[layer]):
                    nc.gpsimd.indirect_dma_start(
                        out=G[:, b % 2, k, :], out_offset=None, in_=ys_dram[layer],
                        in_offset=bass.IndirectOffsetOnAxis(ap=yslot[:, b, k:k + 1], axis=0))\
                        .then_inc(gathered[b % 2], 16)

            def ln_pow(b):
                pool.wait_ge(ln_stats, b + 2)
                rsqrt_eps(rstd[:, b:b + 1], var_eps[:, b:b + 1], mv[:, b, 1:2], 1).then_inc(ln_rstd, 1)

            for b in range(B + 3):
                if 0 <= b - 1 < B:
                    route_rstd(0, b - 1)
                if 0 <= b - 3 < B:
                    scatter(0, b - 3)

            pool.wait_ge(freed["O"], J("O", "table", 0))

            def turn(i, first):
                for u in (0, 2):
                    j = i * UNROLL[0] + u
                    ex = pool.value_load(table[0:1, bass.ds(j + TILES[0], 1)], min_val=0, max_val=E[0] - 1)
                    if not first:
                        yb = ("O", "M")[u // 2]
                        pool.wait_ge(filled[yb], i + J(yb, "loop", 0))
                    pool.dma_start(w0[:, u, :], wp0[bass.ds(ex, 1), :, :].rearrange("e p n -> p (e n)"))\
                        .then_inc(w_in[0][u], 16)
                for u in range(UNROLL[0]):
                    pool.wait_ge(w_in[0][u], i * 16 + 16)
                    nc.gpsimd.tensor_tensor(w0[:, u, 385:386], w0[:, u, 385:386], ones[:, 0:1], ALU.add)\
                        .then_inc(bias_up, 1)

            turn(0, True)
            with pool.Fori(1, TILES[0] // UNROLL[0]) as i:
                turn(i, False)

            pool.wait_ge(yslot_ready, 1)
            pool.wait_ge(y_out[0], 16 * (TILES[0] // UNROLL[0]))
            gather(0, 0)
            gather(0, 1)
            ln_pow(0)
            gather(0, 2)
            ln_pow(1)
            for b in range(B + 3):
                if b + 3 < B:
                    gather(0, b + 3)
                if b + 2 < B:
                    ln_pow(b + 2)
                if 0 <= b - 1 < B:
                    route_rstd(1, b - 1)
                if 0 <= b - 3 < B:
                    scatter(1, b - 3)
            pool.wait_ge(yslot_ready, 2)
            pool.wait_ge(y_out[1], 16 * (TILES[1] // UNROLL[1]))
            pool.wait_ge(combined, B)
            for b in range(B):
                gather(1, b)

        @block.scalar
        def _(act):
            act.dma_start(C[:], cst).then_inc(ld_a, 16)
            act.dma_start(ctx_sb[:], ctxT).then_inc(ld_a, 16)
            act.dma_start(kvw_sb[:], kv_w).then_inc(ld_a, 16)
            act.dma_start(kvb_sb[:], kv_b).then_inc(ld_a, 16)

            def copy_out(bk, n, dst, src, func=ACT.Copy, **kw):
                act.wait_ge(filled[bk], n)
                nc.scalar.activation(dst, src, func, **kw).then_inc(freed[bk], 1)

            act.wait_ge(ld_a, LD_A)
            act.wait_ge(ones_v, 2)
            for n in range(2):
                bk = ("O", "M")[n]
                copy_out(bk, J(bk, "v0", n), V0[:, 4 * n:4 * n + 4, :, 0:8],
                         bank[bk][0:M, :].rearrange("p (b h d) -> p b h d", b=4, h=NH))
            copy_out("S0", J("S0", "xT0", 0), XT0[:, 0:512], bank["S0"][:])
            copy_out("S2", J("S2", "q0", 0), QT0[:, 0:512], bank["S2"][:], ACT.Identity, bias=qb_sb[:, 0:1])

            def exps(layer, b, g):
                act.wait_ge(freed[f"S{g}"], J(f"S{g}", "scores", layer, b, g))
                pg = P[:, b % 2, g, :]
                nc.scalar.activation(pg, pg, ACT.Exp, scale=float(HD[layer]) ** -0.5).then_inc(exp_done, 1)

            def pT_out(layer, b, g):
                if b > 0:
                    bk, n = pvjob(layer, b - 1, g)
                    act.wait_ge(filled[bk], n)
                elif layer:
                    bk, n = pvjob(0, B - 1, g)
                    act.wait_ge(filled[bk], n)
                bk = f"T{g % 2}"
                copy_out(bk, J(bk, "pT", layer, b, g), PT[:, g, :], bank[bk][0:M, :])

            def xT_out(b):
                if b > 0:
                    act.wait_ge(filled["M"], J("M", "q", b - 1, 1))
                copy_out("M", J("M", "xT", b), XT1[:], bank["M"][:, 0:128])

            def q_out(b, n):
                if b >= 2:
                    act.wait_ge(filled["S3"], J("S3", "scores", 1, b - 2, 3))
                copy_out("M", J("M", "q", b, n), QT1[:, b % 2, 4 * n:4 * n + 4, :],
                         bank["M"][:, :].rearrange("p (c t) -> p c t", c=4))

            def attention(layer):
                for g in range(NG):
                    exps(layer, 0, g)
                for b in range(B + 3):
                    if layer and b + 1 < B:
                        xT_out(b + 1)
                    for n in range(layer + 1):
                        if 0 <= b - 1 < B:
                            bk = obank(layer, "oT")
                            if b - 2 >= 0:
                                act.wait_ge(filled[bk], J(bk, "proj", layer, b - 2))
                            elif layer:
                                act.wait_ge(filled["M"], J("M", "proj", 0, B - 1))
                            if layer:
                                copy_out(bk, J(bk, "oT", layer, b - 1, n), OT[:, 4 * n:4 * n + 4, :],
                                         bank[bk][:].rearrange("p (c t) -> p c t", c=4))
                            else:
                                copy_out(bk, J(bk, "oT", layer, b - 1, n), OT[:, 0, :], bank[bk][:, 0:128],
                                         ACT.Identity, bias=kvb_sb[:, 1:2])
                        if layer and b + 1 < B:
                            q_out(b + 1, n)
                    if b < B:
                        pT_out(layer, b, 0)
                    if 0 <= b - 2 < B:
                        if b - 3 >= 0:
                            act.wait_ge(filled["M"], J("M", "logits", layer, b - 3))
                        elif layer:
                            act.wait_ge(filled["M"], J("M", "logits", 0, B - 1))
                        copy_out("M", J("M", "xnT", layer, b - 2), XNT[:], bank["M"][:, 0:128])
                    if b < B:
                        for g in range(1, NG):
                            pT_out(layer, b, g)
                    if b + 1 < B:
                        exps(layer, b + 1, 0)
                        exps(layer, b + 1, 1)
                    if 0 <= b - 2 < B:
                        act.wait_ge(vdif_ready, layer * B + b - 1)
                        w = (4, 8)[layer]
                        nc.scalar.activation(vexp[:, b - 2, 0:w], vdif[:, b - 2, 0:w], ACT.Exp,
                                             accum_out=vsum[:, b - 2:b - 1]).then_inc(vexp_ready, 1)
                    if b + 1 < B:
                        exps(layer, b + 1, 2)
                        exps(layer, b + 1, 3)

            def gT_out(layer):
                for n in range(2):
                    bk = f"T{n}"
                    copy_out(bk, J(bk, "gT", layer, n), gfT[0:E[layer], 512 * n:512 * n + 512],
                             bank[bk][0:E[layer], :])

            attention(0)
            for n in range(16):
                bk = f"S{n % 4}"
                c, half = n // 2, n % 2
                copy_out(bk, J(bk, "k1", n), K1[:, c, 308 * half:308 * half + 308], bank[bk][:, 0:308])
                if n == 7:
                    gT_out(0)

            def turn0(i):
                for q in range(2):
                    tb, yb = f"T{q}", ("O", "M")[q]
                    s2 = slice(2 * q, 2 * q + 2)
                    act.wait_ge(filled[tb], i + 1 + J(tb, "loop", 0))
                    nc.scalar.activation(xeT[:, s2, :], bank[tb][:, 0:256].rearrange("p (u t) -> p u t", u=2),
                                         ACT.Copy).then_inc(freed[tb], 1)
                for q in range(2):
                    s2 = slice(2 * q, 2 * q + 2)
                    for u in (2 * q, 2 * q + 1):
                        act.wait_ge(freed[f"S{u}"], i + 1 + J(f"S{u}", "loop", 0))
                    nc.scalar.activation(th[:, s2, :], ha[:, s2, :], ACT.Tanh, scale=ALPHA / 2).then_inc(th_ready, 1)
                for q in range(2):
                    yb = ("O", "M")[q]
                    s2 = slice(2 * q, 2 * q + 2)
                    act.wait_ge(filled[yb], i + 1 + J(yb, "loop", 0))
                    nc.scalar.activation(yo[:, s2, :], bank[yb][:, 0:256].rearrange("p (u t) -> p u t", u=2),
                                         ACT.Copy, scale=0.5).then_inc(freed[yb], 1)
                for q in range(2):
                    yb = ("O", "M")[q]
                    act.wait_ge(freed[yb], i + 1 + J(yb, "loop", 0))
                act.dma_start(ys_dram[0][bass.ds(i * 512, 512), :].rearrange("(u p) d -> p u d", p=128),
                              yo[:, :, :]).then_inc(y_out[0], 16)
                act.wait_ge(y_out[0], 16 * i + 16)

            turn0(0)
            with act.Fori(1, TILES[0] // UNROLL[0]) as i:
                turn0(i)

            for n in range(16):
                bk = f"S{n % 4}"
                b, half = n // 2, n % 2
                copy_out(bk, J(bk, "v1", n), V1[:, b, 8 * half:8 * half + 8, 0:64],
                         bank[bk][0:M, :].rearrange("p (h d) -> p h d", h=8))
            xT_out(0)
            q_out(0, 0)
            q_out(0, 1)
            attention(1)
            gT_out(1)

            def turn1(i):
                for u in range(2):
                    tb = f"T{u}"
                    act.wait_ge(filled[tb], i + 1 + J(tb, "loop", 1))
                    nc.scalar.activation(xeT[:, u, :], bank[tb][:, 0:128], ACT.Copy).then_inc(freed[tb], 1)
                for u in range(2):
                    hbk = f"S{2 * u}"
                    act.wait_ge(filled[hbk], i + 1 + J(hbk, "loop", 1))
                    for c in range(2):
                        ins = nc.scalar.activation(h1[u][:, c, :], bank[hbk][:, 128 * c:128 * c + 128], ACT.Relu,
                                                   bias=w1[:, u, 1024 + c:1025 + c])
                    ins.then_inc(freed[hbk], 1)
                for u in range(2):
                    yb = ("O", "M")[u]
                    act.wait_ge(filled[yb], i + 1 + J(yb, "loop", 1))
                    nc.scalar.activation(yo[:, u, :], bank[yb][:, 0:128], ACT.Copy).then_inc(freed[yb], 1)
                for u in range(2):
                    yb = ("O", "M")[u]
                    act.wait_ge(freed[yb], i + 1 + J(yb, "loop", 1))
                act.dma_start(ys_dram[1][bass.ds(i * 256, 256), :].rearrange("(u p) d -> p u d", p=128),
                              yo[:, 0:2, :]).then_inc(y_out[1], 16)
                act.wait_ge(y_out[1], 16 * i + 16)

            turn1(0)
            with act.Fori(1, TILES[1] // UNROLL[1]) as i:
                turn1(i)

            for b in range(B):
                act.wait_ge(combined, B + b + 1)
                act.dma_start(out[b], X[:, b, :]).then_inc(out_done, 16)

        @block.vector
        def _(dve):
            steps = [0]

            def link(ins):
                steps[0] += 1
                ins.then_inc(dve_step, 1)
                dve.wait_ge(dve_step, steps[0])

            def stats(src, b):
                link(nc.vector.bn_stats(st6[:, b, :], src))
                return nc.vector.bn_aggr(mv[:, b, :], st6[:, b, :])

            for b in range(B):
                dve.wait_ge(ld_x[b // 4], 16)
                ins = stats(X[:, b, :], b)
            ins.then_inc(ln_stats, 1)

            dve.wait_ge(ld_a, LD_A)
            for n in range(2):
                bk = f"T{n}"
                dve.wait_ge(filled[bk], J(bk, "k0", n))
                for j in range(GH):
                    ins = nc.vector.tensor_scalar(KX0[:, j, 308 * n:308 * n + 308], bank[bk][:, 0:308],
                                                  kvb_sb[:, 0:1], C[:, C_HEAD + j:C_HEAD + j + 1], ALU.add, ALU.mult)
                ins.then_inc(freed[bk], 1)
            for b in range(B):
                dve.wait_ge(ln_rstd, b + 1)
                nc.vector.tensor_scalar(XA[:, b, :], X[:, b, :], mv[:, b, 0:1], rstd[:, b:b + 1],
                                        ALU.subtract, ALU.mult).then_inc(xa_ready, 1)
            dve.wait_ge(filled["S1"], J("S1", "xT0", 1))
            nc.vector.tensor_copy(XT0[:, 512:1024], bank["S1"][:]).then_inc(freed["S1"], 1)
            dve.wait_ge(filled["S3"], J("S3", "q0", 1))
            nc.vector.tensor_scalar(QT0[:, 512:1024], bank["S3"][:], qb_sb[:, 0:1], None, ALU.add)\
                .then_inc(freed["S3"], 1)

            def shift(layer, b, g):
                bk = f"S{g}"
                sc = bank[bk][:, 0:GM].rearrange("p (h m) -> p h m", h=GH)
                dve.wait_ge(filled[bk], J(bk, "scores", layer, b, g))
                link(nc.vector.tensor_reduce(negmax[:, g, :], sc, AX_X, ALU.max, negate=True))
                tb = f"T{g % 2}"
                if b >= 2:
                    dve.wait_ge(filled[tb], J(tb, "pT", layer, b - 2, g))
                elif layer:
                    dve.wait_ge(filled[tb], J(tb, "pT", 0, B - 2 + b, g))
                nc.vector.tensor_tensor(P[:, b % 2, g, :].rearrange("p (h m) -> p h m", h=GH), sc,
                                        negmax[:, g, :, None].to_broadcast([128, GH, M]), ALU.add)\
                    .then_inc(freed[bk], 1)

            def pv_out(layer, b, g):
                bk, n = pvjob(layer, b, g)
                d = HD[layer]
                heads = GH if layer else NH
                o = bank[bk][:, 0:heads * (d + 1)].rearrange("p (h e) -> p h e", h=heads)
                dve.wait_ge(filled[bk], n)
                link(nc.vector.reciprocal(recip[:, g, 0:heads], o[:, :, d]))
                if b > 0:
                    ob = obank(layer, "oT")
                    dve.wait_ge(filled[ob], J(ob, "oT", layer, b - 1, layer))
                elif layer:
                    dve.wait_ge(filled["M"], J("M", "oT", 0, B - 1, 0))
                if layer:
                    h0 = 8 * (g // 2) + g % 2
                    dst = OS[:, :].rearrange("p (h d) -> p h d", d=64)[:, h0:h0 + 7:2, :]
                else:
                    dst = OS[:, 0:128].rearrange("p (h d) -> p h d", d=8)
                nc.vector.tensor_tensor(dst, o[:, :, 0:d], recip[:, g, 0:heads, None].to_broadcast([128, heads, d]),
                                        ALU.mult).then_inc(freed[bk], 1)

            def proj_out(layer, b):
                bk = obank(layer, "proj")
                dve.wait_ge(filled[bk], J(bk, "proj", layer, b))
                if layer == 0:
                    dve.wait_ge(xb_ready, b + 1)
                base = XB[:, b, :]
                ins = nc.vector.tensor_tensor(XR[:, b, :], bank[bk][:, 0:128], base, ALU.add)
                ins.then_inc(freed[bk], 1)
                dve.wait_ge(freed[bk], J(bk, "proj", layer, b))
                stats(XR[:, b, :], b).then_inc(rt_stats, 1)

            def normed(layer, b):
                dve.wait_ge(rt_rstd, layer * B + b + 1)
                if layer == 0:
                    link(nc.vector.tensor_scalar(XF[:, b, :], XR[:, b, :], mv[:, b, 0:1], rstd[:, b:b + 1],
                                                 ALU.subtract, ALU.mult))
                    nc.vector.scalar_tensor_tensor(XN[:, b, :], XF[:, b, :], rrms[:, b:b + 1], ns_sb[:],
                                                   ALU.mult, ALU.mult).then_inc(xn_ready, 1)
                else:
                    nc.vector.tensor_scalar(XN[:, b, :], XR[:, b, :], mv[:, b, 0:1], rstd[:, b:b + 1],
                                            ALU.subtract, ALU.mult).then_inc(xn_ready, 1)

            def choose(layer, b):
                e, k = E[layer], TOPK[layer]
                dve.wait_ge(filled["M"], J("M", "logits", layer, b))
                nc.vector.tensor_tensor(lg[:, 0:e], bank["M"][:, 0:e], br_l[layer][:, 0:e], ALU.add)\
                    .then_inc(freed["M"], 1)
                dve.wait_ge(freed["M"], J("M", "logits", layer, b))
                link(nc.vector.max(top8[:], lg[:, 0:e]))
                link(nc.vector.max_index(idx8[:], top8[:], lg[:, 0:e]))
                src = top8[:, 0:4] if layer == 0 else lg[:, 0:8]
                nc.vector.tensor_scalar(vdif[:, b, 0:(4, 8)[layer]], src, top8[:, 0:1], None, ALU.subtract)\
                    .then_inc(vdif_ready, 1)
                link(nc.vector.tensor_tensor(hot[:, b, 0:k, 0:e],
                                             C[:, None, C_IOTA:C_IOTA + e].to_broadcast([128, k, e]),
                                             idx8[:, 0:k, None].to_broadcast([128, k, e]), ALU.is_equal))
                if k > 1:
                    link(nc.vector.tensor_reduce(mask[:, b, 0:e],
                                                 hot[:, b, 0:k, 0:e].rearrange("p k e -> p e k"), AX_X, ALU.add))
                else:
                    link(nc.vector.tensor_copy(mask[:, b, 0:e], hot[:, b, 0, 0:e]))
                if b == 0:
                    nc.vector.tensor_copy(mcum[:, b, 0:e], mask[:, b, 0:e]).then_inc(mask_ready, 1)
                else:
                    nc.vector.tensor_tensor(mcum[:, b, 0:e], mcum[:, b - 1, 0:e], mask[:, b, 0:e], ALU.add)\
                        .then_inc(mask_ready, 1)

            def place(layer, b):
                e, k = E[layer], TOPK[layer]
                n = J("M", "rank", layer, b)
                dve.wait_ge(filled["M"], n)
                nc.vector.tensor_tensor(posm[:, 0:e], bank["M"][:, 0:e], C[:, C_RB:C_RB + e], ALU.add)\
                    .then_inc(freed["M"], 1)
                dve.wait_ge(freed["M"], n)
                link(nc.vector.tensor_tensor(prod[:, 0:k, 0:e], hot[:, b, 0:k, 0:e],
                                             posm[:, None, 0:e].to_broadcast([128, k, e]), ALU.mult))
                link(nc.vector.tensor_reduce(slot_f[:, b, 0:k], prod[:, 0:k, 0:e], AX_X, ALU.add))
                nc.vector.tensor_copy(slot_u[:, b, 0:k], slot_f[:, b, 0:k]).then_inc(slot_ready, 1)

            def combine(layer, b):
                k = TOPK[layer]
                dst = (X2, X)[layer]
                nth = b // 2 + 1 + (B // 2 * layer)
                per = 16 * k
                total = per * (b // 2 + 1) + (16 * TOPK[0] * (B // 2) if layer else 0)
                dve.wait_ge(gathered[b % 2], total)
                for j in range(k):
                    ins = nc.vector.scalar_tensor_tensor(dst[:, b, :], G[:, b % 2, j, :], gates[:, b, j:j + 1],
                                                         XR[:, b, :] if j == 0 else dst[:, b, :], ALU.mult, ALU.add)
                    if j < k - 1:
                        link(ins)
                ins.then_inc(combined, 1)
                if layer == 0:
                    dve.wait_ge(combined, b + 1)
                    nc.vector.tensor_tensor(XB[:, b, :], X2[:, b, :], bo_sb[:], ALU.add)
                    stats(X2[:, b, :], b).then_inc(ln_stats, 1)

            def attn_norm(b):
                dve.wait_ge(ln_rstd, B + b + 1)
                nc.vector.tensor_scalar(XA[:, b, :], X2[:, b, :], mv[:, b, 0:1], rstd[:, b:b + 1],
                                        ALU.subtract, ALU.mult).then_inc(xa_ready, 1)

            def attention(layer):
                for g in range(NG):
                    shift(layer, 0, g)
                for b in range(B + 3):
                    if 0 <= b - 1 < B:
                        proj_out(layer, b - 1)
                    if b < B and layer:
                        pv_out(layer, b, 0)
                    if layer and b + 2 < B:
                        combine(0, b + 2)
                    if 0 <= b - 2 < B:
                        choose(layer, b - 2)
                    if b < B and layer:
                        pv_out(layer, b, 1)
                    if 0 <= b - 1 < B:
                        normed(layer, b - 1)
                    if 0 <= b - 3 < B:
                        place(layer, b - 3)
                    if b + 1 < B:
                        shift(layer, b + 1, 0)
                        shift(layer, b + 1, 1)
                    if b < B:
                        pv_out(layer, b, 2 if layer else 0)
                    if b + 1 < B:
                        shift(layer, b + 1, 2)
                    if b < B and layer:
                        pv_out(layer, b, 3)
                    if b + 1 < B:
                        shift(layer, b + 1, 3)
                    if layer and b + 2 < B:
                        attn_norm(b + 2)

            def tables(layer):
                e, k = E[layer], TOPK[layer]
                nc_ = e * CAND
                o = C_PL + layer * C_PL_W
                nt = TILES[layer]
                nc.vector.tensor_copy(mexp[:, 0:e, :], mcum[:, B - 1, 0:e, None].to_broadcast([128, e, CAND]))\
                    .then_inc(mexp_ready, 1)
                dve.wait_ge(vexp_ready, layer * B + B)
                link(nc.vector.reciprocal(vrec[:], vsum[:]))
                if k > 1:
                    link(nc.vector.tensor_tensor(gates[:, :, 0:k], vexp[:, :, 0:k],
                                                 vrec[:, :, None].to_broadcast([128, B, k]), ALU.mult))
                else:
                    link(nc.vector.tensor_copy(gates[:, :, 0], vrec[:]))
                dve.wait_ge(filled["O"], J("O", "count", layer))
                nc.vector.tensor_tensor(act_c[0:nc_, :], bank["O"][0:nc_, 0:1], C[0:nc_, o:o + 1], ALU.is_gt)\
                    .then_inc(freed["O"], 1)
                dve.wait_ge(freed["O"], J("O", "count", layer))
                nc.vector.tensor_scalar(act_bc[0:nc_, :], C[0:nc_, C_ONE:C_ONE + 128], act_c[0:nc_, :], None, ALU.mult)\
                    .then_inc(act_ready, 1)
                dve.wait_ge(filled["O"], J("O", "pos", layer))
                nc.vector.tensor_copy(pos_c[0:nc_, :], bank["O"][0:nc_, 0:1]).then_inc(freed["O"], 1)
                dve.wait_ge(freed["O"], J("O", "pos", layer))
                nc.vector.tensor_scalar(ohj[0:nc_, 0:nt], C[0:nc_, C_IOTA:C_IOTA + nt], pos_c[0:nc_, :],
                                        act_c[0:nc_, :], ALU.is_equal, ALU.mult).then_inc(ohj_ready, 1)
                dve.wait_ge(filled["O"], J("O", "table", layer))
                nc.vector.tensor_scalar(table[0:1, 0:nt], bank["O"][0:1, 0:nt], float(REGION * e), None, ALU.add)
                ins = nc.vector.tensor_copy(table[0:1, nt:2 * nt], bank["O"][0:1, nt:2 * nt])
                ins.then_inc(freed["O"], 1)
                dve.wait_ge(freed["O"], J("O", "table", layer))
                dve.wait_ge(filled["M"], J("M", "start", layer))
                nc.vector.tensor_tensor(region_shift[:, 0:e], bank["M"][:, 0:e], C[:, C_RB:C_RB + e], ALU.subtract)\
                    .then_inc(freed["M"], 1)
                dve.wait_ge(freed["M"], J("M", "start", layer))
                for b in range(B):
                    ins = nc.vector.tensor_tensor(gfp[:, b, 0:k, 0:e], hot[:, b, 0:k, 0:e],
                                                  region_shift[:, None, 0:e].to_broadcast([128, k, e]), ALU.mult)
                link(ins)
                for b in range(B):
                    ins = nc.vector.tensor_reduce(red[:, b, 0:k], gfp[:, b, 0:k, 0:e], AX_X, ALU.add)
                link(ins)
                nc.vector.tensor_tensor(yslot[:, :, 0:k], red[:, :, 0:k], slot_f[:, :, 0:k], ALU.add)\
                    .then_inc(yslot_ready, 1)
                for b in range(B):
                    ins = nc.vector.tensor_tensor(gfp[:, b, 0:k, 0:e], hot[:, b, 0:k, 0:e],
                                                  gates[:, b, 0:k, None].to_broadcast([128, k, e]), ALU.mult)
                link(ins)
                for b in range(B):
                    ins = nc.vector.tensor_reduce(gf[:, b, 0:e], gfp[:, b, 0:k, 0:e].rearrange("p k e -> p e k"),
                                                  AX_X, ALU.add)
                ins.then_inc(gf_ready, 1)

            def base(layer):
                if layer == 0:
                    link(nc.vector.tensor_tensor(XR[:], XR[:], XF[:], ALU.add))
                for n in range(2):
                    bk = f"T{n}"
                    dve.wait_ge(filled[bk], J(bk, "b2", layer, n))
                    xr = XR[:, 4 * n:4 * n + 4, :]
                    nc.vector.tensor_tensor(xr, bank[bk][:].rearrange("p (b d) -> p b d", b=4), xr, ALU.add)\
                        .then_inc(freed[bk], 1)
                dve.wait_ge(freed["T1"], J("T1", "b2", layer, 1))

            attention(0)
            tables(0)
            base(0)

            def turn0(i):
                for u in range(4):
                    hbk = f"S{u}"
                    n = i + 1 + J(hbk, "loop", 0)
                    dve.wait_ge(filled[hbk], n)
                    dve.wait_ge(bias_up, 4 * i + u + 1)
                    nc.vector.tensor_scalar(ha[:, u, :], bank[hbk][:, 0:128], w0[:, u, 384:385], LIMIT, ALU.add, ALU.min)
                    nc.vector.tensor_scalar(hb[:, u, :], bank[hbk][:, 128:256], w0[:, u, 385:386], LIMIT + 1.0,
                                            ALU.add, ALU.min).then_inc(freed[hbk], 1)
                    dve.wait_ge(freed[hbk], n)
                for q in range(2):
                    s2 = slice(2 * q, 2 * q + 2)
                    dve.wait_ge(th_ready, 2 * i + q + 1)
                    nc.vector.scalar_tensor_tensor(hu[:, s2, :], th[:, s2, :], 1.0, ha[:, s2, :], ALU.add, ALU.mult)\
                        .then_inc(y_copied[0], 1)
                    dve.wait_ge(y_copied[0], 2 * i + q + 1)
                    nc.vector.scalar_tensor_tensor(hs[:, s2, :], hb[:, s2, :], 1.0 - LIMIT, hu[:, s2, :],
                                                   ALU.max, ALU.mult).then_inc(hs_ready, 1)

            turn0(0)
            with dve.Fori(1, TILES[0] // UNROLL[0]) as i:
                turn0(i)

            dve.wait_ge(ld_c, LD_C)
            combine(0, 0)
            combine(0, 1)
            attn_norm(0)
            attn_norm(1)
            attention(1)
            tables(1)
            base(1)

            def turn1(i):
                for u in range(2):
                    hbk = f"S{2 * u + 1}"
                    dve.wait_ge(filled[hbk], i + 1 + J(hbk, "loop", 1))
                    for c in range(2):
                        ins = nc.vector.tensor_scalar(h1[u][:, 2 + c, :], bank[hbk][:, 128 * c:128 * c + 128],
                                                      w1[:, u, 1026 + c:1027 + c], 0.0, ALU.add, ALU.max)
                    ins.then_inc(freed[hbk], 1)

            turn1(0)
            with dve.Fori(1, TILES[1] // UNROLL[1]) as i:
                turn1(i)
            for b in range(B):
                combine(1, b)

        @block.tensor
        def _(pe):
            def use(bk, n):
                if n > 1:
                    pe.wait_ge(freed[bk], n - 1)
                return bank[bk]

            pe.wait_ge(ld_a, LD_A)
            for n in range(2):
                bk = f"T{n}"
                o = use(bk, J(bk, "k0", n))
                nc.tensor.matmul(o[:, 0:308], kvw_sb[:, 0:128], ctx_sb[:, 308 * n:308 * n + 308],
                                 start=True, stop=True).then_inc(filled[bk], 1)
            for n in range(2):
                bk = ("O", "M")[n]
                o = use(bk, J(bk, "v0", n))
                for c in range(4):
                    b = 4 * n + c
                    ins = nc.tensor.matmul(o[0:M, 128 * c:128 * c + 128], ctx_sb[:, M * b:M * b + M],
                                           kvw_sb[:, 128:256], start=True, stop=True)
                ins.then_inc(filled[bk], 1)
            for n in range(2):
                bk = f"S{n}"
                o = use(bk, J(bk, "xT0", n))
                for c in range(4):
                    pe.wait_ge(xa_ready, 4 * n + c + 1)
                    ins = nc.tensor.transpose(o[:, 128 * c:128 * c + 128], XA[:, 4 * n + c, :], ident)
                ins.then_inc(filled[bk], 1)
            for n in range(2):
                bk = f"S{2 + n}"
                o = use(bk, J(bk, "q0", n))
                pe.wait_ge(freed[f"S{n}"], J(f"S{n}", "xT0", n))
                nc.tensor.matmul(o[:], qw_sb[:], XT0[:, 512 * n:512 * n + 512], start=True, stop=True)\
                    .then_inc(filled[bk], 1)

            def scores(layer, b):
                if layer == 0 and b == 0:
                    for n in range(2):
                        pe.wait_ge(freed[f"T{n}"], J(f"T{n}", "k0", n))
                        pe.wait_ge(freed[f"S{2 + n}"], J(f"S{2 + n}", "q0", n))
                for g in range(NG):
                    use(f"S{g}", J(f"S{g}", "scores", layer, b, g))
                if layer == 0:
                    for g in range(NG):
                        r = slice(32 * g, 32 * g + 32)
                        nc.tensor.matmul(bank[f"S{g}"][:, 0:GM], QT0[r, T * b:T * b + T],
                                         KX0[r, :, M * b:M * b + M], start=True, stop=True)\
                            .then_inc(filled[f"S{g}"], 1)
                else:
                    pe.wait_ge(freed["M"], J("M", "q", b, 1))
                    if b == 0:
                        for n in range(4):
                            pe.wait_ge(freed[f"S{n}"], J(f"S{n}", "k1", 12 + n))
                    for h in range(NH):
                        r = slice(64 * (h % 2), 64 * (h % 2) + 64)
                        bk = f"S{2 * (h // 8) + h % 2}"
                        j = (h // 2) % 4
                        ins = nc.tensor.matmul(bank[bk][:, M * j:M * j + M], QT1[r, b % 2, h // 2, :],
                                               K1[r, h // 2, M * b:M * b + M], start=True, stop=True)
                        if j == 3:
                            ins.then_inc(filled[bk], 1)

            def probsT(layer, b, g):
                bk = f"T{g % 2}"
                o = use(bk, J(bk, "pT", layer, b, g))
                pe.wait_ge(exp_done, S_OFF[layer] + NG * b + g + 1)
                for j in range(GH):
                    ins = nc.tensor.transpose(o[0:M, 128 * j:128 * j + 128], P[:, b % 2, g, M * j:M * j + M], ident)
                ins.then_inc(filled[bk], 1)

            def pv(layer, b, g):
                bk, n = pvjob(layer, b, g)
                if layer or g == 0:
                    use(bk, n)
                if layer == 0 and b == 0 and g == 0:
                    for m in range(2):
                        pe.wait_ge(freed[("O", "M")[m]], J(("O", "M")[m], "v0", m))
                if layer == 1 and b == 0 and g == 0:
                    for m in range(4):
                        pe.wait_ge(freed[f"S{m}"], J(f"S{m}", "v1", 12 + m))
                tb = f"T{g % 2}"
                pe.wait_ge(freed[tb], J(tb, "pT", layer, b, g))
                d = HD[layer] + 1
                for j in range(GH):
                    h = 8 * (g // 2) + 2 * j + g % 2 if layer else GH * g + j
                    c = j if layer else h
                    v = (V0, V1)[layer]
                    ins = nc.tensor.matmul(bank[bk][:, d * c:d * c + d], PT[:, g, 128 * j:128 * j + 128],
                                           v[:, b, h, :], start=True, stop=True)
                if layer or g == NG - 1:
                    ins.then_inc(filled[bk], 1)

            def outT(layer, b, n):
                bk = obank(layer, "oT")
                o = use(bk, J(bk, "oT", layer, b, n))
                if layer:
                    if n == 0:
                        pe.wait_ge(freed["M"], J("M", "pv", 1, b, 2))
                        pe.wait_ge(freed["O"], J("O", "pv", 1, b, 3))
                    for c in range(4):
                        cc = 4 * n + c
                        ins = nc.tensor.transpose(o[:, 128 * c:128 * c + 128], OS[:, 128 * cc:128 * cc + 128], ident)
                else:
                    pe.wait_ge(freed["O"], J("O", "pv", 0, b, 0))
                    ins = nc.tensor.transpose(o[:, 0:128], OS[:, 0:128], ident)
                ins.then_inc(filled[bk], 1)

            def proj(layer, b):
                bk = obank(layer, "proj")
                o = use(bk, J(bk, "proj", layer, b))
                pe.wait_ge(freed[bk], J(bk, "oT", layer, b, layer))
                if layer == 0:
                    if b == 0:
                        pe.wait_ge(ld_b, LD_B)
                    ins = nc.tensor.matmul(o[:, 0:128], OT[:, 0, :], pw_sb[:], start=True, stop=True)
                else:
                    for c in range(8):
                        ins = nc.tensor.matmul(o[:, 0:128], OT[:, c, :], Wo_sb[:, c, :], start=(c == 0), stop=(c == 7))
                ins.then_inc(filled[bk], 1)

            def xnT(layer, b):
                o = use("M", J("M", "xnT", layer, b))
                pe.wait_ge(xn_ready, layer * B + b + 1)
                nc.tensor.transpose(o[:, 0:128], XN[:, b, :], ident).then_inc(filled["M"], 1)

            def logits(layer, b):
                o = use("M", J("M", "logits", layer, b))
                e = E[layer]
                nc.tensor.matmul(o[:, 0:e], XNT[:], wr_l[layer][:], start=True, stop=True).then_inc(filled["M"], 1)

            def rank(layer, b):
                o = use("M", J("M", "rank", layer, b))
                e = E[layer]
                pe.wait_ge(mask_ready, layer * B + b + 1)
                ins = nc.tensor.matmul(o[:, 0:e], before, mask[:, b, 0:e], start=True, stop=(b == 0))
                if b > 0:
                    ins = nc.tensor.matmul(o[:, 0:e], ones, mcum[:, b - 1, 0:e], start=False, stop=True)
                ins.then_inc(filled["M"], 1)

            def xT(b):
                o = use("M", J("M", "xT", b))
                pe.wait_ge(xa_ready, B + b + 1)
                nc.tensor.transpose(o[:, 0:128], XA[:, b, :], ident).then_inc(filled["M"], 1)

            def q(b, n):
                o = use("M", J("M", "q", b, n))
                pe.wait_ge(freed["M"], J("M", "xT", b))
                for c in range(4):
                    cc = 4 * n + c
                    ins = nc.tensor.matmul(o[:, 128 * c:128 * c + 128], Wq_sb[:, 128 * cc:128 * cc + 128], XT1[:],
                                           start=True, stop=True)
                ins.then_inc(filled["M"], 1)

            def attention(layer):
                for b in range(B + 3):
                    if layer and b + 1 < B:
                        xT(b + 1)
                    for n in range(layer + 1):
                        if 0 <= b - 1 < B:
                            outT(layer, b - 1, n)
                        if layer and b + 1 < B:
                            q(b + 1, n)
                    if b < B:
                        probsT(layer, b, 0)
                    if 0 <= b - 2 < B:
                        xnT(layer, b - 2)
                    if b < B:
                        probsT(layer, b, 1)
                    if 0 <= b - 1 < B:
                        proj(layer, b - 1)
                    if b < B:
                        pv(layer, b, 0)
                        probsT(layer, b, 2)
                    if 0 <= b - 2 < B:
                        logits(layer, b - 2)
                    if b < B:
                        pv(layer, b, 1)
                        probsT(layer, b, 3)
                    if 0 <= b - 3 < B:
                        rank(layer, b - 3)
                    if b + 1 < B:
                        scores(layer, b + 1)
                    if b < B:
                        pv(layer, b, 2)
                        pv(layer, b, 3)

            def tables(layer):
                e = E[layer]
                n = e * CAND
                o = C_PL + layer * C_PL_W
                nt = TILES[layer]
                ps = use("O", J("O", "count", layer))
                pe.wait_ge(mexp_ready, layer + 1)
                nc.tensor.matmul(ps[0:n, 0:1], mexp[:, 0:e, :].rearrange("p e t -> p (e t)"), ones[:, 0:1],
                                 start=True, stop=True).then_inc(filled["O"], 1)
                use("O", J("O", "pos", layer))
                pe.wait_ge(act_ready, layer + 1)
                nc.tensor.matmul(ps[0:n, 0:1], C[0:n, C_LT:C_LT + n], act_c[0:n, :], start=True, stop=True)\
                    .then_inc(filled["O"], 1)
                use("O", J("O", "table", layer))
                pe.wait_ge(ohj_ready, layer + 1)
                nc.tensor.matmul(ps[0:1, 0:nt], C[0:n, o + 1:o + 2], ohj[0:n, 0:nt], start=True, stop=True)
                nc.tensor.matmul(ps[0:1, nt:2 * nt], C[0:n, o + 2:o + 3], ohj[0:n, 0:nt], start=True, stop=True)\
                    .then_inc(filled["O"], 1)
                ps = use("M", J("M", "start", layer))
                nc.tensor.matmul(ps[:, 0:e], act_bc[0:n, :], C[0:n, o + 3:o + 3 + e], start=True, stop=True)\
                    .then_inc(filled["M"], 1)
                for m in range(2):
                    ps = use(f"T{m}", J(f"T{m}", "gT", layer, m))
                    pe.wait_ge(gf_ready, layer + 1)
                    for c in range(4):
                        ins = nc.tensor.transpose(ps[0:e, 128 * c:128 * c + 128], gf[:, 4 * m + c, 0:e], ident)
                    ins.then_inc(filled[f"T{m}"], 1)
                for m in range(2):
                    ps = use(f"T{m}", J(f"T{m}", "b2", layer, m))
                    for c in range(4):
                        b = 4 * m + c
                        ins = nc.tensor.matmul(ps[:, 128 * c:128 * c + 128], gfT[0:e, 128 * b:128 * b + 128],
                                               b2_l[layer][:], start=True, stop=True)
                    ins.then_inc(filled[f"T{m}"], 1)

            scores(0, 0)
            attention(0)
            pe.wait_ge(ld_c, LD_C)
            for n in range(16):
                bk = f"S{n % 4}"
                c, half = n // 2, n % 2
                o = use(bk, J(bk, "k1", n))
                nc.tensor.matmul(o[:, 0:308], Wk_sb[:, 128 * c:128 * c + 128], ctx_sb[:, 308 * half:308 * half + 308],
                                 start=True, stop=True).then_inc(filled[bk], 1)
                if n == 7:
                    tables(0)

            def turn0(i, first):
                for p in range(2):
                    tb = f"T{p}"
                    pe.wait_ge(freed[tb], i + J(tb, "loop", 0))
                    for u in (2 * p, 2 * p + 1):
                        pe.wait_ge(x_in[0][u], 16 * i + 16)
                        ins = nc.tensor.transpose(bank[tb][:, 128 * (u % 2):128 * (u % 2) + 128], xin[:, u, :], ident)
                    ins.then_inc(filled[tb], 1)
                for u in range(4):
                    hbk, tb = f"S{u}", f"T{u // 2}"
                    if u % 2 == 0:
                        pe.wait_ge(freed[tb], i + 1 + J(tb, "loop", 0))
                    pe.wait_ge(freed[hbk], i + J(hbk, "loop", 0))
                    pe.wait_ge(w_in[0][u], 16 * i + 16)
                    nc.tensor.matmul(bank[hbk][:, 0:128], w0[:, u, 0:128], xeT[:, u, :], start=True, stop=True)
                    nc.tensor.matmul(bank[hbk][:, 128:256], w0[:, u, 128:256], xeT[:, u, :], start=True, stop=True)\
                        .then_inc(filled[hbk], 1)
                for p in range(2):
                    yb = ("O", "M")[p]
                    pe.wait_ge(freed[yb], i + J(yb, "loop", 0))
                    pe.wait_ge(hs_ready, 2 * i + p + 1)
                    for u in (2 * p, 2 * p + 1):
                        ins = nc.tensor.matmul(bank[yb][:, 128 * (u % 2):128 * (u % 2) + 128], hs[:, u, :],
                                               w0[:, u, 256:384], start=True, stop=True)
                    ins.then_inc(filled[yb], 1)

            turn0(0, True)
            with pe.Fori(1, TILES[0] // UNROLL[0]) as i:
                turn0(i, False)

            for n in range(16):
                bk = f"S{n % 4}"
                b, half = n // 2, n % 2
                o = use(bk, J(bk, "v1", n))
                nc.tensor.matmul(o[0:M, :], ctx_sb[:, M * b:M * b + M], Wv_sb[:, 512 * half:512 * half + 512],
                                 start=True, stop=True).then_inc(filled[bk], 1)
            xT(0)
            q(0, 0)
            q(0, 1)
            scores(1, 0)
            attention(1)
            tables(1)

            def turn1(i):
                for u in range(2):
                    tb = f"T{u}"
                    pe.wait_ge(freed[tb], i + J(tb, "loop", 1))
                    pe.wait_ge(x_in[1][u], 16 * i + 16)
                    nc.tensor.transpose(bank[tb][:, 0:128], xin[:, u, :], ident).then_inc(filled[tb], 1)
                for u in range(2):
                    tb = f"T{u}"
                    pe.wait_ge(freed[tb], i + 1 + J(tb, "loop", 1))
                    pe.wait_ge(w_in[1][u], 16 * i + 16)
                    for half in range(2):
                        hbk = f"S{2 * u + half}"
                        pe.wait_ge(freed[hbk], i + J(hbk, "loop", 1))
                        for c in range(2):
                            cc = 2 * half + c
                            ins = nc.tensor.matmul(bank[hbk][:, 128 * c:128 * c + 128],
                                                   w1[:, u, 128 * cc:128 * cc + 128], xeT[:, u, :],
                                                   start=True, stop=True)
                        ins.then_inc(filled[hbk], 1)
                for u in range(2):
                    yb = ("O", "M")[u]
                    pe.wait_ge(freed[yb], i + J(yb, "loop", 1))
                    for half in range(2):
                        hbk = f"S{2 * u + half}"
                        pe.wait_ge(freed[hbk], i + 1 + J(hbk, "loop", 1))
                    for c in range(4):
                        ins = nc.tensor.matmul(bank[yb][:, 0:128], h1[u][:, c, :],
                                               w1[:, u, 512 + 128 * c:640 + 128 * c], start=(c == 0), stop=(c == 3))
                    ins.then_inc(filled[yb], 1)

            turn1(0)
            with pe.Fori(1, TILES[1] // UNROLL[1]) as i:
                turn1(i)


LD_A = 16 * 6
LD_B = 16 * 6
LD_C = 16 * 8


def kernel(x, ctx_768, L0_xattn_q_w, L0_xattn_q_b, L0_xattn_kv_w, L0_xattn_kv_b, L0_xattn_proj_w, L0_xattn_proj_b,
           L0_ffn_norm_scale, L0_ffn_wg, L0_ffn_bg, L0_ffn_w1, L0_ffn_b1, L0_ffn_w2, L0_ffn_b2,
           L1_xattn_Wq, L1_xattn_Wk, L1_xattn_Wv, L1_xattn_Wo, L1_xattn_bo,
           L1_ffn_Wr, L1_ffn_br, L1_ffn_W1, L1_ffn_b1, L1_ffn_W2, L1_ffn_b2):
    import concourse.bacc as bacc
    from concourse.bass_utils import run_bass_kernel_spmd

    def a(v):
        return np.asarray(v)

    w1, b1 = a(L0_ffn_w1), a(L0_ffn_b1)
    pack0 = np.concatenate([w1[:, :, 0::2], w1[:, :, 1::2], a(L0_ffn_w2), b1[:, 0::2, None], b1[:, 1::2, None]], axis=2)
    W2 = a(L1_ffn_W2).reshape(8, 4, 128, 128).transpose(0, 2, 1, 3).reshape(8, 128, 512)
    pack1 = np.concatenate([a(L1_ffn_W1), W2, a(L1_ffn_b1).reshape(8, 4, 128).transpose(0, 2, 1)], axis=2)
    arrays = {
        "x": a(x),
        "ctxT": a(ctx_768).reshape(B * M, DC).T,
        "cst": shape_constants(),
        "q_w": a(L0_xattn_q_w),
        "q_b": a(L0_xattn_q_b).reshape(128, 1),
        "kv_w": a(L0_xattn_kv_w),
        "kv_b": a(L0_xattn_kv_b).reshape(2, 128).T,
        "proj_w": a(L0_xattn_proj_w),
        "proj_b": a(L0_xattn_proj_b),
        "norm_s": a(L0_ffn_norm_scale),
        "wg": a(L0_ffn_wg),
        "bg": a(L0_ffn_bg),
        "wp0": pack0,
        "b2_0": a(L0_ffn_b2),
        "Wq": a(L1_xattn_Wq),
        "Wk": a(L1_xattn_Wk),
        "Wv": a(L1_xattn_Wv),
        "Wo": a(L1_xattn_Wo).reshape(8, 128, 128).transpose(1, 0, 2),
        "bo": a(L1_xattn_bo),
        "Wr": a(L1_ffn_Wr),
        "br": a(L1_ffn_br),
        "wp1": pack1,
        "b2_1": a(L1_ffn_b2),
    }
    arrays = {k: np.ascontiguousarray(v) for k, v in arrays.items()}
    nc = bacc.Bacc("TRN2", target_bir_lowering=False, num_devices=1)
    aps = {k: nc.dram_tensor(f"{k}_dram", v.shape, mybir.dt.from_np(v.dtype), kind="ExternalInput").ap()
           for k, v in arrays.items()}
    out = nc.dram_tensor("out_dram", (B, T, D), F32, kind="ExternalOutput").ap()
    build(nc, out=out, **aps)
    r = run_bass_kernel_spmd(nc, [{f"{k}_dram": v for k, v in arrays.items()}], core_ids=[0])
    return r.results[0]["out_dram"]
```

```python
from contextlib import ExitStack

import numpy as np

import concourse.bass as bass
from concourse import mybir

ALU = mybir.AluOpType
ACT = mybir.ActivationFunctionType
F32 = mybir.dt.float32
I32 = mybir.dt.int32
U32 = mybir.dt.uint32
AX_X = mybir.AxisListType.X

B = 8
T = 128
D = 128
M = 77
DC = 96
NH = 16
HD = (8, 64)
NG = 4
GH = NH // NG
GM = GH * M
E = (16, 8)
TOPK = (4, 1)
REGION = 8
UNIT = (2, 1)
CAND = tuple(REGION // u for u in UNIT)
UNITS = tuple(B * TOPK[n] // UNIT[n] + E[n] for n in range(2))
FF = (128, 512)
WCOL = (2 * 128 + 128 + 2, 512 + 512 + 4)
EPS = 1e-5
WARM = (12, 2, 2)
LIMIT = 7.0
ALPHA = 1.702
DEPTH = (8, 4)
RING = 4
TURNS = tuple(UNITS[n] // DEPTH[n] for n in range(2))
STORES = tuple(DEPTH[n] * TURNS[n] // RING for n in range(2))
LAG_H, LAG_HS, LAG_Y = (2, 1), 3, (4, 2)

C_ID = 0
C_LT = C_ID + 128
C_ONE = C_LT + 128
C_IOTA = C_ONE + 128
C_HEAD = C_IOTA + 48
C_RB = C_HEAD + 4
C_PL = C_RB + 16
C_PL_W = 3 + 16
C_NH = C_PL + 2 * C_PL_W
C_ALL = C_NH + 1


def shape_constants():
    c = np.zeros((128, C_ALL), np.float32)
    p = np.arange(128)
    c[:, C_ID:C_ID + 128] = np.eye(128)
    c[:, C_LT:C_LT + 128] = p[:, None] < p[None, :]
    c[:, C_ONE:C_ONE + 128] = 1
    c[:, C_IOTA:C_IOTA + 48] = np.arange(48)
    c[:, C_HEAD:C_HEAD + 4] = (p[:, None] % 32) // 8 == np.arange(4)[None, :]
    c[:, C_RB:C_RB + 16] = np.arange(16) * REGION * 128
    for layer in range(2):
        o = C_PL + layer * C_PL_W
        e, t = p // CAND[layer], p % CAND[layer]
        c[:, o] = 128 * UNIT[layer] * t
        c[:, o + 1] = REGION * e + UNIT[layer] * t - REGION * E[layer]
        c[:, o + 2] = e
        c[:, o + 3:o + 3 + E[layer]] = 128 * UNIT[layer] * (e[:, None] < np.arange(E[layer])[None, :])
    c[:, C_NH] = -0.5
    return c


BANK = ({"xnT": "M", "pv": "OOOO", "oT": "M", "logits": "M", "proj": "M", "rank": "M"},
        {"xT": "M", "q": "M", "xnT": "O", "pv": "OMMO", "oT": "O", "logits": "O", "proj": "M", "rank": "O"})


def plan_banks():
    job, count = {}, {}

    def use(bank, *what):
        count[bank] = count.get(bank, 0) + 1
        job[(bank, *what)] = count[bank]

    for n in range(2):
        use(f"T{n}", "k0", n)
    use("O", "v0", 0)
    use("M", "v0", 1)
    for n in range(2):
        use(f"S{n}", "xT0", n)
    for n in range(2):
        use(f"T{n}", "q0", n)

    def scores(layer, b):
        for g in range(NG):
            use(f"S{g}", "scores", layer, b, g)

    def attention(layer):
        where = BANK[layer]
        for b in range(B + 2):
            if b < B:
                use("T0", "pT", layer, b, 0)
            if layer and b + 1 < B:
                use(where["xT"], "xT", b + 1)
            if layer == 0 and 0 <= b - 2 < B:
                use(where["xnT"], "xnT", layer, b - 2)
            if b < B:
                use("T1", "pT", layer, b, 1)
            if layer and 0 <= b - 1 < B:
                use(where["oT"], "oT", layer, b - 1, 0)
            if layer and b + 1 < B:
                use(where["q"], "q", b + 1, 0)
            if b < B:
                use(where["pv"][0], "pv", layer, b, 0)
            if layer == 0 and 0 <= b - 1 < B:
                use(where["oT"], "oT", layer, b - 1, 0)
            if layer and b + 1 < B:
                use(where["q"], "q", b + 1, 1)
            if b < B:
                use("T0", "pT", layer, b, 2)
            if layer == 0 and 0 <= b - 2 < B:
                use(where["logits"], "logits", layer, b - 2)
            if layer and 0 <= b - 1 < B:
                use(where["oT"], "oT", layer, b - 1, 1)
            if layer and b < B:
                use(where["pv"][1], "pv", layer, b, 1)
            if layer == 0 and 0 <= b - 1 < B:
                use(where["proj"], "proj", layer, b - 1)
            if b < B:
                use("T1", "pT", layer, b, 3)
            if layer and 0 <= b - 2 < B:
                use(where["xnT"], "xnT", layer, b - 2)
                use(where["logits"], "logits", layer, b - 2)
            if layer and b < B:
                use(where["pv"][2], "pv", layer, b, 2)
                use(where["pv"][3], "pv", layer, b, 3)
            if layer and 0 <= b - 1 < B:
                use(where["proj"], "proj", layer, b - 1)
            if 0 <= b - 2 < B:
                use(where["rank"], "rank", layer, b - 2)
            if b + 1 < B:
                scores(layer, b + 1)

    def tables(layer):
        use("O", "count", layer)
        use("O", "pos", layer)
        use("O", "table", layer)
        use("M", "start", layer)

    def base(layer):
        for n in range(2):
            use(f"T{n}", "gT", layer, n)
        for n in range(2):
            use(f"T{n}", "b2", layer, n)

    def loop(layer):
        for bank, share in LOOP_SHARE.items():
            job[(bank, "loop", layer)] = count[bank]
            count[bank] += DEPTH[layer] // share * TURNS[layer]

    scores(0, 0)
    attention(0)
    for n in range(16):
        use(f"S{n % 4}", "k1", n)
    tables(0)
    loop(0)
    base(0)
    for n in range(16):
        use(f"S{n % 4}", "v1", n)
    use("M", "xT", 0)
    use("M", "q", 0, 0)
    use("M", "q", 0, 1)
    scores(1, 0)
    attention(1)
    tables(1)
    loop(1)
    base(1)
    return job


LOOP_SHARE = {"T0": 2, "T1": 2, "S0": 4, "S1": 4, "S2": 4, "S3": 4, "O": 2, "M": 2}


def build(nc, x, ctxT, cst, q_w, q_b, kv_w, kv_b, proj_w, proj_b, norm_s, wg, bg, wp0, b2_0,
          Wq, Wk, Wv, Wo, bo, Wr, br, wp1, b2_1, out):
    job = plan_banks()
    rows = (REGION * E[0] + 2) * 128
    xs_dram = nc.dram_tensor("dispatched", [rows, D], F32, kind="Internal").ap()
    ys_dram = [nc.dram_tensor(f"expert_out{n}", [UNITS[n] * UNIT[n] * 128, D], F32, kind="Internal").ap() for n in range(2)]

    with ExitStack() as ctx:
        def sb(name, shape, dt=F32):
            return ctx.enter_context(nc.sbuf_tensor(name, shape, dt))

        def sem(name):
            return ctx.enter_context(nc.semaphore(name))

        bank = {n: ctx.enter_context(nc.psum_tensor(f"bank_{n}", [128, 512], F32))
                for n in ("S0", "S1", "S2", "S3", "T0", "T1", "O", "M")}
        filled = {n: sem(f"filled_{n}") for n in bank}
        freed = {n: sem(f"freed_{n}") for n in bank}

        C = sb("C", [128, C_ALL])
        ident = C[:, C_ID:C_ID + 128]
        before = C[:, C_LT:C_LT + 128]
        ones = C[:, C_ONE:C_ONE + 128]
        X = sb("X", [128, B, D])
        XB = sb("XB", [128, B, D])
        XR = sb("XR", [128, B, D])
        XF = sb("XF", [128, B, D])
        XN = sb("XN", [128, B, D])
        X2 = sb("X2", [128, B, D])
        XA = sb("XA", [128, B, D])
        ctx_sb = sb("ctx_sb", [DC, B * M])
        qw_sb = sb("qw_sb", [128, 128])
        qb_sb = sb("qb_sb", [128, 1])
        kvw_sb = sb("kvw_sb", [DC, 256])
        kvb_sb = sb("kvb_sb", [128, 2])
        pw_sb = sb("pw_sb", [128, 128])
        pb_sb = sb("pb_sb", [128, 128])
        ns_sb = sb("ns_sb", [128, 128])
        wg_sb = sb("wg_sb", [128, 16])
        bg_sb = sb("bg_sb", [128, 16])
        b20_sb = sb("b20_sb", [16, 128])
        Wq_sb = sb("Wq_sb", [128, 1024])
        Wk_sb = sb("Wk_sb", [DC, 1024])
        Wv_sb = sb("Wv_sb", [DC, 1024])
        Wo_sb = sb("Wo_sb", [128, 8, 128])
        bo_sb = sb("bo_sb", [128, 128])
        Wr_sb = sb("Wr_sb", [128, 8])
        br_sb = sb("br_sb", [128, 8])
        b21_sb = sb("b21_sb", [8, 128])
        wr_l, br_l, b2_l = (wg_sb, Wr_sb), (bg_sb, br_sb), (b20_sb, b21_sb)

        keys1 = sb("keys1", [128, 8 * 2 * B * M])
        K1 = keys1[:].rearrange("p (c k m) -> p c k m", c=8, k=2)
        a0, a1, a2 = GH * B * M, GH * B * M + B * T, GH * B * M + B * T + B * NH * (HD[0] + 1)
        assert a2 <= 4 * 2 * B * M
        KX0 = keys1[:, 0:a0].rearrange("p (j c) -> p j c", j=GH)
        QT0 = keys1[:, a0:a1]
        V0 = keys1[0:M, a1:a2].rearrange("p (b h d) -> p b h d", b=B, h=NH)
        shared = sb("shared", [128, max([B * NH * (HD[1] + 1), NH * B * M] + [DEPTH[n] * WCOL[n] for n in range(2)])])
        V1 = shared[0:M, 0:B * NH * (HD[1] + 1)].rearrange("p (b h d) -> p b h d", b=B, h=NH)
        KF0 = shared[:, 0:NH * B * M].rearrange("p (h c) -> p h c", h=NH)
        w0 = shared[:, 0:DEPTH[0] * WCOL[0]].rearrange("p (u c) -> p u c", c=WCOL[0])
        w1 = shared[:, 0:DEPTH[1] * WCOL[1]].rearrange("p (u c) -> p u c", c=WCOL[1])
        XT1 = sb("XT1", [128, 128])
        QT1 = sb("QT1", [128, 2, 8, 128])
        XT0 = QT1[:, 0, :, :].rearrange("p c t -> p (c t)")
        scratch = sb("scratch", [128, 2 * NG * GM])
        P = scratch[:].rearrange("p (s g c) -> p s g c", s=2, g=NG)
        PT = sb("PT", [M, NG, GH * 128])
        negmax = sb("negmax", [128, NG, GH])
        recip = sb("recip", [128, NG, NH])
        OS = sb("OS", [128, 2, NH * 64])
        OT = sb("OT", [128, 8, 128])
        XNT = sb("XNT", [128, 128])
        zeros = sb("zeros", [128, 128])
        warm = sb("warm", [128, 512], mybir.dt.bfloat16)

        st6 = sb("st6", [128, B, 6])
        mv = sb("mv", [128, B, 2])
        var_eps = sb("var_eps", [128, B])
        rstd = sb("rstd", [128, B])
        rms = sb("rms", [128, B])
        rrms = sb("rrms", [128, B])

        lg = sb("lg", [128, 16])
        top8 = sb("top8", [128, 8])
        idx8 = sb("idx8", [128, 8], U32)
        vdif = sb("vdif", [128, B, 8])
        vexp = sb("vexp", [128, B, 8])
        vsum = sb("vsum", [128, B])
        vrec = sb("vrec", [128, B])
        gates = sb("gates", [128, B, 4])
        hot = sb("hot", [128, B, 4, 16])
        mask = sb("mask", [128, B, 16])
        mcum = sb("mcum", [128, B, 16])
        posm = sb("posm", [128, 16])
        prod = sb("prod", [128, 4, 16])
        slot_f = sb("slot_f", [128, B, 4])
        slot_u = sb("slot_u", [128, B, 4], U32)
        gfp = sb("gfp", [128, B, 4, 16])
        gf = sb("gf", [128, B, 16])
        mexp = sb("mexp", [128, 64])
        act_c = sb("act_c", [128, 1])
        act_bc = sb("act_bc", [128, 128])
        pos_c = sb("pos_c", [128, 1])
        ohj = sb("ohj", [128, 48])
        table = sb("table", [1, 96], I32)
        region_shift = sb("region_shift", [128, 16])
        red = sb("red", [128, B, 4])
        yslot = sb("yslot", [128, B, 4], U32)
        gfT = sb("gfT", [16, B * 128])
        G = sb("G", [128, 2, 4, 128])

        xin = sb("xin", [128, 8, 128])
        xeT = sb("xeT", [128, 8, 128])
        ha, hb, th, hu = (scratch[:, 512 * n:512 * n + 512].rearrange("p (u t) -> p u t", u=4) for n in range(4))
        hs = sb("hs", [128, 8, 128])
        h1 = (ha, hb)
        yo = sb("yo", [128, 8, 128])

        ld_x = [sem(f"ld_x{n}") for n in range(2)]
        ld_a = sem("ld_a")
        ld_b = sem("ld_b")
        ld_c = sem("ld_c")
        dve_step = sem("dve_step")
        pool_step = sem("pool_step")
        ones_v = sem("ones_v")
        zero_set = sem("zero_set")
        warm_ready = sem("warm_ready")
        keys_zeroed = sem("keys_zeroed")
        keys1_zeroed = sem("keys1_zeroed")
        keys_spread = [sem(f"keys_spread{n}") for n in range(2)]
        zeroed = [sem(f"zeroed{n}") for n in range(REGION + 1)]
        xb_ready = sem("xb_ready")
        ln_stats = sem("ln_stats")
        ln_rstd = sem("ln_rstd")
        xa_ready = sem("xa_ready")
        exp_done = sem("exp_done")
        rt_stats = sem("rt_stats")
        rt_rstd = sem("rt_rstd")
        xn_ready = sem("xn_ready")
        vdif_ready = sem("vdif_ready")
        vexp_ready = sem("vexp_ready")
        mask_ready = sem("mask_ready")
        slot_ready = sem("slot_ready")
        scattered = [sem(f"scattered{n}") for n in range(2)]
        gf_ready = sem("gf_ready")
        mexp_ready = sem("mexp_ready")
        act_ready = sem("act_ready")
        ohj_ready = sem("ohj_ready")
        yslot_ready = sem("yslot_ready")
        base_ready = sem("base_ready")
        gathered = [sem(f"gathered{n}") for n in range(2)]
        gathered_1 = [sem(f"gathered_1_{b}") for b in range(B)]
        combined = sem("combined")
        x_in = [[sem(f"x_in{n}_{q}") for q in range(RING)] for n in range(2)]
        w_in = [[sem(f"w_in{n}_{q}") for q in range(DEPTH[n])] for n in range(2)]
        bias_up = sem("bias_up")
        th_ready = sem("th_ready")
        hs_ready = sem("hs_ready")
        y_out = [[sem(f"y_out{n}_{half}") for half in range(2)] for n in range(2)]
        ha_ready = sem("ha_ready")
        hu_ready = sem("hu_ready")
        out_done = sem("out_done")

        def J(b, *what):
            return job[(b, *what)]

        def pvjob(layer, b, g):
            bk = BANK[layer]["pv"][g]
            return bk, J(bk, "pv", layer, b, g if layer else 0)

        def tbank(q):
            return f"T{q % 2}"

        def hbank(q):
            return f"S{q % 4}"

        def ybank(q):
            return ("O", "M")[q % 2]

        def unit_use(bk, layer, i, d, q):
            per = DEPTH[layer] // LOOP_SHARE[bk]
            return i * per + (J(bk, "loop", layer) + per * d + q // LOOP_SHARE[bk] + 1)

        def unit_count(layer, i, d, q, ring=1):
            return i * (DEPTH[layer] // ring) + (DEPTH[layer] * d + q) // ring + 1

        def expert_loop(engine, step, layer, deepest):
            for p in range(DEPTH[layer]):
                step(0, p, True, False)
            with engine.Fori(1, TURNS[layer]) as i:
                for p in range(DEPTH[layer]):
                    step(i, p, False, False)
            for p in range(deepest):
                step(TURNS[layer], p, False, True)

        def at(layer, p, lag, first, last):
            d, q = (p - lag) // DEPTH[layer], (p - lag) % DEPTH[layer]
            if first and d < 0 or last and d >= 0:
                return None
            return d, q

        def load_tokens(engine, layer, i, p, first):
            unit = UNIT[layer]
            row = engine.value_load(table[0:1, bass.ds(i * DEPTH[layer] + p, 1)], min_val=0, max_val=REGION * E[layer])
            row = engine.snap(row * 128)
            before_it = at(layer, p, RING, first, False)
            if before_it:
                engine.wait_ge(filled[tbank(p)], unit_use(tbank(p), layer, i, *before_it))
            r = p % RING
            engine.dma_start(xin[:, unit * r:unit * r + unit, :],
                             xs_dram[bass.ds(row, 128 * unit), :].rearrange("(u p) d -> p u d", p=128))\
                .then_inc(x_in[layer][r], 16)

        def load_weights(engine, layer, i, d, q, first):
            wp, wbuf = ((wp0, w0), (wp1, w1))[layer]
            ex = engine.value_load(table[0:1, bass.ds(i * DEPTH[layer] + (DEPTH[layer] * d + q + UNITS[layer]), 1)],
                                   min_val=0, max_val=E[layer] - 1)
            if not first:
                engine.wait_ge(filled[ybank(q)], unit_use(ybank(q), layer, i, d - 1, q))
            engine.dma_start(wbuf[:, q, :], wp[bass.ds(ex, 1), :, :].rearrange("e p n -> p (e n)"))\
                .then_inc(w_in[layer][q], 16)

        block = ctx.enter_context(nc.Block())

        @block.sync
        def _(sp):
            xv = x.rearrange("b t d -> t b d")
            sp.dma_start(X[:, 0:4, :], xv[:, 0:4, :]).then_inc(ld_x[0], 16)
            sp.dma_start(X[:, 4:8, :], xv[:, 4:8, :]).then_inc(ld_x[1], 16)
            sp.dma_start(qw_sb[:], q_w).then_inc(ld_a, 16)
            sp.dma_start(qb_sb[:], q_b).then_inc(ld_a, 16)
            sp.dma_start(pb_sb[:], proj_b.partition_broadcast(128)).then_inc(ld_b, 16)
            sp.dma_start(pw_sb[:], proj_w).then_inc(ld_b, 16)
            sp.dma_start(ns_sb[:], norm_s.partition_broadcast(128)).then_inc(ld_b, 16)
            sp.dma_start(wg_sb[:], wg).then_inc(ld_b, 16)
            sp.dma_start(bg_sb[:], bg.partition_broadcast(128)).then_inc(ld_b, 16)
            sp.dma_start(b20_sb[:], b2_0).then_inc(ld_b, 16)
            sp.wait_ge(keys_zeroed, 2)
            for n in range(2):
                sp.wait_ge(freed[f"T{n}"], J(f"T{n}", "k0", n))
                cols = slice(4 * M * n, 4 * M * (n + 1))
                for g in range(NG):
                    sp.dma_start(KF0[32 * g:32 * g + 32, GH * g:GH * g + GH, cols],
                                 KX0[32 * g:32 * g + 32, :, cols]).then_inc(keys_spread[n], 16)
            sp.wait_ge(zero_set, 1)
            xz = xs_dram[0:REGION * E[0] * 128, :].rearrange("(e r p) d -> r p e d", r=REGION, p=128)
            for r in range(REGION):
                sp.dma_start(xz[r], zeros[:, None, :].to_broadcast([128, E[0], D])).then_inc(zeroed[r], 16)
            sp.dma_start(xs_dram[REGION * E[0] * 128:rows, :].rearrange("(u p) d -> p u d", p=128),
                         zeros[:, None, :].to_broadcast([128, 2, D])).then_inc(zeroed[REGION], 16)
            sp.dma_start(Wk_sb[:], Wk).then_inc(ld_c, 16)
            sp.dma_start(Wv_sb[:], Wv).then_inc(ld_c, 16)
            sp.dma_start(Wq_sb[:], Wq).then_inc(ld_c, 16)
            sp.dma_start(Wo_sb[:], Wo).then_inc(ld_c, 16)
            sp.dma_start(bo_sb[:], bo.partition_broadcast(128)).then_inc(ld_c, 16)
            sp.dma_start(Wr_sb[:], Wr).then_inc(ld_c, 16)
            sp.dma_start(br_sb[:], br.partition_broadcast(128)).then_inc(ld_c, 16)
            sp.dma_start(b21_sb[:], b2_1).then_inc(ld_c, 16)

            for layer in range(2):
                sp.wait_ge(freed["O"], J("O", "table", layer))

                def step(i, p, first, last):
                    if p % RING == 0 and not last:
                        if first and p == 0:
                            sp.wait_ge(scattered[layer], 16 * B * TOPK[layer])
                            sp.wait_ge(zeroed[REGION], 16)
                        load_tokens(sp, layer, i, p, first)
                    where = at(layer, p, 1, first, last)
                    if where:
                        load_weights(sp, layer, i, *where, first)

                expert_loop(sp, step, layer, 1)
            for n in range(2):
                for half in range(2):
                    sp.wait_ge(y_out[n][half], 16 * STORES[n])
            sp.wait_ge(out_done, 16 * B)

        @block.gpsimd
        def _(pool):
            steps = [0]

            def link(ins):
                steps[0] += 1
                ins.then_inc(pool_step, 1)
                pool.wait_ge(pool_step, steps[0])

            nc.gpsimd.memset(zeros[:], 0.0).then_inc(zero_set, 1)
            nc.gpsimd.memset(V0[:], 1.0).then_inc(ones_v, 1)
            nc.gpsimd.memset(KF0[:, 0:8, :], 0.0).then_inc(keys_zeroed, 1)

            def rsqrt_eps(dst, tmp, src, n):
                link(nc.gpsimd.tensor_scalar(tmp, src, EPS, None, ALU.add))
                return nc.gpsimd.tensor_tensor(dst, tmp, C[:, C_NH:C_NH + 1].to_broadcast([128, n]) if n > 1 else C[:, C_NH:C_NH + 1], ALU.pow)

            pool.wait_ge(ld_a, LD_A)
            pool.wait_ge(ln_stats, 1)
            rsqrt_eps(rstd[:], var_eps[:], mv[:, :, 1], B).then_inc(ln_rstd, 1)
            pool.wait_ge(ld_b, LD_B)
            for b in range(B):
                nc.gpsimd.tensor_tensor(XB[:, b, :], X[:, b, :], pb_sb[:], ALU.add).then_inc(xb_ready, 1)

            nc.gpsimd.memset(K1[:, 4:8, :, :], 0.0).then_inc(keys1_zeroed, 1)

            def route_rstd(layer, b):
                pool.wait_ge(rt_stats, layer * B + b + 1)
                if layer == 0:
                    link(rsqrt_eps(rstd[:, b:b + 1], var_eps[:, b:b + 1], mv[:, b, 1:2], 1))
                    link(nc.gpsimd.tensor_scalar(rms[:, b:b + 1], mv[:, b, 1:2], rstd[:, b:b + 1], rstd[:, b:b + 1],
                                                 ALU.mult, ALU.mult))
                    rsqrt_eps(rrms[:, b:b + 1], var_eps[:, b:b + 1], rms[:, b:b + 1], 1).then_inc(rt_rstd, 1)
                else:
                    rsqrt_eps(rstd[:, b:b + 1], var_eps[:, b:b + 1], mv[:, b, 1:2], 1).then_inc(rt_rstd, 1)

            def scatter(layer, b):
                pool.wait_ge(slot_ready, layer * B + b + 1)
                if layer == 0:
                    pool.wait_ge(zeroed[b], 16)
                for k in range(TOPK[layer]):
                    nc.gpsimd.indirect_dma_start(
                        out=xs_dram, out_offset=bass.IndirectOffsetOnAxis(ap=slot_u[:, b, k:k + 1], axis=0),
                        in_=XN[:, b, :], in_offset=None).then_inc(scattered[layer], 16)

            def gather(layer, b):
                if b >= 2 and layer == 0:
                    pool.wait_ge(combined, b - 1)
                for k in range(TOPK[layer]):
                    nc.gpsimd.indirect_dma_start(
                        out=G[:, b % 2, k, :] if layer == 0 else G[:, b // 4, b % 4, :],
                        out_offset=None, in_=ys_dram[layer],
                        in_offset=bass.IndirectOffsetOnAxis(ap=yslot[:, b, k:k + 1], axis=0))\
                        .then_inc(gathered[b % 2] if layer == 0 else gathered_1[b], 16)

            def ln_pow(b):
                pool.wait_ge(ln_stats, b + 2)
                rsqrt_eps(rstd[:, b:b + 1], var_eps[:, b:b + 1], mv[:, b, 1:2], 1).then_inc(ln_rstd, 1)

            for b in range(B + 2):
                if 0 <= b - 1 < B:
                    route_rstd(0, b - 1)
                if 0 <= b - 2 < B:
                    scatter(0, b - 2)

            def expert_steps(layer):
                def step(i, p, first, last):
                    where = at(layer, p, 2, first, last)
                    if layer == 0 and where:
                        d, q = where
                        pool.wait_ge(w_in[0][q], 16 * i + 16 * (d + 1))
                        nc.gpsimd.tensor_tensor(w0[:, q, 385:386], w0[:, q, 385:386], ones[:, 0:1], ALU.add)\
                            .then_inc(bias_up, 1)
                    if not last and p % RING > 0:
                        load_tokens(pool, layer, i, p, first)

                return step

            pool.wait_ge(freed["O"], J("O", "table", 0))
            pool.wait_ge(scattered[0], 16 * B * TOPK[0])
            pool.wait_ge(zeroed[REGION], 16)
            expert_loop(pool, expert_steps(0), 0, 2)

            pool.wait_ge(yslot_ready, 1)
            for half in range(2):
                pool.wait_ge(y_out[0][half], 16 * STORES[0])
            nc.gpsimd.memset(V1[:, :, :, HD[1]:HD[1] + 1], 1.0).then_inc(ones_v, 1)
            gather(0, 0)
            gather(0, 1)
            ln_pow(0)
            gather(0, 2)
            ln_pow(1)
            for b in range(B + 2):
                if b + 3 < B:
                    gather(0, b + 3)
                if b + 2 < B:
                    ln_pow(b + 2)
                if 0 <= b - 1 < B:
                    route_rstd(1, b - 1)
                if 0 <= b - 2 < B:
                    scatter(1, b - 2)
            pool.wait_ge(freed["O"], J("O", "table", 1))
            pool.wait_ge(scattered[1], 16 * B * TOPK[1])
            expert_loop(pool, expert_steps(1), 1, 0)
            pool.wait_ge(yslot_ready, 2)
            for half in range(2):
                pool.wait_ge(y_out[1][half], 16 * STORES[1])
            pool.wait_ge(combined, B)
            for b in range(B):
                gather(1, b)

        @block.scalar
        def _(act):
            act.dma_start(C[:], cst).then_inc(ld_a, 16)
            act.dma_start(ctx_sb[:], ctxT).then_inc(ld_a, 16)
            act.dma_start(kvw_sb[:], kv_w).then_inc(ld_a, 16)
            act.dma_start(kvb_sb[:], kv_b).then_inc(ld_a, 16)

            def copy_out(bk, n, dst, src, func=ACT.Copy, **kw):
                act.wait_ge(filled[bk], n)
                nc.scalar.activation(dst, src, func, **kw).then_inc(freed[bk], 1)

            act.wait_ge(ld_a, LD_A)
            act.wait_ge(ones_v, 1)
            for n in range(2):
                bk = ("O", "M")[n]
                copy_out(bk, J(bk, "v0", n), V0[:, 4 * n:4 * n + 4, :, 0:8],
                         bank[bk][0:M, :].rearrange("p (b h d) -> p b h d", b=4, h=NH))
            copy_out("S0", J("S0", "xT0", 0), XT0[:, 0:512], bank["S0"][:])
            copy_out("T0", J("T0", "q0", 0), QT0[:, 0:512], bank["T0"][:], ACT.Identity, bias=qb_sb[:, 0:1])

            def exps(layer, b, g):
                act.wait_ge(freed[f"S{g}"], J(f"S{g}", "scores", layer, b, g))
                pg = P[:, b % 2, g, :]
                nc.scalar.activation(pg, pg, ACT.Exp, scale=float(HD[layer]) ** -0.5).then_inc(exp_done, 1)

            def pT_out(layer, b, g):
                if b > 0:
                    bk, n = pvjob(layer, b - 1, g)
                    act.wait_ge(filled[bk], n)
                elif layer:
                    bk, n = pvjob(0, B - 1, g)
                    act.wait_ge(filled[bk], n)
                bk = f"T{g % 2}"
                copy_out(bk, J(bk, "pT", layer, b, g), PT[:, g, :], bank[bk][0:M, :])

            def xT_out(b):
                if b > 0:
                    act.wait_ge(filled["M"], J("M", "q", b - 1, 1))
                copy_out("M", J("M", "xT", b), XT1[:], bank["M"][:, 0:128])

            def q_out(b, n):
                if b >= 2:
                    act.wait_ge(filled["S3"], J("S3", "scores", 1, b - 2, 3))
                copy_out("M", J("M", "q", b, n), QT1[:, b % 2, 4 * n:4 * n + 4, :],
                         bank["M"][:, :].rearrange("p (c t) -> p c t", c=4))

            def oT_out(layer, b, n):
                bk, done = BANK[layer]["oT"], BANK[layer]["proj"]
                if b > 0:
                    act.wait_ge(filled[done], J(done, "proj", layer, b - 1))
                elif layer:
                    act.wait_ge(filled["M"], J("M", "proj", 0, B - 1))
                if layer:
                    copy_out(bk, J(bk, "oT", layer, b, n), OT[:, 4 * n:4 * n + 4, :],
                             bank[bk][:].rearrange("p (c t) -> p c t", c=4))
                else:
                    copy_out(bk, J(bk, "oT", layer, b, n), OT[:, 0, :], bank[bk][:, 0:128],
                             ACT.Identity, bias=kvb_sb[:, 1:2])

            def xnT_out(layer, b):
                bk, done = BANK[layer]["xnT"], BANK[layer]["logits"]
                if b > 0:
                    act.wait_ge(filled[done], J(done, "logits", layer, b - 1))
                elif layer:
                    act.wait_ge(filled["M"], J("M", "logits", 0, B - 1))
                copy_out(bk, J(bk, "xnT", layer, b), XNT[:], bank[bk][:, 0:128])

            def gate_exps(layer, b):
                act.wait_ge(vdif_ready, layer * B + b + 1)
                w = (4, 8)[layer]
                nc.scalar.activation(vexp[:, b, 0:w], vdif[:, b, 0:w], ACT.Exp,
                                     accum_out=vsum[:, b:b + 1]).then_inc(vexp_ready, 1)

            def k1_out(start, count):
                if start == 0:
                    act.wait_ge(keys1_zeroed, 1)
                for n in range(start, start + count):
                    bk = f"S{n % 4}"
                    c, half = n // 2, n % 2
                    act.wait_ge(filled[bk], J(bk, "k1", n))
                    for k in range(2):
                        r = slice(64 * k, 64 * k + 64)
                        ins = nc.scalar.activation(K1[r, c, k, 308 * half:308 * half + 308], bank[bk][r, 0:308],
                                                   ACT.Copy)
                    ins.then_inc(freed[bk], 1)

            def attention_0():
                for g in range(NG):
                    exps(0, 0, g)
                for b in range(B + 2):
                    now, following, last, routed = b < B, b + 1 < B, 0 <= b - 1 < B, 0 <= b - 2 < B
                    if now:
                        pT_out(0, b, 0)
                    if b == B + 1:
                        k1_out(5, 3)
                    if routed:
                        xnT_out(0, b - 2)
                    if not now:
                        k1_out(0 if b == B else 8, 1)
                    if now:
                        pT_out(0, b, 1)
                    if following:
                        exps(0, b + 1, 0)
                    if last:
                        oT_out(0, b - 1, 0)
                    if b == B:
                        k1_out(1, 1)
                    if now:
                        pT_out(0, b, 2)
                    if following:
                        exps(0, b + 1, 1)
                    if routed:
                        gate_exps(0, b - 2)
                    if not now:
                        k1_out(2 if b == B else 9, 3 if b == B else 2)
                    if now:
                        pT_out(0, b, 3)
                    if following:
                        exps(0, b + 1, 2)
                        exps(0, b + 1, 3)

            def attention_1():
                for g in range(NG):
                    exps(1, 0, g)
                for b in range(B + 2):
                    now, following, last, routed = b < B, b + 1 < B, 0 <= b - 1 < B, 0 <= b - 2 < B
                    if now:
                        pT_out(1, b, 0)
                    if following:
                        xT_out(b + 1)
                    if now:
                        pT_out(1, b, 1)
                    if last:
                        oT_out(1, b - 1, 0)
                    if following:
                        q_out(b + 1, 0)
                        q_out(b + 1, 1)
                    if now:
                        pT_out(1, b, 2)
                    if last:
                        oT_out(1, b - 1, 1)
                    if following:
                        exps(1, b + 1, 0)
                    if now:
                        pT_out(1, b, 3)
                    if following:
                        exps(1, b + 1, 1)
                    if routed:
                        xnT_out(1, b - 2)
                        gate_exps(1, b - 2)
                    if following:
                        exps(1, b + 1, 2)
                        exps(1, b + 1, 3)

            def gT_out(layer):
                for n in range(2):
                    bk = f"T{n}"
                    copy_out(bk, J(bk, "gT", layer, n), gfT[0:E[layer], 512 * n:512 * n + 512],
                             bank[bk][0:E[layer], :])

            attention_0()
            k1_out(11, 5)
            for k in range(2):
                r = slice(64 * (1 - k), 64 * (1 - k) + 64)
                ins = nc.scalar.activation(K1[r, 0:4, k, :], C[r, None, C_IOTA:C_IOTA + 1].to_broadcast([64, 4, B * M]),
                                           ACT.Copy)
            ins.then_inc(keys1_zeroed, 1)

            def expert_steps(layer):
                unit = UNIT[layer]
                w = 128 * unit

                def step(i, p, first, last):
                    if not last:
                        before_it = at(layer, p, RING, first, False)
                        if before_it:
                            hbk = hbank(before_it[1])
                            act.wait_ge(filled[hbk], unit_use(hbk, layer, i, *before_it))
                        tb = tbank(p)
                        act.wait_ge(filled[tb], unit_use(tb, layer, i, 0, p))
                        x0 = unit * (p % RING)
                        nc.scalar.activation(xeT[:, x0:x0 + unit, :],
                                             bank[tb][:, 0:w].rearrange("p (u t) -> p u t", u=unit), ACT.Copy)\
                            .then_inc(freed[tb], 1)
                    where = at(layer, p, LAG_H[layer], first, last)
                    if layer == 0 and where:
                        d, q = where
                        s2 = slice(2 * (q % 2), 2 * (q % 2) + 2)
                        act.wait_ge(ha_ready, unit_count(0, i, d, q))
                        nc.scalar.activation(th[:, s2, :], ha[:, s2, :], ACT.Tanh, scale=ALPHA / 2)\
                            .then_inc(th_ready, 1)
                    where = at(layer, p, LAG_Y[layer], first, last)
                    if where:
                        d, q = where
                        yb, r = ybank(q), q % RING
                        half = r // 2
                        if layer == 0 and q % 2 == 0 and (not first or q >= RING):
                            act.wait_ge(y_out[0][half], 16 * unit_count(0, i, d, q, RING) - 16)
                        act.wait_ge(filled[yb], unit_use(yb, layer, i, d, q))
                        nc.scalar.activation(yo[:, unit * r:unit * r + unit, :],
                                             bank[yb][:, 0:w].rearrange("p (u t) -> p u t", u=unit),
                                             ACT.Copy, scale=(0.5, 1.0)[layer]).then_inc(freed[yb], 1)
                        if q % 2 == 1:
                            for written in (q - 1, q):
                                act.wait_ge(freed[ybank(written)], unit_use(ybank(written), layer, i, d, written))
                            act.dma_start(
                                ys_dram[layer][bass.ds(i * (DEPTH[layer] * w) + (DEPTH[layer] * d + q - 1) * w, 2 * w), :]
                                .rearrange("(u p) d -> p u d", p=128),
                                yo[:, 2 * half * unit:2 * (half + 1) * unit, :]).then_inc(y_out[layer][half], 16)
                            if layer == 1 and not (last and q + 1 >= DEPTH[layer]) and not (first and q + 1 < RING):
                                act.wait_ge(y_out[layer][1 - half], 16 * unit_count(layer, i, d, q + 1, RING) - 16)

                return step

            expert_loop(act, expert_steps(0), 0, LAG_Y[0])
            gT_out(0)

            for n in range(16):
                bk = f"S{n % 4}"
                b, half = n // 2, n % 2
                copy_out(bk, J(bk, "v1", n), V1[:, b, 8 * half:8 * half + 8, 0:64],
                         bank[bk][0:M, :].rearrange("p (h d) -> p h d", h=8))
            xT_out(0)
            q_out(0, 0)
            q_out(0, 1)
            attention_1()

            expert_loop(act, expert_steps(1), 1, LAG_Y[1])
            gT_out(1)

            for b in range(B):
                act.wait_ge(combined, B + b + 1)
                act.dma_start(out[b], X[:, b, :]).then_inc(out_done, 16)

        @block.vector
        def _(dve):
            steps = [0]

            def link(ins):
                steps[0] += 1
                ins.then_inc(dve_step, 1)
                dve.wait_ge(dve_step, steps[0])

            def stats(src, b):
                link(nc.vector.bn_stats(st6[:, b, :], src))
                return nc.vector.bn_aggr(mv[:, b, :], st6[:, b, :])

            nc.vector.memset(warm[:], 0.0).then_inc(warm_ready, 1)
            nc.vector.memset(KF0[:, 8:16, :], 0.0).then_inc(keys_zeroed, 1)
            for b in range(B):
                dve.wait_ge(ld_x[b // 4], 16)
                ins = stats(X[:, b, :], b)
            ins.then_inc(ln_stats, 1)

            def keys_out(n):
                bk = f"T{n}"
                dve.wait_ge(filled[bk], J(bk, "k0", n))
                for j in range(GH):
                    ins = nc.vector.tensor_scalar(KX0[:, j, 308 * n:308 * n + 308], bank[bk][:, 0:308],
                                                  kvb_sb[:, 0:1], C[:, C_HEAD + j:C_HEAD + j + 1], ALU.add, ALU.mult)
                ins.then_inc(freed[bk], 1)

            dve.wait_ge(ld_a, LD_A)
            keys_out(0)
            dve.wait_ge(ln_rstd, 1)
            for b in range(B):
                nc.vector.tensor_scalar(XA[:, b, :], X[:, b, :], mv[:, b, 0:1], rstd[:, b:b + 1],
                                        ALU.subtract, ALU.mult).then_inc(xa_ready, 1)
            dve.wait_ge(filled["S1"], J("S1", "xT0", 1))
            nc.vector.tensor_copy(XT0[:, 512:1024], bank["S1"][:]).then_inc(freed["S1"], 1)
            keys_out(1)

            def shift(layer, b, g):
                bk = f"S{g}"
                sc = bank[bk][:, 0:GM].rearrange("p (h m) -> p h m", h=GH)
                dve.wait_ge(filled[bk], J(bk, "scores", layer, b, g))
                link(nc.vector.tensor_reduce(negmax[:, g, :], sc, AX_X, ALU.max, negate=True))
                tb = f"T{g % 2}"
                if b >= 2:
                    dve.wait_ge(filled[tb], J(tb, "pT", layer, b - 2, g))
                elif layer:
                    dve.wait_ge(filled[tb], J(tb, "pT", 0, B - 2 + b, g))
                nc.vector.tensor_tensor(P[:, b % 2, g, :].rearrange("p (h m) -> p h m", h=GH), sc,
                                        negmax[:, g, :, None].to_broadcast([128, GH, M]), ALU.add)\
                    .then_inc(freed[bk], 1)

            def pv_out(layer, b, g):
                bk, n = pvjob(layer, b, g)
                d = HD[layer]
                heads = GH if layer else NH
                o = bank[bk][:, 0:heads * (d + 1)].rearrange("p (h e) -> p h e", h=heads)
                dve.wait_ge(filled[bk], n)
                link(nc.vector.reciprocal(recip[:, g, 0:heads], o[:, :, d]))
                if b > 1:
                    ob = BANK[layer]["oT"]
                    dve.wait_ge(filled[ob], J(ob, "oT", layer, b - 2, layer))
                elif layer:
                    dve.wait_ge(filled["M"], J("M", "oT", 0, B - 2 + b, 0))
                if layer:
                    dst = OS[:, b % 2, 256 * g:256 * g + 256].rearrange("p (h d) -> p h d", d=64)
                else:
                    dst = OS[:, b % 2, 0:128].rearrange("p (h d) -> p h d", d=8)
                nc.vector.tensor_tensor(dst, o[:, :, 0:d], recip[:, g, 0:heads, None].to_broadcast([128, heads, d]),
                                        ALU.mult).then_inc(freed[bk], 1)

            def proj_out(layer, b):
                bk = BANK[layer]["proj"]
                dve.wait_ge(filled[bk], J(bk, "proj", layer, b))
                if layer == 0:
                    dve.wait_ge(xb_ready, b + 1)
                base = XB[:, b, :]
                ins = nc.vector.tensor_tensor(XR[:, b, :], bank[bk][:, 0:128], base, ALU.add)
                ins.then_inc(freed[bk], 1)
                dve.wait_ge(freed[bk], J(bk, "proj", layer, b))
                stats(XR[:, b, :], b).then_inc(rt_stats, 1)

            def normed(layer, b):
                dve.wait_ge(rt_rstd, layer * B + b + 1)
                if layer == 0:
                    link(nc.vector.tensor_scalar(XF[:, b, :], XR[:, b, :], mv[:, b, 0:1], rstd[:, b:b + 1],
                                                 ALU.subtract, ALU.mult))
                    nc.vector.scalar_tensor_tensor(XN[:, b, :], XF[:, b, :], rrms[:, b:b + 1], ns_sb[:],
                                                   ALU.mult, ALU.mult).then_inc(xn_ready, 1)
                else:
                    nc.vector.tensor_scalar(XN[:, b, :], XR[:, b, :], mv[:, b, 0:1], rstd[:, b:b + 1],
                                            ALU.subtract, ALU.mult).then_inc(xn_ready, 1)

            def choose(layer, b):
                e, k = E[layer], TOPK[layer]
                bk = BANK[layer]["logits"]
                dve.wait_ge(filled[bk], J(bk, "logits", layer, b))
                nc.vector.tensor_tensor(lg[:, 0:e], bank[bk][:, 0:e], br_l[layer][:, 0:e], ALU.add)\
                    .then_inc(freed[bk], 1)
                dve.wait_ge(freed[bk], J(bk, "logits", layer, b))
                link(nc.vector.max(top8[:], lg[:, 0:e]))
                link(nc.vector.max_index(idx8[:], top8[:], lg[:, 0:e]))
                src = top8[:, 0:4] if layer == 0 else lg[:, 0:8]
                nc.vector.tensor_scalar(vdif[:, b, 0:(4, 8)[layer]], src, top8[:, 0:1], None, ALU.subtract)\
                    .then_inc(vdif_ready, 1)
                link(nc.vector.tensor_tensor(hot[:, b, 0:k, 0:e],
                                             C[:, None, C_IOTA:C_IOTA + e].to_broadcast([128, k, e]),
                                             idx8[:, 0:k, None].to_broadcast([128, k, e]), ALU.is_equal))
                if k > 1:
                    link(nc.vector.tensor_reduce(mask[:, b, 0:e],
                                                 hot[:, b, 0:k, 0:e].rearrange("p k e -> p e k"), AX_X, ALU.add))
                else:
                    link(nc.vector.tensor_copy(mask[:, b, 0:e], hot[:, b, 0, 0:e]))
                if b == 0:
                    nc.vector.tensor_copy(mcum[:, b, 0:e], mask[:, b, 0:e]).then_inc(mask_ready, 1)
                else:
                    nc.vector.tensor_tensor(mcum[:, b, 0:e], mcum[:, b - 1, 0:e], mask[:, b, 0:e], ALU.add)\
                        .then_inc(mask_ready, 1)

            def place(layer, b):
                e, k = E[layer], TOPK[layer]
                bk = BANK[layer]["rank"]
                n = J(bk, "rank", layer, b)
                dve.wait_ge(filled[bk], n)
                nc.vector.tensor_tensor(posm[:, 0:e], bank[bk][:, 0:e], C[:, C_RB:C_RB + e], ALU.add)\
                    .then_inc(freed[bk], 1)
                dve.wait_ge(freed[bk], n)
                link(nc.vector.tensor_tensor(prod[:, 0:k, 0:e], hot[:, b, 0:k, 0:e],
                                             posm[:, None, 0:e].to_broadcast([128, k, e]), ALU.mult))
                link(nc.vector.tensor_reduce(slot_f[:, b, 0:k], prod[:, 0:k, 0:e], AX_X, ALU.add))
                nc.vector.tensor_copy(slot_u[:, b, 0:k], slot_f[:, b, 0:k]).then_inc(slot_ready, 1)

            def combine(layer, b):
                k = TOPK[layer]
                dst = (X2, X)[layer]
                rows = G[:, b % 2, :, :] if layer == 0 else G[:, b // 4, b % 4:b % 4 + 1, :]
                if layer == 0:
                    dve.wait_ge(gathered[b % 2], 16 * k * (b // 2 + 1))
                else:
                    dve.wait_ge(gathered_1[b], 16)
                for j in range(k):
                    ins = nc.vector.scalar_tensor_tensor(dst[:, b, :], rows[:, j, :], gates[:, b, j:j + 1],
                                                         XR[:, b, :] if j == 0 else dst[:, b, :], ALU.mult, ALU.add)
                    if j < k - 1:
                        link(ins)
                ins.then_inc(combined, 1)
                if layer == 0:
                    dve.wait_ge(combined, b + 1)
                    nc.vector.tensor_tensor(XB[:, b, :], X2[:, b, :], bo_sb[:], ALU.add)
                    stats(X2[:, b, :], b).then_inc(ln_stats, 1)

            def attn_norm(b):
                dve.wait_ge(ln_rstd, 1 + b + 1)
                nc.vector.tensor_scalar(XA[:, b, :], X2[:, b, :], mv[:, b, 0:1], rstd[:, b:b + 1],
                                        ALU.subtract, ALU.mult).then_inc(xa_ready, 1)

            def attention_0():
                shift(0, 0, 0)
                shift(0, 0, 1)
                dve.wait_ge(filled["T1"], J("T1", "q0", 1))
                nc.vector.tensor_scalar(QT0[:, 512:1024], bank["T1"][:], qb_sb[:, 0:1], None, ALU.add)\
                    .then_inc(freed["T1"], 1)
                shift(0, 0, 2)
                shift(0, 0, 3)
                for b in range(B + 2):
                    following, last, routed = b + 1 < B, 0 <= b - 1 < B, 0 <= b - 2 < B
                    if last:
                        pv_out(0, b - 1, 0)
                    if following:
                        shift(0, b + 1, 0)
                        shift(0, b + 1, 1)
                    if routed:
                        choose(0, b - 2)
                    if last:
                        proj_out(0, b - 1)
                    if following:
                        shift(0, b + 1, 2)
                    if routed:
                        place(0, b - 2)
                    if following:
                        shift(0, b + 1, 3)
                    if last:
                        normed(0, b - 1)

            def attention_1():
                for g in range(NG):
                    shift(1, 0, g)
                for b in range(B + 2):
                    now, following, last, routed = b < B, b + 1 < B, 0 <= b - 1 < B, 0 <= b - 2 < B
                    if b + 2 < B:
                        combine(0, b + 2)
                    if now:
                        pv_out(1, b, 0)
                    if following:
                        shift(1, b + 1, 0)
                        shift(1, b + 1, 1)
                    if now:
                        pv_out(1, b, 1)
                    if following:
                        shift(1, b + 1, 2)
                    if now:
                        pv_out(1, b, 2)
                    if routed:
                        choose(1, b - 2)
                    if following:
                        shift(1, b + 1, 3)
                    if now:
                        pv_out(1, b, 3)
                    if b + 2 < B:
                        attn_norm(b + 2)
                    if last:
                        proj_out(1, b - 1)
                    if routed:
                        place(1, b - 2)
                    if last:
                        normed(1, b - 1)

            def tables(layer):
                e, k = E[layer], TOPK[layer]
                cand = CAND[layer]
                nc_ = e * cand
                o = C_PL + layer * C_PL_W
                nt = UNITS[layer]
                nc.vector.tensor_copy(mexp[:].rearrange("p (e t) -> p e t", t=cand),
                                      mcum[:, B - 1, 0:e, None].to_broadcast([128, e, cand]))\
                    .then_inc(mexp_ready, 1)
                dve.wait_ge(vexp_ready, layer * B + B)
                link(nc.vector.reciprocal(vrec[:], vsum[:]))
                if k > 1:
                    link(nc.vector.tensor_tensor(gates[:, :, 0:k], vexp[:, :, 0:k],
                                                 vrec[:, :, None].to_broadcast([128, B, k]), ALU.mult))
                else:
                    link(nc.vector.tensor_copy(gates[:, :, 0], vrec[:]))
                dve.wait_ge(filled["O"], J("O", "count", layer))
                nc.vector.tensor_tensor(act_c[0:nc_, :], bank["O"][0:nc_, 0:1], C[0:nc_, o:o + 1], ALU.is_gt)\
                    .then_inc(freed["O"], 1)
                dve.wait_ge(freed["O"], J("O", "count", layer))
                nc.vector.tensor_scalar(act_bc[0:nc_, :], C[0:nc_, C_ONE:C_ONE + 128], act_c[0:nc_, :], None, ALU.mult)\
                    .then_inc(act_ready, 1)
                dve.wait_ge(filled["O"], J("O", "pos", layer))
                nc.vector.tensor_copy(pos_c[0:nc_, :], bank["O"][0:nc_, 0:1]).then_inc(freed["O"], 1)
                dve.wait_ge(freed["O"], J("O", "pos", layer))
                nc.vector.tensor_scalar(ohj[0:nc_, 0:nt], C[0:nc_, C_IOTA:C_IOTA + nt], pos_c[0:nc_, :],
                                        act_c[0:nc_, :], ALU.is_equal, ALU.mult).then_inc(ohj_ready, 1)
                dve.wait_ge(filled["O"], J("O", "table", layer))
                nc.vector.tensor_scalar(table[0:1, 0:nt], bank["O"][0:1, 0:nt], float(REGION * e), None, ALU.add)
                ins = nc.vector.tensor_copy(table[0:1, nt:2 * nt], bank["O"][0:1, nt:2 * nt])
                ins.then_inc(freed["O"], 1)
                dve.wait_ge(freed["O"], J("O", "table", layer))
                dve.wait_ge(filled["M"], J("M", "start", layer))
                nc.vector.tensor_tensor(region_shift[:, 0:e], bank["M"][:, 0:e], C[:, C_RB:C_RB + e], ALU.subtract)\
                    .then_inc(freed["M"], 1)
                dve.wait_ge(freed["M"], J("M", "start", layer))
                for b in range(B):
                    ins = nc.vector.tensor_tensor(gfp[:, b, 0:k, 0:e], hot[:, b, 0:k, 0:e],
                                                  region_shift[:, None, 0:e].to_broadcast([128, k, e]), ALU.mult)
                link(ins)
                for b in range(B):
                    ins = nc.vector.tensor_reduce(red[:, b, 0:k], gfp[:, b, 0:k, 0:e], AX_X, ALU.add)
                link(ins)
                nc.vector.tensor_tensor(yslot[:, :, 0:k], red[:, :, 0:k], slot_f[:, :, 0:k], ALU.add)\
                    .then_inc(yslot_ready, 1)
                for b in range(B):
                    ins = nc.vector.tensor_tensor(gfp[:, b, 0:k, 0:e], hot[:, b, 0:k, 0:e],
                                                  gates[:, b, 0:k, None].to_broadcast([128, k, e]), ALU.mult)
                link(ins)
                for b in range(B):
                    ins = nc.vector.tensor_reduce(gf[:, b, 0:e], gfp[:, b, 0:k, 0:e].rearrange("p k e -> p e k"),
                                                  AX_X, ALU.add)
                ins.then_inc(gf_ready, 1)

            def base(layer):
                for n in range(2):
                    bk = f"T{n}"
                    dve.wait_ge(filled[bk], J(bk, "b2", layer, n))
                    xr = XR[:, 4 * n:4 * n + 4, :]
                    nc.vector.tensor_tensor(xr, bank[bk][:].rearrange("p (b d) -> p b d", b=4), xr, ALU.add)\
                        .then_inc(freed[bk], 1)
                dve.wait_ge(freed["T1"], J("T1", "b2", layer, 1))

            attention_0()
            tables(0)
            link(nc.vector.tensor_tensor(XR[:], XR[:], XF[:], ALU.add))

            def expert_steps(layer):
                def step(i, p, first, last):
                    hidden, scaled = at(layer, p, LAG_H[layer], first, last), at(layer, p, LAG_HS, first, last)
                    if layer == 1:
                        if hidden:
                            d, q = hidden
                            hbk = hbank(q)
                            dve.wait_ge(filled[hbk], unit_use(hbk, 1, i, d, q))
                            for c in range(4):
                                ins = nc.vector.tensor_scalar(h1[q % 2][:, c, :], bank[hbk][:, 128 * c:128 * c + 128],
                                                              w1[:, q, 1024 + c:1025 + c], 0.0, ALU.add, ALU.max)
                            ins.then_inc(freed[hbk], 1)
                        return
                    if scaled:
                        d, q = scaled
                        number = unit_count(0, i, d, q)
                        m2, r = slice(2 * (q % 2), 2 * (q % 2) + 2), q % RING
                        dve.wait_ge(th_ready, number)
                        nc.vector.scalar_tensor_tensor(hu[:, m2, :], th[:, m2, :], 1.0, ha[:, m2, :],
                                                       ALU.add, ALU.mult).then_inc(hu_ready, 1)
                    if hidden:
                        dh, qh = hidden
                        hbk = hbank(qh)
                        s2 = slice(2 * (qh % 2), 2 * (qh % 2) + 2)
                        h = bank[hbk][:, :].rearrange("p (half u t) -> p half u t", half=2, u=2)
                        dve.wait_ge(filled[hbk], unit_use(hbk, 0, i, dh, qh))
                        nc.vector.tensor_scalar(ha[:, s2, :], h[:, 0, :, :], w0[:, qh, 384:385], LIMIT,
                                                ALU.add, ALU.min).then_inc(ha_ready, 1)
                    if scaled:
                        dve.wait_ge(hu_ready, number)
                        nc.vector.scalar_tensor_tensor(hs[:, 2 * r:2 * r + 2, :], hb[:, m2, :], 1.0 - LIMIT,
                                                       hu[:, m2, :], ALU.max, ALU.mult).then_inc(hs_ready, 1)
                    if hidden:
                        dve.wait_ge(bias_up, unit_count(0, i, dh, qh))
                        if not first or p > LAG_HS:
                            dve.wait_ge(hs_ready, unit_count(0, i, dh, qh) - 2)
                        nc.vector.tensor_scalar(hb[:, s2, :], h[:, 1, :, :], w0[:, qh, 385:386], LIMIT + 1.0,
                                                ALU.add, ALU.min).then_inc(freed[hbk], 1)

                return step

            expert_loop(dve, expert_steps(0), 0, LAG_HS)
            base(0)

            dve.wait_ge(ld_c, LD_C)
            combine(0, 0)
            combine(0, 1)
            attn_norm(0)
            attn_norm(1)
            attention_1()
            tables(1)

            expert_loop(dve, expert_steps(1), 1, LAG_H[1])
            base(1)
            for b in range(B):
                combine(1, b)

        @block.tensor
        def _(pe):
            def use(bk, n):
                if n > 1:
                    pe.wait_ge(freed[bk], n - 1)
                return bank[bk]

            def keep_clock(o, n=1):
                for _ in range(n):
                    nc.tensor.matmul(o[:], warm[:, 0:128], warm[:], start=True, stop=True)

            pe.wait_ge(warm_ready, 1)
            keep_clock(bank["T0"], WARM[0])
            pe.wait_ge(ld_a, LD_A)
            for n in range(2):
                bk = f"T{n}"
                o = use(bk, J(bk, "k0", n))
                nc.tensor.matmul(o[:, 0:308], kvw_sb[:, 0:128], ctx_sb[:, 308 * n:308 * n + 308],
                                 start=True, stop=True).then_inc(filled[bk], 1)
            for n in range(2):
                bk = ("O", "M")[n]
                o = use(bk, J(bk, "v0", n))
                for c in range(4):
                    b = 4 * n + c
                    ins = nc.tensor.matmul(o[0:M, 128 * c:128 * c + 128], ctx_sb[:, M * b:M * b + M],
                                           kvw_sb[:, 128:256], start=True, stop=True)
                ins.then_inc(filled[bk], 1)
            for n in range(2):
                bk = f"S{n}"
                o = use(bk, J(bk, "xT0", n))
                keep_clock(o, WARM[1])
                for c in range(4):
                    pe.wait_ge(xa_ready, 4 * n + c + 1)
                    ins = nc.tensor.transpose(o[:, 128 * c:128 * c + 128], XA[:, 4 * n + c, :], ident)
                ins.then_inc(filled[bk], 1)
            def q0(n):
                bk = f"T{n}"
                o = use(bk, J(bk, "q0", n))
                keep_clock(o, WARM[2])
                pe.wait_ge(freed[f"S{n}"], J(f"S{n}", "xT0", n))
                nc.tensor.matmul(o[:], qw_sb[:], XT0[:, 512 * n:512 * n + 512], start=True, stop=True)\
                    .then_inc(filled[bk], 1)

            q0(0)

            def scores(layer, b, groups=range(NG)):
                if layer == 0 and b % 4 == 0 and groups[0] == 0:
                    pe.wait_ge(freed[f"T{b // 4}"], J(f"T{b // 4}", "q0", b // 4))
                    pe.wait_ge(keys_spread[b // 4], 16 * NG)
                if layer == 1:
                    pe.wait_ge(freed["M"], J("M", "q", b, groups[-1] // 2))
                    if b == 0:
                        pe.wait_ge(keys1_zeroed, 2)
                        for n in range(4):
                            pe.wait_ge(freed[f"S{n}"], J(f"S{n}", "k1", 12 + n))
                for g in groups:
                    o = use(f"S{g}", J(f"S{g}", "scores", layer, b, g))
                    if layer == 0:
                        ins = nc.tensor.matmul(o[:, 0:GM], QT0[:, T * b:T * b + T],
                                               KF0[:, GH * g:GH * g + GH, M * b:M * b + M], start=True, stop=True)
                    else:
                        for c in (2 * g, 2 * g + 1):
                            ins = nc.tensor.matmul(o[:, 2 * M * (c % 2):2 * M * (c % 2 + 1)], QT1[:, b % 2, c, :],
                                                   K1[:, c, :, M * b:M * b + M], start=True, stop=True)
                    ins.then_inc(filled[f"S{g}"], 1)

            def probsT(layer, b, g):
                bk = f"T{g % 2}"
                o = use(bk, J(bk, "pT", layer, b, g))
                pe.wait_ge(exp_done, NG * (B * layer + b) + g + 1)
                for j in range(GH):
                    ins = nc.tensor.transpose(o[0:M, 128 * j:128 * j + 128], P[:, b % 2, g, M * j:M * j + M], ident)
                ins.then_inc(filled[bk], 1)

            def pv(layer, b, g):
                bk, n = pvjob(layer, b, g)
                if layer or g == 0:
                    use(bk, n)
                if layer == 0 and b == 0 and g == 0:
                    for m in range(2):
                        pe.wait_ge(freed[("O", "M")[m]], J(("O", "M")[m], "v0", m))
                if layer == 1 and b == 0 and g == 0:
                    pe.wait_ge(ones_v, 2)
                    for m in range(4):
                        pe.wait_ge(freed[f"S{m}"], J(f"S{m}", "v1", 12 + m))
                tb = f"T{g % 2}"
                pe.wait_ge(freed[tb], J(tb, "pT", layer, b, g))
                d = HD[layer] + 1
                for j in range(GH):
                    h = GH * g + j
                    c = j if layer else h
                    v = (V0, V1)[layer]
                    ins = nc.tensor.matmul(bank[bk][:, d * c:d * c + d], PT[:, g, 128 * j:128 * j + 128],
                                           v[:, b, h, :], start=True, stop=True)
                if layer or g == NG - 1:
                    ins.then_inc(filled[bk], 1)

            def outT(layer, b, n):
                bk = BANK[layer]["oT"]
                o = use(bk, J(bk, "oT", layer, b, n))
                for g in (range(2 * n, 2 * n + 2) if layer else (0,)):
                    pk, done = pvjob(layer, b, g)
                    pe.wait_ge(freed[pk], done)
                if layer:
                    for c in range(4):
                        cc = 4 * n + c
                        ins = nc.tensor.transpose(o[:, 128 * c:128 * c + 128], OS[:, b % 2, 128 * cc:128 * cc + 128],
                                                  ident)
                else:
                    ins = nc.tensor.transpose(o[:, 0:128], OS[:, b % 2, 0:128], ident)
                ins.then_inc(filled[bk], 1)

            def proj(layer, b):
                bk, tk = BANK[layer]["proj"], BANK[layer]["oT"]
                o = use(bk, J(bk, "proj", layer, b))
                pe.wait_ge(freed[tk], J(tk, "oT", layer, b, layer))
                if layer == 0:
                    if b == 0:
                        pe.wait_ge(ld_b, LD_B)
                    ins = nc.tensor.matmul(o[:, 0:128], OT[:, 0, :], pw_sb[:], start=True, stop=True)
                else:
                    for c in range(8):
                        ins = nc.tensor.matmul(o[:, 0:128], OT[:, c, :], Wo_sb[:, c, :], start=(c == 0), stop=(c == 7))
                ins.then_inc(filled[bk], 1)

            def xnT(layer, b):
                bk = BANK[layer]["xnT"]
                o = use(bk, J(bk, "xnT", layer, b))
                pe.wait_ge(xn_ready, layer * B + b + 1)
                nc.tensor.transpose(o[:, 0:128], XN[:, b, :], ident).then_inc(filled[bk], 1)

            def logits(layer, b):
                bk, tk = BANK[layer]["logits"], BANK[layer]["xnT"]
                o = use(bk, J(bk, "logits", layer, b))
                pe.wait_ge(freed[tk], J(tk, "xnT", layer, b))
                nc.tensor.matmul(o[:, 0:E[layer]], XNT[:], wr_l[layer][:], start=True, stop=True)\
                    .then_inc(filled[bk], 1)

            def rank(layer, b):
                bk = BANK[layer]["rank"]
                o = use(bk, J(bk, "rank", layer, b))
                e = E[layer]
                pe.wait_ge(mask_ready, layer * B + b + 1)
                ins = nc.tensor.matmul(o[:, 0:e], before, mask[:, b, 0:e], start=True, stop=(b == 0))
                if b > 0:
                    ins = nc.tensor.matmul(o[:, 0:e], ones, mcum[:, b - 1, 0:e], start=False, stop=True)
                ins.then_inc(filled[bk], 1)

            def xT(b):
                o = use("M", J("M", "xT", b))
                pe.wait_ge(xa_ready, B + b + 1)
                nc.tensor.transpose(o[:, 0:128], XA[:, b, :], ident).then_inc(filled["M"], 1)

            def q(b, n):
                o = use("M", J("M", "q", b, n))
                pe.wait_ge(freed["M"], J("M", "xT", b))
                for c in range(4):
                    cc = 4 * n + c
                    ins = nc.tensor.matmul(o[:, 128 * c:128 * c + 128], Wq_sb[:, 128 * cc:128 * cc + 128], XT1[:],
                                           start=True, stop=True)
                ins.then_inc(filled["M"], 1)

            def k1(start, count):
                pe.wait_ge(ld_c, LD_C)
                for n in range(start, start + count):
                    bk = f"S{n % 4}"
                    c, half = n // 2, n % 2
                    o = use(bk, J(bk, "k1", n))
                    nc.tensor.matmul(o[:, 0:308], Wk_sb[:, 128 * c:128 * c + 128],
                                     ctx_sb[:, 308 * half:308 * half + 308], start=True, stop=True)\
                        .then_inc(filled[bk], 1)

            def attention_0():
                for b in range(B + 2):
                    now, following, last = b < B, b + 1 < B, 0 <= b - 1 < B
                    routed = 0 <= b - 2 < B
                    if now:
                        probsT(0, b, 0)
                    if following:
                        scores(0, b + 1, (0,))
                    if b == B + 1:
                        k1(5, 3)
                    if routed:
                        xnT(0, b - 2)
                    if not now:
                        k1(0 if b == B else 8, 1)
                    if now:
                        probsT(0, b, 1)
                        pv(0, b, 0)
                    if last:
                        outT(0, b - 1, 0)
                    if b == B:
                        k1(1, 1)
                    if following:
                        scores(0, b + 1, (1,))
                    if now:
                        probsT(0, b, 2)
                    if routed:
                        logits(0, b - 2)
                    if not now:
                        k1(2 if b == B else 9, 1 if b == B else 2)
                    if now:
                        pv(0, b, 1)
                    if last:
                        proj(0, b - 1)
                    if b == B:
                        k1(3, 1)
                    if following:
                        scores(0, b + 1, (2,))
                    if now:
                        probsT(0, b, 3)
                        pv(0, b, 2)
                    if routed:
                        rank(0, b - 2)
                    if b == B:
                        k1(4, 1)
                    if following:
                        scores(0, b + 1, (3,))
                    if now:
                        pv(0, b, 3)

            def attention_1():
                for b in range(B + 2):
                    now, following, last, routed = b < B, b + 1 < B, 0 <= b - 1 < B, 0 <= b - 2 < B
                    if now:
                        probsT(1, b, 0)
                    if following:
                        xT(b + 1)
                    if now:
                        probsT(1, b, 1)
                    if last:
                        outT(1, b - 1, 0)
                    if following:
                        q(b + 1, 0)
                    if now:
                        pv(1, b, 0)
                    if following:
                        scores(1, b + 1, (0, 1))
                        q(b + 1, 1)
                    if now:
                        probsT(1, b, 2)
                    if last:
                        outT(1, b - 1, 1)
                    if now:
                        pv(1, b, 1)
                        probsT(1, b, 3)
                    if routed:
                        xnT(1, b - 2)
                    if following:
                        scores(1, b + 1, (2,))
                    if now:
                        pv(1, b, 2)
                    if routed:
                        logits(1, b - 2)
                    if following:
                        scores(1, b + 1, (3,))
                    if now:
                        pv(1, b, 3)
                    if last:
                        proj(1, b - 1)
                    if routed:
                        rank(1, b - 2)

            def tables(layer):
                e = E[layer]
                n = e * CAND[layer]
                o = C_PL + layer * C_PL_W
                nt = UNITS[layer]
                ps = use("O", J("O", "count", layer))
                pe.wait_ge(mexp_ready, layer + 1)
                nc.tensor.matmul(ps[0:n, 0:1], mexp[:], ones[:, 0:1],
                                 start=True, stop=True).then_inc(filled["O"], 1)
                use("O", J("O", "pos", layer))
                if layer == 0:
                    k1(11, 1)
                pe.wait_ge(act_ready, layer + 1)
                nc.tensor.matmul(ps[0:n, 0:1], C[0:n, C_LT:C_LT + n], act_c[0:n, :], start=True, stop=True)\
                    .then_inc(filled["O"], 1)
                use("O", J("O", "table", layer))
                if layer == 0:
                    k1(12, 1)
                pe.wait_ge(ohj_ready, layer + 1)
                nc.tensor.matmul(ps[0:1, 0:nt], C[0:n, o + 1:o + 2], ohj[0:n, 0:nt], start=True, stop=True)
                nc.tensor.matmul(ps[0:1, nt:2 * nt], C[0:n, o + 2:o + 3], ohj[0:n, 0:nt], start=True, stop=True)\
                    .then_inc(filled["O"], 1)
                ps = use("M", J("M", "start", layer))
                nc.tensor.matmul(ps[:, 0:e], act_bc[0:n, :], C[0:n, o + 3:o + 3 + e], start=True, stop=True)\
                    .then_inc(filled["M"], 1)

            def base(layer):
                e = E[layer]
                for m in range(2):
                    ps = use(f"T{m}", J(f"T{m}", "gT", layer, m))
                    pe.wait_ge(gf_ready, layer + 1)
                    for c in range(4):
                        ins = nc.tensor.transpose(ps[0:e, 128 * c:128 * c + 128], gf[:, 4 * m + c, 0:e], ident)
                    ins.then_inc(filled[f"T{m}"], 1)
                for m in range(2):
                    ps = use(f"T{m}", J(f"T{m}", "b2", layer, m))
                    for c in range(4):
                        b = 4 * m + c
                        ins = nc.tensor.matmul(ps[:, 128 * c:128 * c + 128], gfT[0:e, 128 * b:128 * b + 128],
                                               b2_l[layer][:], start=True, stop=True)
                    ins.then_inc(filled[f"T{m}"], 1)

            scores(0, 0)
            q0(1)
            attention_0()
            tables(0)
            k1(13, 3)

            def expert_steps(layer):
                unit = UNIT[layer]

                def step(i, p, first, last):
                    if not last:
                        tb = tbank(p)
                        pe.wait_ge(freed[tb], unit_use(tb, layer, i, 0, p) - 1)
                        r = p % RING
                        pe.wait_ge(x_in[layer][r], 16 * unit_count(layer, i, 0, p, RING))
                        for u in range(unit):
                            ins = nc.tensor.transpose(bank[tb][:, 128 * u:128 * u + 128], xin[:, unit * r + u, :], ident)
                        ins.then_inc(filled[tb], 1)
                    where = at(layer, p, LAG_H[layer], first, last)
                    if where:
                        d, q = where
                        tb, hbk = tbank(q), hbank(q)
                        pe.wait_ge(freed[tb], unit_use(tb, layer, i, d, q))
                        pe.wait_ge(freed[hbk], unit_use(hbk, layer, i, d, q) - 1)
                        pe.wait_ge(w_in[layer][q], 16 * i + 16 * (d + 1))
                        wbuf = (w0, w1)[layer]
                        u0 = unit * (q % RING)
                        for c in range(4 // unit):
                            ins = nc.tensor.matmul(bank[hbk][:, 128 * unit * c:128 * unit * (c + 1)],
                                                   wbuf[:, q, 128 * c:128 * c + 128], xeT[:, u0:u0 + unit, :],
                                                   start=True, stop=True)
                        ins.then_inc(filled[hbk], 1)
                    where = at(layer, p, LAG_Y[layer], first, last)
                    if where:
                        d, q = where
                        yb = ybank(q)
                        pe.wait_ge(freed[yb], unit_use(yb, layer, i, d, q) - 1)
                        if layer == 0:
                            pe.wait_ge(hs_ready, unit_count(0, i, d, q))
                            for u in range(2):
                                ins = nc.tensor.matmul(bank[yb][:, 128 * u:128 * u + 128], hs[:, 2 * (q % RING) + u, :],
                                                       w0[:, q, 256:384], start=True, stop=True)
                        else:
                            pe.wait_ge(freed[hbank(q)], unit_use(hbank(q), 1, i, d, q))
                            for c in range(4):
                                ins = nc.tensor.matmul(bank[yb][:, 0:128], h1[q % 2][:, c, :],
                                                       w1[:, q, 512 + 128 * c:640 + 128 * c],
                                                       start=(c == 0), stop=(c == 3))
                        ins.then_inc(filled[yb], 1)

                return step

            expert_loop(pe, expert_steps(0), 0, LAG_Y[0])
            base(0)

            for n in range(16):
                bk = f"S{n % 4}"
                b, half = n // 2, n % 2
                o = use(bk, J(bk, "v1", n))
                nc.tensor.matmul(o[0:M, :], ctx_sb[:, M * b:M * b + M], Wv_sb[:, 512 * half:512 * half + 512],
                                 start=True, stop=True).then_inc(filled[bk], 1)
            xT(0)
            q(0, 0)
            q(0, 1)
            scores(1, 0)
            attention_1()
            tables(1)

            expert_loop(pe, expert_steps(1), 1, LAG_Y[1])
            base(1)


LD_A = 16 * 6
LD_B = 16 * 6
LD_C = 16 * 8


def kernel(x, ctx_768, L0_xattn_q_w, L0_xattn_q_b, L0_xattn_kv_w, L0_xattn_kv_b, L0_xattn_proj_w, L0_xattn_proj_b,
           L0_ffn_norm_scale, L0_ffn_wg, L0_ffn_bg, L0_ffn_w1, L0_ffn_b1, L0_ffn_w2, L0_ffn_b2,
           L1_xattn_Wq, L1_xattn_Wk, L1_xattn_Wv, L1_xattn_Wo, L1_xattn_bo,
           L1_ffn_Wr, L1_ffn_br, L1_ffn_W1, L1_ffn_b1, L1_ffn_W2, L1_ffn_b2):
    import concourse.bacc as bacc
    from concourse.bass_utils import run_bass_kernel_spmd

    def a(v):
        return np.asarray(v)

    w1, b1 = a(L0_ffn_w1), a(L0_ffn_b1)
    pack0 = np.concatenate([w1[:, :, 0::2], w1[:, :, 1::2], a(L0_ffn_w2), b1[:, 0::2, None], b1[:, 1::2, None]], axis=2)
    W2 = a(L1_ffn_W2).reshape(8, 4, 128, 128).transpose(0, 2, 1, 3).reshape(8, 128, 512)
    pack1 = np.concatenate([a(L1_ffn_W1), W2, a(L1_ffn_b1).reshape(8, 4, 128).transpose(0, 2, 1)], axis=2)
    arrays = {
        "x": a(x),
        "ctxT": a(ctx_768).reshape(B * M, DC).T,
        "cst": shape_constants(),
        "q_w": a(L0_xattn_q_w),
        "q_b": a(L0_xattn_q_b).reshape(128, 1),
        "kv_w": a(L0_xattn_kv_w),
        "kv_b": a(L0_xattn_kv_b).reshape(2, 128).T,
        "proj_w": a(L0_xattn_proj_w),
        "proj_b": a(L0_xattn_proj_b),
        "norm_s": a(L0_ffn_norm_scale),
        "wg": a(L0_ffn_wg),
        "bg": a(L0_ffn_bg),
        "wp0": pack0,
        "b2_0": a(L0_ffn_b2),
        "Wq": a(L1_xattn_Wq),
        "Wk": a(L1_xattn_Wk),
        "Wv": a(L1_xattn_Wv),
        "Wo": a(L1_xattn_Wo).reshape(8, 128, 128).transpose(1, 0, 2),
        "bo": a(L1_xattn_bo),
        "Wr": a(L1_ffn_Wr),
        "br": a(L1_ffn_br),
        "wp1": pack1,
        "b2_1": a(L1_ffn_b2),
    }
    arrays = {k: np.ascontiguousarray(v) for k, v in arrays.items()}
    nc = bacc.Bacc("TRN2", target_bir_lowering=False, num_devices=1)
    aps = {k: nc.dram_tensor(f"{k}_dram", v.shape, mybir.dt.from_np(v.dtype), kind="ExternalInput").ap()
           for k, v in arrays.items()}
    out = nc.dram_tensor("out_dram", (B, T, D), F32, kind="ExternalOutput").ap()
    build(nc, out=out, **aps)
    r = run_bass_kernel_spmd(nc, [{f"{k}_dram": v for k, v in arrays.items()}], core_ids=[0])
    return r.results[0]["out_dram"]
```

```python
from contextlib import ExitStack

import numpy as np

import concourse.bass as bass
from concourse import mybir

ALU = mybir.AluOpType
ACT = mybir.ActivationFunctionType
F32 = mybir.dt.float32
I32 = mybir.dt.int32
U32 = mybir.dt.uint32
AX_X = mybir.AxisListType.X

B = 8
T = 128
D = 128
M = 77
DC = 96
NH = 16
HD = (8, 64)
NG = 4
GH = NH // NG
GM = GH * M
E = (16, 8)
TOPK = (4, 1)
REGION = 8
UNIT = (2, 1)
CAND = tuple(REGION // u for u in UNIT)
UNITS = tuple(B * TOPK[n] // UNIT[n] + E[n] for n in range(2))
FF = (128, 512)
WCOL = (2 * 128 + 128 + 2, 512 + 512 + 4)
EPS = 1e-5
WARM = (12, 2, 2)
LOOP_WARM = (4, 8)
LAST_WARM = (4, 0)
LIMIT = 7.0
ALPHA = 1.702
DEPTH = (8, 4)
RING = 4
TURNS = tuple(UNITS[n] // DEPTH[n] for n in range(2))
STORES = tuple(DEPTH[n] * TURNS[n] // RING for n in range(2))
LAG_H, LAG_HS, LAG_Y = (2, 1), 3, (4, 2)

C_ID = 0
C_LT = C_ID + 128
C_ONE = C_LT + 128
C_IOTA = C_ONE + 128
C_HEAD = C_IOTA + 48
C_RB = C_HEAD + 4
C_PL = C_RB + 16
C_PL_W = 3 + 16
C_NH = C_PL + 2 * C_PL_W
C_ALL = C_NH + 1


def shape_constants():
    c = np.zeros((128, C_ALL), np.float32)
    p = np.arange(128)
    c[:, C_ID:C_ID + 128] = np.eye(128)
    c[:, C_LT:C_LT + 128] = p[:, None] < p[None, :]
    c[:, C_ONE:C_ONE + 128] = 1
    c[:, C_IOTA:C_IOTA + 48] = np.arange(48)
    c[:, C_HEAD:C_HEAD + 4] = (p[:, None] % 32) // 8 == np.arange(4)[None, :]
    c[:, C_RB:C_RB + 16] = np.arange(16) * REGION * 128
    for layer in range(2):
        o = C_PL + layer * C_PL_W
        e, t = p // CAND[layer], p % CAND[layer]
        c[:, o] = 128 * UNIT[layer] * t
        c[:, o + 1] = REGION * e + UNIT[layer] * t - REGION * E[layer]
        c[:, o + 2] = e
        c[:, o + 3:o + 3 + E[layer]] = 128 * UNIT[layer] * (e[:, None] < np.arange(E[layer])[None, :])
    c[:, C_NH] = -0.5
    return c


BANK = ({"xnT": "M", "pv": "OOOO", "oT": "M", "logits": "M", "proj": "M", "rank": "M"},
        {"xT": "M", "q": "M", "xnT": "O", "pv": "OMMO", "oT": "O", "logits": "O", "proj": "M", "rank": "O"})


LAST = {("oT", 6, 1): "M", ("pv", 7, 0): "S0", ("pv", 7, 1): "S1", ("pv", 7, 2): "S2", ("pv", 7, 3): "S3",
        ("xnT", 5, 0): "T0", ("logits", 5, 0): "T1", ("rank", 5, 0): "T1", ("oT", 7, 0): "O", ("oT", 7, 1): "T0",
        ("xnT", 6, 0): "S0", ("logits", 6, 0): "S1", ("rank", 6, 0): "S2",
        ("xnT", 7, 0): "S3", ("logits", 7, 0): "S0", ("rank", 7, 0): "S1"}


def bank_of(what, layer, b, n=0):
    if layer and (what, b, n) in LAST:
        return LAST[what, b, n]
    return BANK[layer]["pv"][n] if what == "pv" else BANK[layer][what]


def plan_banks():
    job, count = {}, {}

    def use(bank, *what):
        count[bank] = count.get(bank, 0) + 1
        job[(bank, *what)] = count[bank]

    for n in range(2):
        use(f"T{n}", "k0", n)
    use("O", "v0", 0)
    use("M", "v0", 1)
    for n in range(2):
        use(f"S{n}", "xT0", n)
    for n in range(2):
        use(f"T{n}", "q0", n)

    def scores(layer, b):
        for g in range(NG):
            use(f"S{g}", "scores", layer, b, g)

    def product(what, layer, b, n=0):
        use(bank_of(what, layer, b, n), what, layer, b, n)

    def transposed(layer, b, g):
        use(f"T{g % 2}", "pT", layer, b, g)

    def attention_0():
        for b in range(B + 2):
            now, last, routed = b < B, 0 <= b - 1 < B, 0 <= b - 2 < B
            if now:
                transposed(0, b, 0)
            if routed:
                product("xnT", 0, b - 2)
            if now:
                transposed(0, b, 1)
                product("pv", 0, b)
            if last:
                product("oT", 0, b - 1)
            if now:
                transposed(0, b, 2)
            if routed:
                product("logits", 0, b - 2)
            if last:
                product("proj", 0, b - 1)
            if now:
                transposed(0, b, 3)
            if routed:
                product("rank", 0, b - 2)
            if b + 1 < B:
                scores(0, b + 1)

    def attention_1():
        for b in range(B - 1):
            last, routed = 0 <= b - 1, 0 <= b - 2
            transposed(1, b, 0)
            use("M", "xT", b + 1)
            transposed(1, b, 1)
            if last:
                product("oT", 1, b - 1, 0)
            use("M", "q", b + 1, 0)
            product("pv", 1, b, 0)
            use("M", "q", b + 1, 1)
            transposed(1, b, 2)
            if last:
                product("oT", 1, b - 1, 1)
            product("pv", 1, b, 1)
            transposed(1, b, 3)
            if routed:
                product("xnT", 1, b - 2)
                product("logits", 1, b - 2)
            product("pv", 1, b, 2)
            product("pv", 1, b, 3)
            if last:
                product("proj", 1, b - 1)
            if routed:
                product("rank", 1, b - 2)
            scores(1, b + 1)
        transposed(1, B - 1, 0)
        transposed(1, B - 1, 1)
        product("oT", 1, B - 2, 0)
        product("oT", 1, B - 2, 1)
        product("pv", 1, B - 1, 0)
        product("pv", 1, B - 1, 1)
        transposed(1, B - 1, 2)
        transposed(1, B - 1, 3)
        product("xnT", 1, B - 3)
        product("proj", 1, B - 2)
        product("oT", 1, B - 1, 0)
        product("pv", 1, B - 1, 2)
        product("pv", 1, B - 1, 3)
        product("logits", 1, B - 3)
        product("oT", 1, B - 1, 1)
        product("proj", 1, B - 1)
        product("rank", 1, B - 3)
        product("xnT", 1, B - 2)
        product("logits", 1, B - 2)
        product("xnT", 1, B - 1)
        product("logits", 1, B - 1)
        product("rank", 1, B - 2)
        product("rank", 1, B - 1)

    def tables(layer):
        use("O", "count", layer)
        use("O", "pos", layer)
        use("O", "table", layer)
        use("M", "start", layer)

    def base(layer):
        for n in range(2):
            use(f"T{n}", "gT", layer, n)
        for n in range(2):
            use(f"T{n}", "b2", layer, n)

    def loop(layer):
        for bank, share in LOOP_SHARE.items():
            job[(bank, "loop", layer)] = count[bank]
            count[bank] += DEPTH[layer] // share * TURNS[layer]

    scores(0, 0)
    attention_0()
    for n in range(16):
        use(f"S{n % 4}", "k1", n)
    tables(0)
    loop(0)
    base(0)
    for n in range(16):
        use(f"S{n % 4}", "v1", n)
    use("M", "xT", 0)
    use("M", "q", 0, 0)
    use("M", "q", 0, 1)
    scores(1, 0)
    attention_1()
    tables(1)
    loop(1)
    base(1)
    return job


EARLY = (2, 0)

LOOP_SHARE = {"T0": 2, "T1": 2, "S0": 4, "S1": 4, "S2": 4, "S3": 4, "O": 2, "M": 2}


def build(nc, x, ctxT, cst, q_w, q_b, kv_w, kv_b, proj_w, proj_b, norm_s, wg, bg, wp0, b2_0,
          Wq, Wk, Wv, Wo, bo, Wr, br, wp1, b2_1, out):
    job = plan_banks()
    rows = (REGION * E[0] + 2) * 128
    xs_dram = nc.dram_tensor("dispatched", [rows, D], F32, kind="Internal").ap()
    ys_dram = [nc.dram_tensor(f"expert_out{n}", [UNITS[n] * UNIT[n] * 128, D], F32, kind="Internal").ap() for n in range(2)]

    with ExitStack() as ctx:
        def sb(name, shape, dt=F32):
            return ctx.enter_context(nc.sbuf_tensor(name, shape, dt))

        def sem(name):
            return ctx.enter_context(nc.semaphore(name))

        bank = {n: ctx.enter_context(nc.psum_tensor(f"bank_{n}", [128, 512], F32))
                for n in ("S0", "S1", "S2", "S3", "T0", "T1", "O", "M")}
        filled = {n: sem(f"filled_{n}") for n in bank}
        freed = {n: sem(f"freed_{n}") for n in bank}

        C = sb("C", [128, C_ALL])
        ident = C[:, C_ID:C_ID + 128]
        before = C[:, C_LT:C_LT + 128]
        ones = C[:, C_ONE:C_ONE + 128]
        X = sb("X", [128, B, D])
        XB = sb("XB", [128, B, D])
        XR = sb("XR", [128, B, D])
        XF = sb("XF", [128, B, D])
        XN = sb("XN", [128, B, D])
        X2 = sb("X2", [128, B, D])
        XA = sb("XA", [128, B, D])
        ctx_sb = sb("ctx_sb", [DC, B * M])
        qw_sb = sb("qw_sb", [128, 128])
        qb_sb = sb("qb_sb", [128, 1])
        kvw_sb = sb("kvw_sb", [DC, 256])
        kvb_sb = sb("kvb_sb", [128, 2])
        pw_sb = sb("pw_sb", [128, 128])
        pb_sb = sb("pb_sb", [128, 128])
        ns_sb = sb("ns_sb", [128, 128])
        wg_sb = sb("wg_sb", [128, 16])
        bg_sb = sb("bg_sb", [128, 16])
        b20_sb = sb("b20_sb", [16, 128])
        Wq_sb = sb("Wq_sb", [128, 1024])
        Wk_sb = sb("Wk_sb", [DC, 1024])
        Wv_sb = sb("Wv_sb", [DC, 1024])
        Wo_sb = sb("Wo_sb", [128, 8, 128])
        bo_sb = sb("bo_sb", [128, 128])
        Wr_sb = sb("Wr_sb", [128, 8])
        br_sb = sb("br_sb", [128, 8])
        b21_sb = sb("b21_sb", [8, 128])
        wr_l, br_l, b2_l = (wg_sb, Wr_sb), (bg_sb, br_sb), (b20_sb, b21_sb)

        keys1 = sb("keys1", [128, 8 * 2 * B * M])
        K1 = keys1[:].rearrange("p (c k m) -> p c k m", c=8, k=2)
        a0, a1, a2 = GH * B * M, GH * B * M + B * T, GH * B * M + B * T + B * NH * (HD[0] + 1)
        assert a2 <= 4 * 2 * B * M
        KX0 = keys1[:, 0:a0].rearrange("p (j c) -> p j c", j=GH)
        QT0 = keys1[:, a0:a1]
        V0 = keys1[0:M, a1:a2].rearrange("p (b h d) -> p b h d", b=B, h=NH)
        shared = sb("shared", [128, max([B * NH * (HD[1] + 1), NH * B * M] + [DEPTH[n] * WCOL[n] for n in range(2)])])
        V1 = shared[0:M, 0:B * NH * (HD[1] + 1)].rearrange("p (b h d) -> p b h d", b=B, h=NH)
        KF0 = shared[:, 0:NH * B * M].rearrange("p (h c) -> p h c", h=NH)
        w0 = shared[:, 0:DEPTH[0] * WCOL[0]].rearrange("p (u c) -> p u c", c=WCOL[0])
        w1 = shared[:, 0:DEPTH[1] * WCOL[1]].rearrange("p (u c) -> p u c", c=WCOL[1])
        XT1 = sb("XT1", [128, 128])
        QT1 = sb("QT1", [128, 2, 8, 128])
        XT0 = QT1[:, 0, :, :].rearrange("p c t -> p (c t)")
        scratch = sb("scratch", [128, 2 * NG * GM])
        P = scratch[:].rearrange("p (s g c) -> p s g c", s=2, g=NG)
        PT = sb("PT", [M, NG, GH * 128])
        negmax = sb("negmax", [128, NG, GH])
        recip = sb("recip", [128, NG, NH])
        OS = sb("OS", [128, 2, NH * 64])
        OT = sb("OT", [128, 8, 128])
        XNT = sb("XNT", [128, 128])
        zeros = sb("zeros", [128, 128])
        warm = sb("warm", [128, 512], mybir.dt.bfloat16)

        st6 = sb("st6", [128, B, 6])
        mv = sb("mv", [128, B, 2])
        var_eps = sb("var_eps", [128, B])
        rstd = sb("rstd", [128, B])
        rms = sb("rms", [128, B])
        rrms = sb("rrms", [128, B])

        lg = sb("lg", [128, 16])
        top8 = sb("top8", [128, 8])
        idx8 = sb("idx8", [128, 8], U32)
        vdif = sb("vdif", [128, B, 8])
        vexp = sb("vexp", [128, B, 8])
        vsum = sb("vsum", [128, B])
        vrec = sb("vrec", [128, B])
        gates = sb("gates", [128, B, 4])
        hot = sb("hot", [128, B, 4, 16])
        mask = sb("mask", [128, B, 16])
        mcum = sb("mcum", [128, B, 16])
        posm = sb("posm", [128, 16])
        prod = sb("prod", [128, 4, 16])
        slot_f = sb("slot_f", [128, B, 4])
        slot_u = sb("slot_u", [128, B, 4], U32)
        gfp = sb("gfp", [128, B, 4, 16])
        gf = sb("gf", [128, B, 16])
        mexp = sb("mexp", [128, 64])
        act_c = sb("act_c", [128, 1])
        act_bc = sb("act_bc", [128, 128])
        pos_c = sb("pos_c", [128, 1])
        ohj = sb("ohj", [128, 48])
        table = sb("table", [1, 96], I32)
        region_shift = sb("region_shift", [128, 16])
        red = sb("red", [128, B, 4])
        yslot = sb("yslot", [128, B, 4], U32)
        gfT = sb("gfT", [16, B * 128])
        G = sb("G", [128, 2, 4, 128])

        xin = sb("xin", [128, 8, 128])
        xeT = sb("xeT", [128, 8, 128])
        ha, hb, th, hu = (scratch[:, 512 * n:512 * n + 512].rearrange("p (u t) -> p u t", u=4) for n in range(4))
        hs = sb("hs", [128, 8, 128])
        h1 = (ha, hb)
        yo = sb("yo", [128, 8, 128])

        ld_x = [sem(f"ld_x{n}") for n in range(2)]
        ld_a = sem("ld_a")
        ld_b = sem("ld_b")
        ld_c = sem("ld_c")
        dve_step = sem("dve_step")
        pool_step = sem("pool_step")
        ones_v = sem("ones_v")
        zero_set = sem("zero_set")
        warm_ready = sem("warm_ready")
        keys_zeroed = sem("keys_zeroed")
        keys1_zeroed = sem("keys1_zeroed")
        keys1_half = sem("keys1_half")
        keys_spread = [sem(f"keys_spread{n}") for n in range(2)]
        zeroed = [sem(f"zeroed{n}") for n in range(REGION + 1)]
        xb_ready = sem("xb_ready")
        ln_stats = sem("ln_stats")
        ln_rstd = sem("ln_rstd")
        xa_ready = sem("xa_ready")
        exp_done = sem("exp_done")
        rt_stats = sem("rt_stats")
        rt_rstd = sem("rt_rstd")
        xn_ready = sem("xn_ready")
        vdif_ready = sem("vdif_ready")
        vexp_ready = sem("vexp_ready")
        mask_ready = sem("mask_ready")
        slot_ready = sem("slot_ready")
        scattered = [sem(f"scattered{n}") for n in range(2)]
        gf_ready = sem("gf_ready")
        mexp_ready = sem("mexp_ready")
        act_ready = sem("act_ready")
        ohj_ready = sem("ohj_ready")
        yslot_ready = sem("yslot_ready")
        base_ready = sem("base_ready")
        gathered = [sem(f"gathered{n}") for n in range(2)]
        gathered_1 = [sem(f"gathered_1_{b}") for b in range(B)]
        combined = sem("combined")
        x_in = [[sem(f"x_in{n}_{q}") for q in range(RING)] for n in range(2)]
        w_in = [[sem(f"w_in{n}_{q}") for q in range(DEPTH[n])] for n in range(2)]
        bias_up = sem("bias_up")
        th_ready = sem("th_ready")
        hs_ready = sem("hs_ready")
        y_out = [[sem(f"y_out{n}_{half}") for half in range(2)] for n in range(2)]
        ha_ready = sem("ha_ready")
        hu_ready = sem("hu_ready")
        out_done = sem("out_done")

        def J(b, *what):
            return job[(b, *what)]

        def product(what, layer, b, n=0):
            bk = bank_of(what, layer, b, n)
            return bk, J(bk, what, layer, b, n)

        def pvjob(layer, b, g):
            return product("pv", layer, b, g if layer else 0)

        def tbank(q):
            return f"T{q % 2}"

        def hbank(q):
            return f"S{q % 4}"

        def ybank(q):
            return ("O", "M")[q % 2]

        def unit_use(bk, layer, i, d, q):
            per = DEPTH[layer] // LOOP_SHARE[bk]
            return i * per + (J(bk, "loop", layer) + per * d + q // LOOP_SHARE[bk] + 1)

        def unit_count(layer, i, d, q, ring=1):
            return i * (DEPTH[layer] // ring) + (DEPTH[layer] * d + q) // ring + 1

        def expert_loop(engine, step, layer, deepest):
            for p in range(DEPTH[layer]):
                step(0, p, True, False)
            with engine.Fori(1, TURNS[layer]) as i:
                for p in range(DEPTH[layer]):
                    step(i, p, False, False)
            for p in range(deepest):
                step(TURNS[layer], p, False, True)

        def at(layer, p, lag, first, last):
            d, q = (p - lag) // DEPTH[layer], (p - lag) % DEPTH[layer]
            if first and d < 0 or last and d >= 0:
                return None
            return d, q

        def load_tokens(engine, layer, i, p, first):
            unit = UNIT[layer]
            row = engine.value_load(table[0:1, bass.ds(i * DEPTH[layer] + p, 1)], min_val=0, max_val=REGION * E[layer])
            row = engine.snap(row * 128)
            before_it = at(layer, p, RING, first, False)
            if before_it:
                engine.wait_ge(filled[tbank(p)], unit_use(tbank(p), layer, i, *before_it))
            r = p % RING
            engine.dma_start(xin[:, unit * r:unit * r + unit, :],
                             xs_dram[bass.ds(row, 128 * unit), :].rearrange("(u p) d -> p u d", p=128))\
                .then_inc(x_in[layer][r], 16)

        def load_weights(engine, layer, i, d, q, first):
            wp, wbuf = ((wp0, w0), (wp1, w1))[layer]
            ex = engine.value_load(table[0:1, bass.ds(i * DEPTH[layer] + (DEPTH[layer] * d + q + UNITS[layer]), 1)],
                                   min_val=0, max_val=E[layer] - 1)
            if not first:
                engine.wait_ge(filled[ybank(q)], unit_use(ybank(q), layer, i, d - 1, q))
            engine.dma_start(wbuf[:, q, :], wp[bass.ds(ex, 1), :, :].rearrange("e p n -> p (e n)"))\
                .then_inc(w_in[layer][q], 16)

        block = ctx.enter_context(nc.Block())

        @block.sync
        def _(sp):
            xv = x.rearrange("b t d -> t b d")
            sp.dma_start(X[:, 0:4, :], xv[:, 0:4, :]).then_inc(ld_x[0], 16)
            sp.dma_start(X[:, 4:8, :], xv[:, 4:8, :]).then_inc(ld_x[1], 16)
            sp.dma_start(qw_sb[:], q_w).then_inc(ld_a, 16)
            sp.dma_start(qb_sb[:], q_b).then_inc(ld_a, 16)
            sp.dma_start(pb_sb[:], proj_b.partition_broadcast(128)).then_inc(ld_b, 16)
            sp.dma_start(pw_sb[:], proj_w).then_inc(ld_b, 16)
            sp.dma_start(ns_sb[:], norm_s.partition_broadcast(128)).then_inc(ld_b, 16)
            sp.dma_start(wg_sb[:], wg).then_inc(ld_b, 16)
            sp.dma_start(bg_sb[:], bg.partition_broadcast(128)).then_inc(ld_b, 16)
            sp.dma_start(b20_sb[:], b2_0).then_inc(ld_b, 16)
            sp.wait_ge(keys_zeroed, 2)
            for n in range(2):
                sp.wait_ge(freed[f"T{n}"], J(f"T{n}", "k0", n))
                cols = slice(4 * M * n, 4 * M * (n + 1))
                for g in range(NG):
                    sp.dma_start(KF0[32 * g:32 * g + 32, GH * g:GH * g + GH, cols],
                                 KX0[32 * g:32 * g + 32, :, cols]).then_inc(keys_spread[n], 16)
            sp.wait_ge(zero_set, 1)
            xz = xs_dram[0:REGION * E[0] * 128, :].rearrange("(e r p) d -> r p e d", r=REGION, p=128)
            for r in range(REGION):
                sp.dma_start(xz[r], zeros[:, None, :].to_broadcast([128, E[0], D])).then_inc(zeroed[r], 16)
            sp.dma_start(xs_dram[REGION * E[0] * 128:rows, :].rearrange("(u p) d -> p u d", p=128),
                         zeros[:, None, :].to_broadcast([128, 2, D])).then_inc(zeroed[REGION], 16)
            sp.dma_start(Wk_sb[:], Wk).then_inc(ld_c, 16)
            sp.dma_start(Wv_sb[:], Wv).then_inc(ld_c, 16)
            sp.dma_start(Wq_sb[:], Wq).then_inc(ld_c, 16)
            sp.dma_start(Wo_sb[:], Wo).then_inc(ld_c, 16)
            sp.dma_start(bo_sb[:], bo.partition_broadcast(128)).then_inc(ld_c, 16)
            sp.dma_start(Wr_sb[:], Wr).then_inc(ld_c, 16)
            sp.dma_start(br_sb[:], br.partition_broadcast(128)).then_inc(ld_c, 16)
            sp.dma_start(b21_sb[:], b2_1).then_inc(ld_c, 16)

            for layer in range(2):
                sp.wait_ge(freed["O"], J("O", "table", layer))

                def step(i, p, first, last):
                    if first and p == 0:
                        for q in range(EARLY[layer]):
                            load_weights(sp, layer, i, 0, q, first)
                        sp.wait_ge(scattered[layer], 16 * B * TOPK[layer])
                        sp.wait_ge(zeroed[REGION], 16)
                    if p % RING == 0:
                        load_tokens(sp, layer, i, p, first)
                    if not (first and p < EARLY[layer]):
                        load_weights(sp, layer, i, 0, p, first)

                expert_loop(sp, step, layer, 0)
            for n in range(2):
                for half in range(2):
                    sp.wait_ge(y_out[n][half], 16 * STORES[n])
            sp.wait_ge(out_done, 16 * B)

        @block.gpsimd
        def _(pool):
            steps = [0]

            def link(ins):
                steps[0] += 1
                ins.then_inc(pool_step, 1)
                pool.wait_ge(pool_step, steps[0])

            nc.gpsimd.memset(zeros[:], 0.0).then_inc(zero_set, 1)
            nc.gpsimd.memset(V0[:], 1.0).then_inc(ones_v, 1)
            nc.gpsimd.memset(KF0[:, 0:8, :], 0.0).then_inc(keys_zeroed, 1)

            def rsqrt_eps(dst, tmp, src, n):
                link(nc.gpsimd.tensor_scalar(tmp, src, EPS, None, ALU.add))
                return nc.gpsimd.tensor_tensor(dst, tmp, C[:, C_NH:C_NH + 1].to_broadcast([128, n]) if n > 1 else C[:, C_NH:C_NH + 1], ALU.pow)

            pool.wait_ge(ld_a, LD_A)
            pool.wait_ge(ln_stats, 1)
            rsqrt_eps(rstd[:], var_eps[:], mv[:, :, 1], B).then_inc(ln_rstd, 1)
            pool.wait_ge(ld_b, LD_B)
            for b in range(B):
                nc.gpsimd.tensor_tensor(XB[:, b, :], X[:, b, :], pb_sb[:], ALU.add).then_inc(xb_ready, 1)

            nc.gpsimd.memset(K1[:, 4:8, :, :], 0.0).then_inc(keys1_zeroed, 1)

            def route_rstd(layer, b):
                pool.wait_ge(rt_stats, layer * B + b + 1)
                if layer == 0:
                    link(rsqrt_eps(rstd[:, b:b + 1], var_eps[:, b:b + 1], mv[:, b, 1:2], 1))
                    link(nc.gpsimd.tensor_scalar(rms[:, b:b + 1], mv[:, b, 1:2], rstd[:, b:b + 1], rstd[:, b:b + 1],
                                                 ALU.mult, ALU.mult))
                    rsqrt_eps(rrms[:, b:b + 1], var_eps[:, b:b + 1], rms[:, b:b + 1], 1).then_inc(rt_rstd, 1)
                else:
                    rsqrt_eps(rstd[:, b:b + 1], var_eps[:, b:b + 1], mv[:, b, 1:2], 1).then_inc(rt_rstd, 1)

            def scatter(layer, b):
                pool.wait_ge(slot_ready, layer * B + b + 1)
                if layer == 0:
                    pool.wait_ge(zeroed[b], 16)
                for k in range(TOPK[layer]):
                    nc.gpsimd.indirect_dma_start(
                        out=xs_dram, out_offset=bass.IndirectOffsetOnAxis(ap=slot_u[:, b, k:k + 1], axis=0),
                        in_=XN[:, b, :], in_offset=None).then_inc(scattered[layer], 16)

            def gather(layer, b):
                if b >= 2 and layer == 0:
                    pool.wait_ge(combined, b - 1)
                for k in range(TOPK[layer]):
                    nc.gpsimd.indirect_dma_start(
                        out=G[:, b % 2, k, :] if layer == 0 else G[:, b // 4, b % 4, :],
                        out_offset=None, in_=ys_dram[layer],
                        in_offset=bass.IndirectOffsetOnAxis(ap=yslot[:, b, k:k + 1], axis=0))\
                        .then_inc(gathered[b % 2] if layer == 0 else gathered_1[b], 16)

            def ln_pow(b):
                pool.wait_ge(ln_stats, b + 2)
                rsqrt_eps(rstd[:, b:b + 1], var_eps[:, b:b + 1], mv[:, b, 1:2], 1).then_inc(ln_rstd, 1)

            for b in range(B + 2):
                if 0 <= b - 1 < B:
                    route_rstd(0, b - 1)
                if b == B + 1:
                    bk, n = pvjob(0, B - 1, 0)
                    pool.wait_ge(filled[bk], n)
                    pool.wait_ge(rt_rstd, B)
                    nc.gpsimd.memset(K1[64:128, 0:4, 0, :], 0.0).then_inc(keys1_zeroed, 1)
                if 0 <= b - 2 < B:
                    scatter(0, b - 2)
            pool.wait_ge(keys1_zeroed, 2)

            def expert_steps(layer):
                def step(i, p, first, last):
                    where = at(layer, p, 2, first, last)
                    if layer == 0 and where:
                        d, q = where
                        pool.wait_ge(w_in[0][q], 16 * i + 16 * (d + 1))
                        nc.gpsimd.tensor_tensor(w0[:, q, 385:386], w0[:, q, 385:386], ones[:, 0:1], ALU.add)\
                            .then_inc(bias_up, 1)
                    if not last and p % RING > 0:
                        load_tokens(pool, layer, i, p, first)

                return step

            pool.wait_ge(freed["O"], J("O", "table", 0))
            pool.wait_ge(scattered[0], 16 * B * TOPK[0])
            pool.wait_ge(zeroed[REGION], 16)
            expert_loop(pool, expert_steps(0), 0, 2)

            pool.wait_ge(yslot_ready, 1)
            for half in range(2):
                pool.wait_ge(y_out[0][half], 16 * STORES[0])
            nc.gpsimd.memset(V1[:, :, :, HD[1]:HD[1] + 1], 1.0).then_inc(ones_v, 1)
            gather(0, 0)
            gather(0, 1)
            ln_pow(0)
            gather(0, 2)
            ln_pow(1)
            for b in range(B - 1):
                if b + 3 < B:
                    gather(0, b + 3)
                if b + 2 < B:
                    ln_pow(b + 2)
                if 0 <= b - 1:
                    route_rstd(1, b - 1)
                if 0 <= b - 2:
                    scatter(1, b - 2)
            route_rstd(1, B - 2)
            route_rstd(1, B - 1)
            for b in range(B - 3, B):
                scatter(1, b)
            pool.wait_ge(freed["O"], J("O", "table", 1))
            pool.wait_ge(scattered[1], 16 * B * TOPK[1])
            expert_loop(pool, expert_steps(1), 1, 0)
            pool.wait_ge(yslot_ready, 2)
            for half in range(2):
                pool.wait_ge(y_out[1][half], 16 * STORES[1])
            pool.wait_ge(combined, B)
            for b in range(B):
                gather(1, b)

        @block.scalar
        def _(act):
            act.dma_start(C[:], cst).then_inc(ld_a, 16)
            act.dma_start(ctx_sb[:], ctxT).then_inc(ld_a, 16)
            act.dma_start(kvw_sb[:], kv_w).then_inc(ld_a, 16)
            act.dma_start(kvb_sb[:], kv_b).then_inc(ld_a, 16)

            def copy_out(bk, n, dst, src, func=ACT.Copy, **kw):
                act.wait_ge(filled[bk], n)
                nc.scalar.activation(dst, src, func, **kw).then_inc(freed[bk], 1)

            act.wait_ge(ld_a, LD_A)
            act.wait_ge(ones_v, 1)
            for n in range(2):
                bk = ("O", "M")[n]
                copy_out(bk, J(bk, "v0", n), V0[:, 4 * n:4 * n + 4, :, 0:8],
                         bank[bk][0:M, :].rearrange("p (b h d) -> p b h d", b=4, h=NH))
            copy_out("S0", J("S0", "xT0", 0), XT0[:, 0:512], bank["S0"][:])
            copy_out("T0", J("T0", "q0", 0), QT0[:, 0:512], bank["T0"][:], ACT.Identity, bias=qb_sb[:, 0:1])

            def exps(layer, b, g):
                act.wait_ge(freed[f"S{g}"], J(f"S{g}", "scores", layer, b, g))
                pg = P[:, b % 2, g, :]
                nc.scalar.activation(pg, pg, ACT.Exp, scale=float(HD[layer]) ** -0.5).then_inc(exp_done, 1)

            def pT_out(layer, b, g):
                if b > 0:
                    bk, n = pvjob(layer, b - 1, g)
                    act.wait_ge(filled[bk], n)
                elif layer:
                    bk, n = pvjob(0, B - 1, g)
                    act.wait_ge(filled[bk], n)
                bk = f"T{g % 2}"
                copy_out(bk, J(bk, "pT", layer, b, g), PT[:, g, :], bank[bk][0:M, :])

            def xT_out(b):
                if b > 0:
                    act.wait_ge(filled["M"], J("M", "q", b - 1, 1))
                copy_out("M", J("M", "xT", b), XT1[:], bank["M"][:, 0:128])

            def q_out(b, n):
                if b >= 2:
                    act.wait_ge(filled["S3"], J("S3", "scores", 1, b - 2, 3))
                copy_out("M", J("M", "q", b, n), QT1[:, b % 2, 4 * n:4 * n + 4, :],
                         bank["M"][:, :].rearrange("p (c t) -> p c t", c=4))

            def oT_out(layer, b, n):
                bk, use = product("oT", layer, b, n)
                if b > 0 or layer:
                    pk, done = product("proj", layer, b - 1) if b else product("proj", 0, B - 1)
                    act.wait_ge(filled[pk], done)
                if layer:
                    copy_out(bk, use, OT[:, 4 * n:4 * n + 4, :],
                             bank[bk][:].rearrange("p (c t) -> p c t", c=4))
                else:
                    copy_out(bk, use, OT[:, 0, :], bank[bk][:, 0:128],
                             ACT.Identity, bias=kvb_sb[:, 1:2])

            def xnT_out(layer, b):
                bk, use = product("xnT", layer, b)
                if b > 0 or layer:
                    lk, done = product("logits", layer, b - 1) if b else product("logits", 0, B - 1)
                    act.wait_ge(filled[lk], done)
                copy_out(bk, use, XNT[:], bank[bk][:, 0:128])

            def gate_exps(layer, b):
                act.wait_ge(vdif_ready, layer * B + b + 1)
                w = (4, 8)[layer]
                nc.scalar.activation(vexp[:, b, 0:w], vdif[:, b, 0:w], ACT.Exp,
                                     accum_out=vsum[:, b:b + 1]).then_inc(vexp_ready, 1)

            def k1_out(start, count):
                if start == 0:
                    act.wait_ge(keys1_zeroed, 1)
                for n in range(start, start + count):
                    bk = f"S{n % 4}"
                    c, half = n // 2, n % 2
                    act.wait_ge(filled[bk], J(bk, "k1", n))
                    for k in range(2):
                        r = slice(64 * k, 64 * k + 64)
                        ins = nc.scalar.activation(K1[r, c, k, 308 * half:308 * half + 308], bank[bk][r, 0:308],
                                                   ACT.Copy)
                    ins.then_inc(freed[bk], 1)

            def attention_0():
                for g in range(NG):
                    exps(0, 0, g)
                for b in range(B + 2):
                    now, following, last, routed = b < B, b + 1 < B, 0 <= b - 1 < B, 0 <= b - 2 < B
                    if now:
                        pT_out(0, b, 0)
                    if b == B + 1:
                        k1_out(5, 1)
                    if routed:
                        xnT_out(0, b - 2)
                    if not now:
                        k1_out(0 if b == B else 6, 1)
                    if now:
                        pT_out(0, b, 1)
                    if following:
                        exps(0, b + 1, 0)
                    if last:
                        oT_out(0, b - 1, 0)
                    if b == B:
                        k1_out(1, 1)
                    if now:
                        pT_out(0, b, 2)
                    if following:
                        exps(0, b + 1, 1)
                    if routed:
                        gate_exps(0, b - 2)
                    if not now:
                        k1_out(2 if b == B else 7, 3 if b == B else 1)
                    if now:
                        pT_out(0, b, 3)
                    if following:
                        exps(0, b + 1, 2)
                        exps(0, b + 1, 3)

            def attention_1():
                for g in range(NG):
                    exps(1, 0, g)
                for b in range(B - 1):
                    last, routed = 0 <= b - 1, 0 <= b - 2
                    pT_out(1, b, 0)
                    xT_out(b + 1)
                    pT_out(1, b, 1)
                    if last:
                        oT_out(1, b - 1, 0)
                    q_out(b + 1, 0)
                    q_out(b + 1, 1)
                    pT_out(1, b, 2)
                    if last:
                        oT_out(1, b - 1, 1)
                    exps(1, b + 1, 0)
                    pT_out(1, b, 3)
                    exps(1, b + 1, 1)
                    if routed:
                        xnT_out(1, b - 2)
                        gate_exps(1, b - 2)
                    exps(1, b + 1, 2)
                    exps(1, b + 1, 3)
                pT_out(1, B - 1, 0)
                pT_out(1, B - 1, 1)
                oT_out(1, B - 2, 0)
                oT_out(1, B - 2, 1)
                pT_out(1, B - 1, 2)
                pT_out(1, B - 1, 3)
                xnT_out(1, B - 3)
                oT_out(1, B - 1, 0)
                oT_out(1, B - 1, 1)
                gate_exps(1, B - 3)
                xnT_out(1, B - 2)
                xnT_out(1, B - 1)
                gate_exps(1, B - 2)
                gate_exps(1, B - 1)

            def gT_out(layer):
                for n in range(2):
                    bk = f"T{n}"
                    copy_out(bk, J(bk, "gT", layer, n), gfT[0:E[layer], 512 * n:512 * n + 512],
                             bank[bk][0:E[layer], :])

            attention_0()
            k1_out(8, 2)
            nc.scalar.activation(K1[0:64, 0:4, 1, :], C[0:64, None, C_IOTA:C_IOTA + 1].to_broadcast([64, 4, B * M]),
                                 ACT.Copy).then_inc(keys1_half, 1)
            k1_out(10, 6)

            def expert_steps(layer):
                unit = UNIT[layer]
                w = 128 * unit

                def step(i, p, first, last):
                    if not last:
                        before_it = at(layer, p, RING, first, False)
                        if before_it:
                            hbk = hbank(before_it[1])
                            act.wait_ge(filled[hbk], unit_use(hbk, layer, i, *before_it))
                        tb = tbank(p)
                        act.wait_ge(filled[tb], unit_use(tb, layer, i, 0, p))
                        x0 = unit * (p % RING)
                        nc.scalar.activation(xeT[:, x0:x0 + unit, :],
                                             bank[tb][:, 0:w].rearrange("p (u t) -> p u t", u=unit), ACT.Copy)\
                            .then_inc(freed[tb], 1)
                    where = at(layer, p, LAG_H[layer], first, last)
                    if layer == 0 and where:
                        d, q = where
                        s2 = slice(2 * (q % 2), 2 * (q % 2) + 2)
                        act.wait_ge(ha_ready, unit_count(0, i, d, q))
                        nc.scalar.activation(th[:, s2, :], ha[:, s2, :], ACT.Tanh, scale=ALPHA / 2)\
                            .then_inc(th_ready, 1)
                    where = at(layer, p, LAG_Y[layer], first, last)
                    if where:
                        d, q = where
                        yb, r = ybank(q), q % RING
                        half = r // 2
                        if layer == 0 and q % 2 == 0 and (not first or q >= RING):
                            act.wait_ge(y_out[0][half], 16 * unit_count(0, i, d, q, RING) - 16)
                        act.wait_ge(filled[yb], unit_use(yb, layer, i, d, q))
                        nc.scalar.activation(yo[:, unit * r:unit * r + unit, :],
                                             bank[yb][:, 0:w].rearrange("p (u t) -> p u t", u=unit),
                                             ACT.Copy, scale=(0.5, 1.0)[layer]).then_inc(freed[yb], 1)
                        if q % 2 == 1:
                            for written in (q - 1, q):
                                act.wait_ge(freed[ybank(written)], unit_use(ybank(written), layer, i, d, written))
                            act.dma_start(
                                ys_dram[layer][bass.ds(i * (DEPTH[layer] * w) + (DEPTH[layer] * d + q - 1) * w, 2 * w), :]
                                .rearrange("(u p) d -> p u d", p=128),
                                yo[:, 2 * half * unit:2 * (half + 1) * unit, :]).then_inc(y_out[layer][half], 16)
                            if layer == 1 and not (last and q + 1 >= DEPTH[layer]) and not (first and q + 1 < RING):
                                act.wait_ge(y_out[layer][1 - half], 16 * unit_count(layer, i, d, q + 1, RING) - 16)

                return step

            expert_loop(act, expert_steps(0), 0, LAG_Y[0])
            gT_out(0)

            for n in range(16):
                bk = f"S{n % 4}"
                b, half = n // 2, n % 2
                copy_out(bk, J(bk, "v1", n), V1[:, b, 8 * half:8 * half + 8, 0:64],
                         bank[bk][0:M, :].rearrange("p (h d) -> p h d", h=8))
            xT_out(0)
            q_out(0, 0)
            q_out(0, 1)
            attention_1()

            expert_loop(act, expert_steps(1), 1, LAG_Y[1])
            gT_out(1)

            for b in range(B):
                act.wait_ge(combined, B + b + 1)
                act.dma_start(out[b], X[:, b, :]).then_inc(out_done, 16)

        @block.vector
        def _(dve):
            steps = [0]

            def link(ins):
                steps[0] += 1
                ins.then_inc(dve_step, 1)
                dve.wait_ge(dve_step, steps[0])

            def stats(src, b):
                link(nc.vector.bn_stats(st6[:, b, :], src))
                return nc.vector.bn_aggr(mv[:, b, :], st6[:, b, :])

            nc.vector.memset(warm[:], 0.0).then_inc(warm_ready, 1)
            nc.vector.memset(KF0[:, 8:16, :], 0.0).then_inc(keys_zeroed, 1)
            for b in range(B):
                dve.wait_ge(ld_x[b // 4], 16)
                ins = stats(X[:, b, :], b)
            ins.then_inc(ln_stats, 1)

            def keys_out(n):
                bk = f"T{n}"
                dve.wait_ge(filled[bk], J(bk, "k0", n))
                for j in range(GH):
                    ins = nc.vector.tensor_scalar(KX0[:, j, 308 * n:308 * n + 308], bank[bk][:, 0:308],
                                                  kvb_sb[:, 0:1], C[:, C_HEAD + j:C_HEAD + j + 1], ALU.add, ALU.mult)
                ins.then_inc(freed[bk], 1)

            dve.wait_ge(ld_a, LD_A)
            keys_out(0)
            dve.wait_ge(ln_rstd, 1)
            for b in range(B):
                nc.vector.tensor_scalar(XA[:, b, :], X[:, b, :], mv[:, b, 0:1], rstd[:, b:b + 1],
                                        ALU.subtract, ALU.mult).then_inc(xa_ready, 1)
            dve.wait_ge(filled["S1"], J("S1", "xT0", 1))
            nc.vector.tensor_copy(XT0[:, 512:1024], bank["S1"][:]).then_inc(freed["S1"], 1)
            keys_out(1)

            def shift(layer, b, g):
                bk = f"S{g}"
                sc = bank[bk][:, 0:GM].rearrange("p (h m) -> p h m", h=GH)
                dve.wait_ge(filled[bk], J(bk, "scores", layer, b, g))
                link(nc.vector.tensor_reduce(negmax[:, g, :], sc, AX_X, ALU.max, negate=True))
                tb = f"T{g % 2}"
                if b >= 2:
                    dve.wait_ge(filled[tb], J(tb, "pT", layer, b - 2, g))
                elif layer:
                    dve.wait_ge(filled[tb], J(tb, "pT", 0, B - 2 + b, g))
                nc.vector.tensor_tensor(P[:, b % 2, g, :].rearrange("p (h m) -> p h m", h=GH), sc,
                                        negmax[:, g, :, None].to_broadcast([128, GH, M]), ALU.add)\
                    .then_inc(freed[bk], 1)

            def pv_out(layer, b, g):
                bk, n = pvjob(layer, b, g)
                d = HD[layer]
                heads = GH if layer else NH
                o = bank[bk][:, 0:heads * (d + 1)].rearrange("p (h e) -> p h e", h=heads)
                dve.wait_ge(filled[bk], n)
                link(nc.vector.reciprocal(recip[:, g, 0:heads], o[:, :, d]))
                if b > 1 or layer:
                    ob, done = product("oT", layer, b - 2, layer) if b > 1 else product("oT", 0, B - 2 + b)
                    dve.wait_ge(filled[ob], done)
                if layer:
                    dst = OS[:, b % 2, 256 * g:256 * g + 256].rearrange("p (h d) -> p h d", d=64)
                else:
                    dst = OS[:, b % 2, 0:128].rearrange("p (h d) -> p h d", d=8)
                nc.vector.tensor_tensor(dst, o[:, :, 0:d], recip[:, g, 0:heads, None].to_broadcast([128, heads, d]),
                                        ALU.mult).then_inc(freed[bk], 1)

            def proj_out(layer, b):
                bk, n = product("proj", layer, b)
                dve.wait_ge(filled[bk], n)
                if layer == 0:
                    dve.wait_ge(xb_ready, b + 1)
                base = XB[:, b, :]
                ins = nc.vector.tensor_tensor(XR[:, b, :], bank[bk][:, 0:128], base, ALU.add)
                ins.then_inc(freed[bk], 1)
                dve.wait_ge(freed[bk], n)
                stats(XR[:, b, :], b).then_inc(rt_stats, 1)

            def normed(layer, b):
                dve.wait_ge(rt_rstd, layer * B + b + 1)
                if layer == 0:
                    link(nc.vector.tensor_scalar(XF[:, b, :], XR[:, b, :], mv[:, b, 0:1], rstd[:, b:b + 1],
                                                 ALU.subtract, ALU.mult))
                    nc.vector.scalar_tensor_tensor(XN[:, b, :], XF[:, b, :], rrms[:, b:b + 1], ns_sb[:],
                                                   ALU.mult, ALU.mult).then_inc(xn_ready, 1)
                else:
                    nc.vector.tensor_scalar(XN[:, b, :], XR[:, b, :], mv[:, b, 0:1], rstd[:, b:b + 1],
                                            ALU.subtract, ALU.mult).then_inc(xn_ready, 1)

            def choose(layer, b):
                e, k = E[layer], TOPK[layer]
                bk, n = product("logits", layer, b)
                dve.wait_ge(filled[bk], n)
                nc.vector.tensor_tensor(lg[:, 0:e], bank[bk][:, 0:e], br_l[layer][:, 0:e], ALU.add)\
                    .then_inc(freed[bk], 1)
                dve.wait_ge(freed[bk], n)
                link(nc.vector.max(top8[:], lg[:, 0:e]))
                link(nc.vector.max_index(idx8[:], top8[:], lg[:, 0:e]))
                src = top8[:, 0:4] if layer == 0 else lg[:, 0:8]
                nc.vector.tensor_scalar(vdif[:, b, 0:(4, 8)[layer]], src, top8[:, 0:1], None, ALU.subtract)\
                    .then_inc(vdif_ready, 1)
                link(nc.vector.tensor_tensor(hot[:, b, 0:k, 0:e],
                                             C[:, None, C_IOTA:C_IOTA + e].to_broadcast([128, k, e]),
                                             idx8[:, 0:k, None].to_broadcast([128, k, e]), ALU.is_equal))
                if k > 1:
                    link(nc.vector.tensor_reduce(mask[:, b, 0:e],
                                                 hot[:, b, 0:k, 0:e].rearrange("p k e -> p e k"), AX_X, ALU.add))
                else:
                    link(nc.vector.tensor_copy(mask[:, b, 0:e], hot[:, b, 0, 0:e]))
                if b == 0:
                    nc.vector.tensor_copy(mcum[:, b, 0:e], mask[:, b, 0:e]).then_inc(mask_ready, 1)
                else:
                    nc.vector.tensor_tensor(mcum[:, b, 0:e], mcum[:, b - 1, 0:e], mask[:, b, 0:e], ALU.add)\
                        .then_inc(mask_ready, 1)

            def place(layer, b):
                e, k = E[layer], TOPK[layer]
                bk, n = product("rank", layer, b)
                dve.wait_ge(filled[bk], n)
                nc.vector.tensor_tensor(posm[:, 0:e], bank[bk][:, 0:e], C[:, C_RB:C_RB + e], ALU.add)\
                    .then_inc(freed[bk], 1)
                dve.wait_ge(freed[bk], n)
                link(nc.vector.tensor_tensor(prod[:, 0:k, 0:e], hot[:, b, 0:k, 0:e],
                                             posm[:, None, 0:e].to_broadcast([128, k, e]), ALU.mult))
                link(nc.vector.tensor_reduce(slot_f[:, b, 0:k], prod[:, 0:k, 0:e], AX_X, ALU.add))
                nc.vector.tensor_copy(slot_u[:, b, 0:k], slot_f[:, b, 0:k]).then_inc(slot_ready, 1)

            def combine(layer, b):
                k = TOPK[layer]
                dst = (X2, X)[layer]
                rows = G[:, b % 2, :, :] if layer == 0 else G[:, b // 4, b % 4:b % 4 + 1, :]
                if layer == 0:
                    dve.wait_ge(gathered[b % 2], 16 * k * (b // 2 + 1))
                else:
                    dve.wait_ge(gathered_1[b], 16)
                for j in range(k):
                    ins = nc.vector.scalar_tensor_tensor(dst[:, b, :], rows[:, j, :], gates[:, b, j:j + 1],
                                                         XR[:, b, :] if j == 0 else dst[:, b, :], ALU.mult, ALU.add)
                    if j < k - 1:
                        link(ins)
                ins.then_inc(combined, 1)
                if layer == 0:
                    dve.wait_ge(combined, b + 1)
                    nc.vector.tensor_tensor(XB[:, b, :], X2[:, b, :], bo_sb[:], ALU.add)
                    stats(X2[:, b, :], b).then_inc(ln_stats, 1)

            def attn_norm(b):
                dve.wait_ge(ln_rstd, 1 + b + 1)
                nc.vector.tensor_scalar(XA[:, b, :], X2[:, b, :], mv[:, b, 0:1], rstd[:, b:b + 1],
                                        ALU.subtract, ALU.mult).then_inc(xa_ready, 1)

            def attention_0():
                shift(0, 0, 0)
                shift(0, 0, 1)
                dve.wait_ge(filled["T1"], J("T1", "q0", 1))
                nc.vector.tensor_scalar(QT0[:, 512:1024], bank["T1"][:], qb_sb[:, 0:1], None, ALU.add)\
                    .then_inc(freed["T1"], 1)
                shift(0, 0, 2)
                shift(0, 0, 3)
                for b in range(B + 2):
                    following, last, routed = b + 1 < B, 0 <= b - 1 < B, 0 <= b - 2 < B
                    if last:
                        pv_out(0, b - 1, 0)
                    if following:
                        shift(0, b + 1, 0)
                        shift(0, b + 1, 1)
                    if routed:
                        choose(0, b - 2)
                    if last:
                        proj_out(0, b - 1)
                    if following:
                        shift(0, b + 1, 2)
                    if routed:
                        place(0, b - 2)
                    if following:
                        shift(0, b + 1, 3)
                    if last:
                        normed(0, b - 1)

            def attention_1():
                for g in range(NG):
                    shift(1, 0, g)
                for b in range(B - 1):
                    last, routed = 0 <= b - 1, 0 <= b - 2
                    if b + 2 < B:
                        combine(0, b + 2)
                    pv_out(1, b, 0)
                    shift(1, b + 1, 0)
                    shift(1, b + 1, 1)
                    pv_out(1, b, 1)
                    shift(1, b + 1, 2)
                    pv_out(1, b, 2)
                    if routed:
                        choose(1, b - 2)
                    shift(1, b + 1, 3)
                    pv_out(1, b, 3)
                    if b + 2 < B:
                        attn_norm(b + 2)
                    if last:
                        proj_out(1, b - 1)
                    if routed:
                        place(1, b - 2)
                    if last:
                        normed(1, b - 1)
                pv_out(1, B - 1, 0)
                pv_out(1, B - 1, 1)
                proj_out(1, B - 2)
                pv_out(1, B - 1, 2)
                pv_out(1, B - 1, 3)
                normed(1, B - 2)
                choose(1, B - 3)
                proj_out(1, B - 1)
                place(1, B - 3)
                normed(1, B - 1)
                choose(1, B - 2)
                choose(1, B - 1)
                place(1, B - 2)
                place(1, B - 1)

            def tables(layer):
                e, k = E[layer], TOPK[layer]
                cand = CAND[layer]
                nc_ = e * cand
                o = C_PL + layer * C_PL_W
                nt = UNITS[layer]
                nc.vector.tensor_copy(mexp[:].rearrange("p (e t) -> p e t", t=cand),
                                      mcum[:, B - 1, 0:e, None].to_broadcast([128, e, cand]))\
                    .then_inc(mexp_ready, 1)
                dve.wait_ge(vexp_ready, layer * B + B)
                link(nc.vector.reciprocal(vrec[:], vsum[:]))
                if k > 1:
                    link(nc.vector.tensor_tensor(gates[:, :, 0:k], vexp[:, :, 0:k],
                                                 vrec[:, :, None].to_broadcast([128, B, k]), ALU.mult))
                else:
                    link(nc.vector.tensor_copy(gates[:, :, 0], vrec[:]))
                dve.wait_ge(filled["O"], J("O", "count", layer))
                nc.vector.tensor_tensor(act_c[0:nc_, :], bank["O"][0:nc_, 0:1], C[0:nc_, o:o + 1], ALU.is_gt)\
                    .then_inc(freed["O"], 1)
                dve.wait_ge(freed["O"], J("O", "count", layer))
                nc.vector.tensor_scalar(act_bc[0:nc_, :], C[0:nc_, C_ONE:C_ONE + 128], act_c[0:nc_, :], None, ALU.mult)\
                    .then_inc(act_ready, 1)
                dve.wait_ge(filled["O"], J("O", "pos", layer))
                nc.vector.tensor_copy(pos_c[0:nc_, :], bank["O"][0:nc_, 0:1]).then_inc(freed["O"], 1)
                dve.wait_ge(freed["O"], J("O", "pos", layer))
                nc.vector.tensor_scalar(ohj[0:nc_, 0:nt], C[0:nc_, C_IOTA:C_IOTA + nt], pos_c[0:nc_, :],
                                        act_c[0:nc_, :], ALU.is_equal, ALU.mult).then_inc(ohj_ready, 1)
                dve.wait_ge(filled["O"], J("O", "table", layer))
                nc.vector.tensor_scalar(table[0:1, 0:nt], bank["O"][0:1, 0:nt], float(REGION * e), None, ALU.add)
                ins = nc.vector.tensor_copy(table[0:1, nt:2 * nt], bank["O"][0:1, nt:2 * nt])
                ins.then_inc(freed["O"], 1)
                dve.wait_ge(freed["O"], J("O", "table", layer))
                dve.wait_ge(filled["M"], J("M", "start", layer))
                nc.vector.tensor_tensor(region_shift[:, 0:e], bank["M"][:, 0:e], C[:, C_RB:C_RB + e], ALU.subtract)\
                    .then_inc(freed["M"], 1)
                dve.wait_ge(freed["M"], J("M", "start", layer))
                for b in range(B):
                    ins = nc.vector.tensor_tensor(gfp[:, b, 0:k, 0:e], hot[:, b, 0:k, 0:e],
                                                  region_shift[:, None, 0:e].to_broadcast([128, k, e]), ALU.mult)
                link(ins)
                for b in range(B):
                    ins = nc.vector.tensor_reduce(red[:, b, 0:k], gfp[:, b, 0:k, 0:e], AX_X, ALU.add)
                link(ins)
                nc.vector.tensor_tensor(yslot[:, :, 0:k], red[:, :, 0:k], slot_f[:, :, 0:k], ALU.add)\
                    .then_inc(yslot_ready, 1)
                for b in range(B):
                    ins = nc.vector.tensor_tensor(gfp[:, b, 0:k, 0:e], hot[:, b, 0:k, 0:e],
                                                  gates[:, b, 0:k, None].to_broadcast([128, k, e]), ALU.mult)
                link(ins)
                for b in range(B):
                    ins = nc.vector.tensor_reduce(gf[:, b, 0:e], gfp[:, b, 0:k, 0:e].rearrange("p k e -> p e k"),
                                                  AX_X, ALU.add)
                ins.then_inc(gf_ready, 1)

            def base(layer):
                for n in range(2):
                    bk = f"T{n}"
                    dve.wait_ge(filled[bk], J(bk, "b2", layer, n))
                    xr = XR[:, 4 * n:4 * n + 4, :]
                    nc.vector.tensor_tensor(xr, bank[bk][:].rearrange("p (b d) -> p b d", b=4), xr, ALU.add)\
                        .then_inc(freed[bk], 1)
                dve.wait_ge(freed["T1"], J("T1", "b2", layer, 1))

            attention_0()
            tables(0)
            link(nc.vector.tensor_tensor(XR[:], XR[:], XF[:], ALU.add))

            def expert_steps(layer):
                def step(i, p, first, last):
                    hidden, scaled = at(layer, p, LAG_H[layer], first, last), at(layer, p, LAG_HS, first, last)
                    if layer == 1:
                        if hidden:
                            d, q = hidden
                            hbk = hbank(q)
                            dve.wait_ge(filled[hbk], unit_use(hbk, 1, i, d, q))
                            for c in range(4):
                                ins = nc.vector.tensor_scalar(h1[q % 2][:, c, :], bank[hbk][:, 128 * c:128 * c + 128],
                                                              w1[:, q, 1024 + c:1025 + c], 0.0, ALU.add, ALU.max)
                            ins.then_inc(freed[hbk], 1)
                        return
                    if scaled:
                        d, q = scaled
                        number = unit_count(0, i, d, q)
                        m2, r = slice(2 * (q % 2), 2 * (q % 2) + 2), q % RING
                        dve.wait_ge(th_ready, number)
                        nc.vector.scalar_tensor_tensor(hu[:, m2, :], th[:, m2, :], 1.0, ha[:, m2, :],
                                                       ALU.add, ALU.mult).then_inc(hu_ready, 1)
                    if hidden:
                        dh, qh = hidden
                        hbk = hbank(qh)
                        s2 = slice(2 * (qh % 2), 2 * (qh % 2) + 2)
                        h = bank[hbk][:, :].rearrange("p (half u t) -> p half u t", half=2, u=2)
                        dve.wait_ge(filled[hbk], unit_use(hbk, 0, i, dh, qh))
                        nc.vector.tensor_scalar(ha[:, s2, :], h[:, 0, :, :], w0[:, qh, 384:385], LIMIT,
                                                ALU.add, ALU.min).then_inc(ha_ready, 1)
                    if scaled:
                        dve.wait_ge(hu_ready, number)
                        nc.vector.scalar_tensor_tensor(hs[:, 2 * r:2 * r + 2, :], hb[:, m2, :], 1.0 - LIMIT,
                                                       hu[:, m2, :], ALU.max, ALU.mult).then_inc(hs_ready, 1)
                    if hidden:
                        dve.wait_ge(bias_up, unit_count(0, i, dh, qh))
                        if not first or p > LAG_HS:
                            dve.wait_ge(hs_ready, unit_count(0, i, dh, qh) - 2)
                        nc.vector.tensor_scalar(hb[:, s2, :], h[:, 1, :, :], w0[:, qh, 385:386], LIMIT + 1.0,
                                                ALU.add, ALU.min).then_inc(freed[hbk], 1)

                return step

            expert_loop(dve, expert_steps(0), 0, LAG_HS)
            base(0)

            dve.wait_ge(ld_c, LD_C)
            for b in range(2):
                combine(0, b)
                attn_norm(b)
            attention_1()
            tables(1)

            expert_loop(dve, expert_steps(1), 1, LAG_H[1])
            base(1)
            for b in range(B):
                combine(1, b)

        @block.tensor
        def _(pe):
            def use(bk, n):
                if n > 1:
                    pe.wait_ge(freed[bk], n - 1)
                return bank[bk]

            def keep_clock(o, n=1):
                for _ in range(n):
                    nc.tensor.matmul(o[:], warm[:, 0:128], warm[:], start=True, stop=True)

            pe.wait_ge(warm_ready, 1)
            keep_clock(bank["T0"], WARM[0])
            pe.wait_ge(ld_a, LD_A)
            for n in range(2):
                bk = f"T{n}"
                o = use(bk, J(bk, "k0", n))
                nc.tensor.matmul(o[:, 0:308], kvw_sb[:, 0:128], ctx_sb[:, 308 * n:308 * n + 308],
                                 start=True, stop=True).then_inc(filled[bk], 1)
            for n in range(2):
                bk = ("O", "M")[n]
                o = use(bk, J(bk, "v0", n))
                for c in range(4):
                    b = 4 * n + c
                    ins = nc.tensor.matmul(o[0:M, 128 * c:128 * c + 128], ctx_sb[:, M * b:M * b + M],
                                           kvw_sb[:, 128:256], start=True, stop=True)
                ins.then_inc(filled[bk], 1)
            for n in range(2):
                bk = f"S{n}"
                o = use(bk, J(bk, "xT0", n))
                keep_clock(o, WARM[1])
                for c in range(4):
                    pe.wait_ge(xa_ready, 4 * n + c + 1)
                    ins = nc.tensor.transpose(o[:, 128 * c:128 * c + 128], XA[:, 4 * n + c, :], ident)
                ins.then_inc(filled[bk], 1)
            def q0(n):
                bk = f"T{n}"
                o = use(bk, J(bk, "q0", n))
                keep_clock(o, WARM[2])
                pe.wait_ge(freed[f"S{n}"], J(f"S{n}", "xT0", n))
                nc.tensor.matmul(o[:], qw_sb[:], XT0[:, 512 * n:512 * n + 512], start=True, stop=True)\
                    .then_inc(filled[bk], 1)

            q0(0)

            def scores(layer, b, groups=range(NG)):
                if layer == 0 and b % 4 == 0 and groups[0] == 0:
                    pe.wait_ge(freed[f"T{b // 4}"], J(f"T{b // 4}", "q0", b // 4))
                    pe.wait_ge(keys_spread[b // 4], 16 * NG)
                if layer == 1:
                    pe.wait_ge(freed["M"], J("M", "q", b, groups[-1] // 2))
                    if b == 0:
                        pe.wait_ge(keys1_zeroed, 2)
                        pe.wait_ge(keys1_half, 1)
                        for n in range(4):
                            pe.wait_ge(freed[f"S{n}"], J(f"S{n}", "k1", 12 + n))
                for g in groups:
                    o = use(f"S{g}", J(f"S{g}", "scores", layer, b, g))
                    if layer == 0:
                        ins = nc.tensor.matmul(o[:, 0:GM], QT0[:, T * b:T * b + T],
                                               KF0[:, GH * g:GH * g + GH, M * b:M * b + M], start=True, stop=True)
                    else:
                        for c in (2 * g, 2 * g + 1):
                            ins = nc.tensor.matmul(o[:, 2 * M * (c % 2):2 * M * (c % 2 + 1)], QT1[:, b % 2, c, :],
                                                   K1[:, c, :, M * b:M * b + M], start=True, stop=True)
                    ins.then_inc(filled[f"S{g}"], 1)

            def probsT(layer, b, g):
                bk = f"T{g % 2}"
                o = use(bk, J(bk, "pT", layer, b, g))
                pe.wait_ge(exp_done, NG * (B * layer + b) + g + 1)
                for j in range(GH):
                    ins = nc.tensor.transpose(o[0:M, 128 * j:128 * j + 128], P[:, b % 2, g, M * j:M * j + M], ident)
                ins.then_inc(filled[bk], 1)

            def pv(layer, b, g):
                bk, n = pvjob(layer, b, g)
                if layer or g == 0:
                    use(bk, n)
                if layer == 0 and b == 0 and g == 0:
                    for m in range(2):
                        pe.wait_ge(freed[("O", "M")[m]], J(("O", "M")[m], "v0", m))
                if layer == 1 and b == 0 and g == 0:
                    pe.wait_ge(ones_v, 2)
                    for m in range(4):
                        pe.wait_ge(freed[f"S{m}"], J(f"S{m}", "v1", 12 + m))
                tb = f"T{g % 2}"
                pe.wait_ge(freed[tb], J(tb, "pT", layer, b, g))
                d = HD[layer] + 1
                for j in range(GH):
                    h = GH * g + j
                    c = j if layer else h
                    v = (V0, V1)[layer]
                    ins = nc.tensor.matmul(bank[bk][:, d * c:d * c + d], PT[:, g, 128 * j:128 * j + 128],
                                           v[:, b, h, :], start=True, stop=True)
                if layer or g == NG - 1:
                    ins.then_inc(filled[bk], 1)

            def outT(layer, b, n):
                bk, number = product("oT", layer, b, n)
                o = use(bk, number)
                for g in (range(2 * n, 2 * n + 2) if layer else (0,)):
                    pk, done = pvjob(layer, b, g)
                    pe.wait_ge(freed[pk], done)
                if layer:
                    for c in range(4):
                        cc = 4 * n + c
                        ins = nc.tensor.transpose(o[:, 128 * c:128 * c + 128], OS[:, b % 2, 128 * cc:128 * cc + 128],
                                                  ident)
                else:
                    ins = nc.tensor.transpose(o[:, 0:128], OS[:, b % 2, 0:128], ident)
                ins.then_inc(filled[bk], 1)

            def proj(layer, b):
                bk, number = product("proj", layer, b)
                o = use(bk, number)
                for n in range(1 + layer):
                    tk, done = product("oT", layer, b, n)
                    pe.wait_ge(freed[tk], done)
                if layer == 0:
                    if b == 0:
                        pe.wait_ge(ld_b, LD_B)
                    ins = nc.tensor.matmul(o[:, 0:128], OT[:, 0, :], pw_sb[:], start=True, stop=True)
                else:
                    for c in range(8):
                        ins = nc.tensor.matmul(o[:, 0:128], OT[:, c, :], Wo_sb[:, c, :], start=(c == 0), stop=(c == 7))
                ins.then_inc(filled[bk], 1)

            def xnT(layer, b):
                bk, number = product("xnT", layer, b)
                o = use(bk, number)
                pe.wait_ge(xn_ready, layer * B + b + 1)
                nc.tensor.transpose(o[:, 0:128], XN[:, b, :], ident).then_inc(filled[bk], 1)

            def logits(layer, b):
                bk, number = product("logits", layer, b)
                o = use(bk, number)
                tk, done = product("xnT", layer, b)
                pe.wait_ge(freed[tk], done)
                nc.tensor.matmul(o[:, 0:E[layer]], XNT[:], wr_l[layer][:], start=True, stop=True)\
                    .then_inc(filled[bk], 1)

            def rank(layer, b):
                bk, number = product("rank", layer, b)
                o = use(bk, number)
                e = E[layer]
                pe.wait_ge(mask_ready, layer * B + b + 1)
                ins = nc.tensor.matmul(o[:, 0:e], before, mask[:, b, 0:e], start=True, stop=(b == 0))
                if b > 0:
                    ins = nc.tensor.matmul(o[:, 0:e], ones, mcum[:, b - 1, 0:e], start=False, stop=True)
                ins.then_inc(filled[bk], 1)

            def xT(b):
                o = use("M", J("M", "xT", b))
                pe.wait_ge(xa_ready, B + b + 1)
                nc.tensor.transpose(o[:, 0:128], XA[:, b, :], ident).then_inc(filled["M"], 1)

            def q(b, n):
                o = use("M", J("M", "q", b, n))
                pe.wait_ge(freed["M"], J("M", "xT", b))
                for c in range(4):
                    cc = 4 * n + c
                    ins = nc.tensor.matmul(o[:, 128 * c:128 * c + 128], Wq_sb[:, 128 * cc:128 * cc + 128], XT1[:],
                                           start=True, stop=True)
                ins.then_inc(filled["M"], 1)

            def k1(start, count):
                pe.wait_ge(ld_c, LD_C)
                for n in range(start, start + count):
                    bk = f"S{n % 4}"
                    c, half = n // 2, n % 2
                    o = use(bk, J(bk, "k1", n))
                    nc.tensor.matmul(o[:, 0:308], Wk_sb[:, 128 * c:128 * c + 128],
                                     ctx_sb[:, 308 * half:308 * half + 308], start=True, stop=True)\
                        .then_inc(filled[bk], 1)

            def attention_0():
                for b in range(B + 2):
                    now, following, last = b < B, b + 1 < B, 0 <= b - 1 < B
                    routed = 0 <= b - 2 < B
                    if now:
                        probsT(0, b, 0)
                    if following:
                        scores(0, b + 1, (0,))
                    if b == B + 1:
                        k1(5, 1)
                    if routed:
                        xnT(0, b - 2)
                    if not now:
                        k1(0 if b == B else 6, 1)
                    if now:
                        probsT(0, b, 1)
                        pv(0, b, 0)
                    if last:
                        outT(0, b - 1, 0)
                    if b == B:
                        k1(1, 1)
                    if following:
                        scores(0, b + 1, (1,))
                    if now:
                        probsT(0, b, 2)
                    if routed:
                        logits(0, b - 2)
                    if not now:
                        k1(2 if b == B else 7, 1)
                    if now:
                        pv(0, b, 1)
                    if last:
                        proj(0, b - 1)
                    if b == B:
                        k1(3, 1)
                    if following:
                        scores(0, b + 1, (2,))
                    if now:
                        probsT(0, b, 3)
                        pv(0, b, 2)
                    if routed:
                        rank(0, b - 2)
                    if b == B:
                        k1(4, 1)
                    if following:
                        scores(0, b + 1, (3,))
                    if now:
                        pv(0, b, 3)
                k1(8, 2)

            def attention_1():
                for b in range(B - 1):
                    last, routed = 0 <= b - 1, 0 <= b - 2
                    probsT(1, b, 0)
                    xT(b + 1)
                    probsT(1, b, 1)
                    if last:
                        outT(1, b - 1, 0)
                    q(b + 1, 0)
                    pv(1, b, 0)
                    scores(1, b + 1, (0, 1))
                    q(b + 1, 1)
                    probsT(1, b, 2)
                    if last:
                        outT(1, b - 1, 1)
                    pv(1, b, 1)
                    probsT(1, b, 3)
                    if routed:
                        xnT(1, b - 2)
                    scores(1, b + 1, (2,))
                    pv(1, b, 2)
                    if routed:
                        logits(1, b - 2)
                    scores(1, b + 1, (3,))
                    pv(1, b, 3)
                    if last:
                        proj(1, b - 1)
                    if routed:
                        rank(1, b - 2)
                probsT(1, B - 1, 0)
                probsT(1, B - 1, 1)
                outT(1, B - 2, 0)
                outT(1, B - 2, 1)
                pv(1, B - 1, 0)
                pv(1, B - 1, 1)
                probsT(1, B - 1, 2)
                probsT(1, B - 1, 3)
                xnT(1, B - 3)
                proj(1, B - 2)
                outT(1, B - 1, 0)
                pv(1, B - 1, 2)
                pv(1, B - 1, 3)
                logits(1, B - 3)
                outT(1, B - 1, 1)
                proj(1, B - 1)
                rank(1, B - 3)
                xnT(1, B - 2)
                logits(1, B - 2)
                xnT(1, B - 1)
                logits(1, B - 1)
                rank(1, B - 2)
                rank(1, B - 1)

            def tables(layer):
                e = E[layer]
                n = e * CAND[layer]
                o = C_PL + layer * C_PL_W
                nt = UNITS[layer]
                ps = use("O", J("O", "count", layer))
                pe.wait_ge(mexp_ready, layer + 1)
                nc.tensor.matmul(ps[0:n, 0:1], mexp[:], ones[:, 0:1],
                                 start=True, stop=True).then_inc(filled["O"], 1)
                use("O", J("O", "pos", layer))
                if layer == 0:
                    k1(10, 1)
                pe.wait_ge(act_ready, layer + 1)
                nc.tensor.matmul(ps[0:n, 0:1], C[0:n, C_LT:C_LT + n], act_c[0:n, :], start=True, stop=True)\
                    .then_inc(filled["O"], 1)
                use("O", J("O", "table", layer))
                if layer == 0:
                    k1(11, 1)
                pe.wait_ge(ohj_ready, layer + 1)
                nc.tensor.matmul(ps[0:1, 0:nt], C[0:n, o + 1:o + 2], ohj[0:n, 0:nt], start=True, stop=True)
                nc.tensor.matmul(ps[0:1, nt:2 * nt], C[0:n, o + 2:o + 3], ohj[0:n, 0:nt], start=True, stop=True)\
                    .then_inc(filled["O"], 1)
                ps = use("M", J("M", "start", layer))
                nc.tensor.matmul(ps[:, 0:e], act_bc[0:n, :], C[0:n, o + 3:o + 3 + e], start=True, stop=True)\
                    .then_inc(filled["M"], 1)

            def base(layer):
                e = E[layer]
                for m in range(2):
                    ps = use(f"T{m}", J(f"T{m}", "gT", layer, m))
                    pe.wait_ge(gf_ready, layer + 1)
                    for c in range(4):
                        ins = nc.tensor.transpose(ps[0:e, 128 * c:128 * c + 128], gf[:, 4 * m + c, 0:e], ident)
                    ins.then_inc(filled[f"T{m}"], 1)
                for m in range(2):
                    ps = use(f"T{m}", J(f"T{m}", "b2", layer, m))
                    for c in range(4):
                        b = 4 * m + c
                        ins = nc.tensor.matmul(ps[:, 128 * c:128 * c + 128], gfT[0:e, 128 * b:128 * b + 128],
                                               b2_l[layer][:], start=True, stop=True)
                    ins.then_inc(filled[f"T{m}"], 1)

            scores(0, 0)
            q0(1)
            attention_0()
            tables(0)
            k1(12, 4)

            def expert_steps(layer):
                unit = UNIT[layer]

                def step(i, p, first, last):
                    if not last:
                        tb = tbank(p)
                        pe.wait_ge(freed[tb], unit_use(tb, layer, i, 0, p) - 1)
                        if first and p == 0:
                            keep_clock(bank[tb], LOOP_WARM[layer])
                        r = p % RING
                        pe.wait_ge(x_in[layer][r], 16 * unit_count(layer, i, 0, p, RING))
                        for u in range(unit):
                            ins = nc.tensor.transpose(bank[tb][:, 128 * u:128 * u + 128], xin[:, unit * r + u, :], ident)
                        ins.then_inc(filled[tb], 1)
                    where = at(layer, p, LAG_H[layer], first, last)
                    if where:
                        d, q = where
                        tb, hbk = tbank(q), hbank(q)
                        pe.wait_ge(freed[tb], unit_use(tb, layer, i, d, q))
                        pe.wait_ge(freed[hbk], unit_use(hbk, layer, i, d, q) - 1)
                        pe.wait_ge(w_in[layer][q], 16 * i + 16 * (d + 1))
                        wbuf = (w0, w1)[layer]
                        u0 = unit * (q % RING)
                        for c in range(4 // unit):
                            ins = nc.tensor.matmul(bank[hbk][:, 128 * unit * c:128 * unit * (c + 1)],
                                                   wbuf[:, q, 128 * c:128 * c + 128], xeT[:, u0:u0 + unit, :],
                                                   start=True, stop=True)
                        ins.then_inc(filled[hbk], 1)
                    where = at(layer, p, LAG_Y[layer], first, last)
                    if where:
                        d, q = where
                        yb = ybank(q)
                        pe.wait_ge(freed[yb], unit_use(yb, layer, i, d, q) - 1)
                        if last:
                            keep_clock(bank[yb], LAST_WARM[layer])
                        if layer == 0:
                            pe.wait_ge(hs_ready, unit_count(0, i, d, q))
                            for u in range(2):
                                ins = nc.tensor.matmul(bank[yb][:, 128 * u:128 * u + 128], hs[:, 2 * (q % RING) + u, :],
                                                       w0[:, q, 256:384], start=True, stop=True)
                        else:
                            pe.wait_ge(freed[hbank(q)], unit_use(hbank(q), 1, i, d, q))
                            for c in range(4):
                                ins = nc.tensor.matmul(bank[yb][:, 0:128], h1[q % 2][:, c, :],
                                                       w1[:, q, 512 + 128 * c:640 + 128 * c],
                                                       start=(c == 0), stop=(c == 3))
                        ins.then_inc(filled[yb], 1)

                return step

            expert_loop(pe, expert_steps(0), 0, LAG_Y[0])
            base(0)

            for n in range(16):
                bk = f"S{n % 4}"
                b, half = n // 2, n % 2
                o = use(bk, J(bk, "v1", n))
                nc.tensor.matmul(o[0:M, :], ctx_sb[:, M * b:M * b + M], Wv_sb[:, 512 * half:512 * half + 512],
                                 start=True, stop=True).then_inc(filled[bk], 1)
            xT(0)
            q(0, 0)
            q(0, 1)
            scores(1, 0)
            attention_1()
            tables(1)

            expert_loop(pe, expert_steps(1), 1, LAG_Y[1])
            base(1)


LD_A = 16 * 6
LD_B = 16 * 6
LD_C = 16 * 8


def kernel(x, ctx_768, L0_xattn_q_w, L0_xattn_q_b, L0_xattn_kv_w, L0_xattn_kv_b, L0_xattn_proj_w, L0_xattn_proj_b,
           L0_ffn_norm_scale, L0_ffn_wg, L0_ffn_bg, L0_ffn_w1, L0_ffn_b1, L0_ffn_w2, L0_ffn_b2,
           L1_xattn_Wq, L1_xattn_Wk, L1_xattn_Wv, L1_xattn_Wo, L1_xattn_bo,
           L1_ffn_Wr, L1_ffn_br, L1_ffn_W1, L1_ffn_b1, L1_ffn_W2, L1_ffn_b2):
    import concourse.bacc as bacc
    from concourse.bass_utils import run_bass_kernel_spmd

    def a(v):
        return np.asarray(v)

    w1, b1 = a(L0_ffn_w1), a(L0_ffn_b1)
    pack0 = np.concatenate([w1[:, :, 0::2], w1[:, :, 1::2], a(L0_ffn_w2), b1[:, 0::2, None], b1[:, 1::2, None]], axis=2)
    W2 = a(L1_ffn_W2).reshape(8, 4, 128, 128).transpose(0, 2, 1, 3).reshape(8, 128, 512)
    pack1 = np.concatenate([a(L1_ffn_W1), W2, a(L1_ffn_b1).reshape(8, 4, 128).transpose(0, 2, 1)], axis=2)
    arrays = {
        "x": a(x),
        "ctxT": a(ctx_768).reshape(B * M, DC).T,
        "cst": shape_constants(),
        "q_w": a(L0_xattn_q_w),
        "q_b": a(L0_xattn_q_b).reshape(128, 1),
        "kv_w": a(L0_xattn_kv_w),
        "kv_b": a(L0_xattn_kv_b).reshape(2, 128).T,
        "proj_w": a(L0_xattn_proj_w),
        "proj_b": a(L0_xattn_proj_b),
        "norm_s": a(L0_ffn_norm_scale),
        "wg": a(L0_ffn_wg),
        "bg": a(L0_ffn_bg),
        "wp0": pack0,
        "b2_0": a(L0_ffn_b2),
        "Wq": a(L1_xattn_Wq),
        "Wk": a(L1_xattn_Wk),
        "Wv": a(L1_xattn_Wv),
        "Wo": a(L1_xattn_Wo).reshape(8, 128, 128).transpose(1, 0, 2),
        "bo": a(L1_xattn_bo),
        "Wr": a(L1_ffn_Wr),
        "br": a(L1_ffn_br),
        "wp1": pack1,
        "b2_1": a(L1_ffn_b2),
    }
    arrays = {k: np.ascontiguousarray(v) for k, v in arrays.items()}
    nc = bacc.Bacc("TRN2", target_bir_lowering=False, num_devices=1)
    aps = {k: nc.dram_tensor(f"{k}_dram", v.shape, mybir.dt.from_np(v.dtype), kind="ExternalInput").ap()
           for k, v in arrays.items()}
    out = nc.dram_tensor("out_dram", (B, T, D), F32, kind="ExternalOutput").ap()
    build(nc, out=out, **aps)
    r = run_bass_kernel_spmd(nc, [{f"{k}_dram": v for k, v in arrays.items()}], core_ids=[0])
    return r.results[0]["out_dram"]
```
